# Optimizing a Trainium2 kernel written in Bass

```python
import numpy as np
import jax
import jax.numpy as jnp

def _softmax(x, axis=-1):
    return jax.nn.softmax(x, axis=axis)

def _gelu(x):
    return jax.nn.gelu(x, approximate=True)

def _silu(x):
    return jax.nn.silu(x)

def _sigmoid(x):
    return jax.nn.sigmoid(x)

def _layernorm(x, axis=-1, eps=1e-05):
    m = jnp.mean(x, axis=axis, keepdims=True)
    v = jnp.var(x, axis=axis, keepdims=True)
    return (x - m) / jnp.sqrt(v + eps)

def _scatter_add(tgt, idx, src, axis=0):
    return tgt.at[idx].add(src)

def _segment_sum(src, seg, n):
    return jax.ops.segment_sum(src, seg, n)
kernel_name = 'mk_sandwich_d2_jaxref_r8_56099b'

def setup_inputs(seed: int=0):
    np.random.seed(seed)
    _w = jnp.asarray

    def _L0_attn_setup():
        import jax, jax.numpy as jnp
        import numpy as np
        D = 128
        EXPAND = 2
        H = D * EXPAND
        B, S = (4, 256)
        EPS = 1e-05

        def _layer_norm(x, gamma, beta):
            mu = jnp.mean(x, axis=-1, keepdims=True)
            var = jnp.mean(jnp.square(x - mu), axis=-1, keepdims=True)
            return (x - mu) * jax.lax.rsqrt(var + EPS) * gamma + beta

        def _gru(y, w_ih, w_hh, b_ih, b_hh):
            xi = jnp.einsum('bsd,gd->bsg', y, w_ih) + b_ih
            xr, xz, xn = jnp.split(xi, 3, axis=-1)
            w_hr, w_hz, w_hn = jnp.split(w_hh, 3, axis=0)
            b_hr, b_hz, b_hn = jnp.split(b_hh, 3, axis=0)

            def step(h, xt):
                xr_t, xz_t, xn_t = xt
                r = jax.nn.sigmoid(xr_t + h @ w_hr.T + b_hr)
                z = jax.nn.sigmoid(xz_t + h @ w_hz.T + b_hz)
                n = jnp.tanh(xn_t + r * (h @ w_hn.T + b_hn))
                h_new = (1.0 - z) * n + z * h
                return (h_new, h_new)
            h0 = jnp.zeros((y.shape[0], w_hh.shape[1]), dtype=y.dtype)
            xs = (jnp.swapaxes(xr, 0, 1), jnp.swapaxes(xz, 0, 1), jnp.swapaxes(xn, 0, 1))
            _, hs = jax.lax.scan(step, h0, xs)
            return jnp.swapaxes(hs, 0, 1)
        key = jax.random.key(seed)
        ks = jax.random.split(key, 9)
        sc_ih = 1.0 / np.sqrt(D)
        sc_hh = 1.0 / np.sqrt(H)
        return {'x': jax.random.normal(ks[0], (B, S, D), dtype=jnp.float32), 'gamma': jnp.ones((D,), dtype=jnp.float32), 'beta': jnp.zeros((D,), dtype=jnp.float32), 'w_ih': jax.random.uniform(ks[1], (3 * H, D), jnp.float32, -sc_hh, sc_hh), 'w_hh': jax.random.uniform(ks[2], (3 * H, H), jnp.float32, -sc_hh, sc_hh), 'b_ih': jax.random.uniform(ks[3], (3 * H,), jnp.float32, -sc_hh, sc_hh), 'b_hh': jax.random.uniform(ks[4], (3 * H,), jnp.float32, -sc_hh, sc_hh), 'w_out': jax.random.uniform(ks[5], (D, H), jnp.float32, -sc_ih, sc_ih), 'b_out': jax.random.uniform(ks[6], (D,), jnp.float32, -sc_ih, sc_ih)}
    _L0_attn_in = _L0_attn_setup()

    def _L0_ffn_setup():
        import jax, jax.numpy as jnp
        import numpy as np
        B, S, D, F, E, R = (4, 256, 128, 512, 8, 4)
        key = jax.random.key(seed)
        ks = jax.random.split(key, 8)
        s_in = 1.0 / np.sqrt(D)
        s_ff = 1.0 / np.sqrt(F)
        return {'hidden_states': jax.random.normal(ks[0], (B, S, D), jnp.float32), 'gate_W': jax.random.normal(ks[1], (E, D), jnp.float32) * s_in, 'gate_b': jnp.zeros((E,), jnp.float32), 'wi_W': jax.random.normal(ks[2], (F, D), jnp.float32) * s_in, 'wi_b': jnp.zeros((F,), jnp.float32), 'wo_W': jax.random.normal(ks[3], (D, F), jnp.float32) * s_ff, 'wo_b': jnp.zeros((D,), jnp.float32), 'lora_A': jax.random.normal(ks[4], (E, R, D), jnp.float32) * s_in, 'lora_B': jax.random.normal(ks[5], (E, F, R), jnp.float32) * 0.02}
    _L0_ffn_in = _L0_ffn_setup()

    def _L1_attn_setup():
        import jax, jax.numpy as jnp
        import numpy as np
        HEADS = 16
        D_MODEL = 128
        EXPANSION = 2
        D_EXP = D_MODEL * EXPANSION
        D_HEAD = D_EXP // HEADS
        B, SEQ = (1, 256)
        LN_EPS = 1e-05
        NEG_BIG = -10000000000.0

        def layer_norm(x, w, b):
            mu = jnp.mean(x, axis=-1, keepdims=True)
            var = jnp.var(x, axis=-1, keepdims=True)
            return (x - mu) * jax.lax.rsqrt(var + LN_EPS) * w + b
        key = jax.random.key(seed)
        ks = jax.random.split(key, 8)
        d_out = 4 * D_EXP + HEADS
        x = jax.random.normal(ks[0], (B, SEQ, D_MODEL), dtype=jnp.float32)
        W_in = 0.02 * jax.random.normal(ks[1], (d_out, D_MODEL), dtype=jnp.float32)
        b_in = jnp.zeros((d_out,), dtype=jnp.float32)
        W_in = W_in.at[4 * D_EXP:].set(0.0)
        b_in = b_in.at[4 * D_EXP:].set(jnp.linspace(-8.0, 8.0, HEADS))
        W_out = 0.02 * (2 * 12) ** (-0.5) * jax.random.normal(ks[2], (D_MODEL, D_EXP), dtype=jnp.float32)
        in_ln_w = jnp.ones((D_MODEL,), dtype=jnp.float32)
        in_ln_b = jnp.zeros((D_MODEL,), dtype=jnp.float32)
        out_ln_w = jnp.ones((D_MODEL,), dtype=jnp.float32)
        out_ln_b = jnp.zeros((D_MODEL,), dtype=jnp.float32)
        smear_factor = jnp.linspace(-6.0, 6.0, HEADS)
        log_scale = jnp.zeros((HEADS,), dtype=jnp.float32)
        return {'x': x, 'W_in': W_in, 'b_in': b_in, 'in_ln_w': in_ln_w, 'in_ln_b': in_ln_b, 'W_out': W_out, 'out_ln_w': out_ln_w, 'out_ln_b': out_ln_b, 'smear_factor': smear_factor, 'log_scale': log_scale}
    _L1_attn_in = _L1_attn_setup()

    def _L1_ffn_setup():
        import jax, jax.numpy as jnp
        import numpy as np
        DIM = 128
        HIDDEN = 384
        SCALE = 1.0 / 127.0

        def _dequant(w_int, dtype):
            return w_int.astype(dtype) * jnp.asarray(SCALE, dtype)
        key = jax.random.key(seed)
        k_x, k_g, k_u, k_d = jax.random.split(key, 4)
        x = jax.random.normal(k_x, (4, 256, DIM), dtype=jnp.float32)
        w_gate = jax.random.randint(k_g, (HIDDEN, DIM), -127, 128, dtype=jnp.int32)
        w_up = jax.random.randint(k_u, (HIDDEN, DIM), -127, 128, dtype=jnp.int32)
        w_down = jax.random.randint(k_d, (DIM, HIDDEN), -127, 128, dtype=jnp.int32)
        return {'x': x, 'w_gate': w_gate, 'w_up': w_up, 'w_down': w_down}
    _L1_ffn_in = _L1_ffn_setup()
    _d = {'L0_attn_x': _L0_attn_in['x'], 'L0_attn_gamma': _L0_attn_in['gamma'], 'L0_attn_beta': _L0_attn_in['beta'], 'L0_attn_w_ih': _L0_attn_in['w_ih'], 'L0_attn_w_hh': _L0_attn_in['w_hh'], 'L0_attn_b_ih': _L0_attn_in['b_ih'], 'L0_attn_b_hh': _L0_attn_in['b_hh'], 'L0_attn_w_out': _L0_attn_in['w_out'], 'L0_attn_b_out': _L0_attn_in['b_out'], 'L0_ffn_gate_W': _L0_ffn_in['gate_W'], 'L0_ffn_gate_b': _L0_ffn_in['gate_b'], 'L0_ffn_wi_W': _L0_ffn_in['wi_W'], 'L0_ffn_wi_b': _L0_ffn_in['wi_b'], 'L0_ffn_wo_W': _L0_ffn_in['wo_W'], 'L0_ffn_wo_b': _L0_ffn_in['wo_b'], 'L0_ffn_lora_A': _L0_ffn_in['lora_A'], 'L0_ffn_lora_B': _L0_ffn_in['lora_B'], 'L1_attn_W_in': _L1_attn_in['W_in'], 'L1_attn_b_in': _L1_attn_in['b_in'], 'L1_attn_in_ln_w': _L1_attn_in['in_ln_w'], 'L1_attn_in_ln_b': _L1_attn_in['in_ln_b'], 'L1_attn_W_out': _L1_attn_in['W_out'], 'L1_attn_out_ln_w': _L1_attn_in['out_ln_w'], 'L1_attn_out_ln_b': _L1_attn_in['out_ln_b'], 'L1_attn_smear_factor': _L1_attn_in['smear_factor'], 'L1_attn_log_scale': _L1_attn_in['log_scale'], 'L1_ffn_w_gate': _L1_ffn_in['w_gate'], 'L1_ffn_w_up': _L1_ffn_in['w_up'], 'L1_ffn_w_down': _L1_ffn_in['w_down']}
    _x0 = _d['L0_attn_x']
    _d['L0_attn_x'] = jax.random.normal(jax.random.fold_in(jax.random.key(seed), 1), (8, 512, 128), dtype=_x0.dtype)
    del _x0
    return _d

def reference(L0_attn_x, L0_attn_gamma, L0_attn_beta, L0_attn_w_ih, L0_attn_w_hh, L0_attn_b_ih, L0_attn_b_hh, L0_attn_w_out, L0_attn_b_out, L0_ffn_gate_W, L0_ffn_gate_b, L0_ffn_wi_W, L0_ffn_wi_b, L0_ffn_wo_W, L0_ffn_wo_b, L0_ffn_lora_A, L0_ffn_lora_B, L1_attn_W_in, L1_attn_b_in, L1_attn_in_ln_w, L1_attn_in_ln_b, L1_attn_W_out, L1_attn_out_ln_w, L1_attn_out_ln_b, L1_attn_smear_factor, L1_attn_log_scale, L1_ffn_w_gate, L1_ffn_w_up, L1_ffn_w_down):

    def _L0_attn_ref(x, gamma, beta, w_ih, w_hh, b_ih, b_hh, w_out, b_out):
        import jax, jax.numpy as jnp
        import numpy as np
        D = 128
        EXPAND = 2
        H = D * EXPAND
        B, S = (4, 256)
        EPS = 1e-05

        def _layer_norm(x, gamma, beta):
            mu = jnp.mean(x, axis=-1, keepdims=True)
            var = jnp.mean(jnp.square(x - mu), axis=-1, keepdims=True)
            return (x - mu) * jax.lax.rsqrt(var + EPS) * gamma + beta

        def _gru(y, w_ih, w_hh, b_ih, b_hh):
            xi = jnp.einsum('bsd,gd->bsg', y, w_ih) + b_ih
            xr, xz, xn = jnp.split(xi, 3, axis=-1)
            w_hr, w_hz, w_hn = jnp.split(w_hh, 3, axis=0)
            b_hr, b_hz, b_hn = jnp.split(b_hh, 3, axis=0)

            def step(h, xt):
                xr_t, xz_t, xn_t = xt
                r = jax.nn.sigmoid(xr_t + h @ w_hr.T + b_hr)
                z = jax.nn.sigmoid(xz_t + h @ w_hz.T + b_hz)
                n = jnp.tanh(xn_t + r * (h @ w_hn.T + b_hn))
                h_new = (1.0 - z) * n + z * h
                return (h_new, h_new)
            h0 = jnp.zeros((y.shape[0], w_hh.shape[1]), dtype=y.dtype)
            xs = (jnp.swapaxes(xr, 0, 1), jnp.swapaxes(xz, 0, 1), jnp.swapaxes(xn, 0, 1))
            _, hs = jax.lax.scan(step, h0, xs)
            return jnp.swapaxes(hs, 0, 1)
        y = _layer_norm(x, gamma, beta)
        h = _gru(y, w_ih, w_hh, b_ih, b_hh)
        y = jnp.einsum('bsh,dh->bsd', h, w_out) + b_out
        return x + y

    def _L0_ffn_ref(hidden_states, gate_W, gate_b, wi_W, wi_b, wo_W, wo_b, lora_A, lora_B):
        import jax, jax.numpy as jnp
        import numpy as np
        B, S, D, F, E, R = (4, 256, 128, 512, 8, 4)
        x = hidden_states
        logits = jnp.einsum('bsd,ed->bse', x, gate_W) + gate_b
        top1 = jnp.argmax(jax.nn.softmax(logits, axis=-1), axis=-1)
        base = jnp.einsum('bsd,fd->bsf', x, wi_W) + wi_b
        out = jnp.zeros_like(x)
        for i in range(lora_A.shape[0]):
            lora = jnp.einsum('bsr,fr->bsf', jnp.einsum('bsd,rd->bsr', x, lora_A[i]), lora_B[i])
            inter = jax.nn.relu(base + lora)
            expert_out = jnp.einsum('bsf,df->bsd', inter, wo_W) + wo_b
            mask = (top1 == i).astype(x.dtype)[..., None]
            out = out + mask * expert_out
        return out

    def _L1_attn_ref(x, W_in, b_in, in_ln_w, in_ln_b, W_out, out_ln_w, out_ln_b, smear_factor, log_scale):
        import jax, jax.numpy as jnp
        import numpy as np
        HEADS = 16
        D_MODEL = 128
        EXPANSION = 2
        D_EXP = D_MODEL * EXPANSION
        D_HEAD = D_EXP // HEADS
        B, SEQ = (1, 256)
        LN_EPS = 1e-05
        NEG_BIG = -10000000000.0

        def layer_norm(x, w, b):
            mu = jnp.mean(x, axis=-1, keepdims=True)
            var = jnp.var(x, axis=-1, keepdims=True)
            return (x - mu) * jax.lax.rsqrt(var + LN_EPS) * w + b
        b, i, d = x.shape
        xn = layer_norm(x, in_ln_w, in_ln_b)
        proj = xn @ W_in.T + b_in
        q, k, v, p, y = jnp.split(proj, [D_EXP, 2 * D_EXP, 3 * D_EXP, 4 * D_EXP], axis=-1)
        to_heads = lambda t: t.reshape(b, i, HEADS, D_HEAD).transpose(0, 2, 1, 3)
        q, k, v = (to_heads(q), to_heads(k), to_heads(v))
        smear = jax.nn.sigmoid(smear_factor)[None, :, None, None]
        k_prev = jnp.pad(k, ((0, 0), (0, 0), (1, 0), (0, 0)))[:, :, :-1, :]
        k = (1 - smear) * k + smear * k_prev
        s = jnp.exp(log_scale)[None, :, None, None]
        pos = jnp.cumsum(jax.nn.sigmoid(y).transpose(0, 2, 1), axis=-1)
        relpos = pos[..., :, None] - pos[..., None, :]
        causal = jnp.triu(jnp.full((i, i), NEG_BIG, dtype=x.dtype), k=1)
        mask = causal - relpos
        scores = jnp.einsum('bhid,bhjd->bhij', q / s, k / s) / np.sqrt(D_HEAD) + mask
        attn = jax.nn.softmax(scores, axis=-1)
        o = jnp.einsum('bhij,bhjd->bhid', attn, v)
        o = o.transpose(0, 2, 1, 3).reshape(b, i, D_EXP)
        out = jax.nn.silu(p) * o @ W_out.T
        return layer_norm(out, out_ln_w, out_ln_b)

    def _L1_ffn_ref(x, w_gate, w_up, w_down):
        import jax, jax.numpy as jnp
        import numpy as np
        DIM = 128
        HIDDEN = 384
        SCALE = 1.0 / 127.0

        def _dequant(w_int, dtype):
            return w_int.astype(dtype) * jnp.asarray(SCALE, dtype)
        wg = _dequant(w_gate, x.dtype)
        wu = _dequant(w_up, x.dtype)
        wd = _dequant(w_down, x.dtype)
        gate = jnp.einsum('bsd,hd->bsh', x, wg)
        up = jnp.einsum('bsd,hd->bsh', x, wu)
        h = jax.nn.silu(gate) * up
        return jnp.einsum('bsh,dh->bsd', h, wd)
    x = L0_attn_x
    x = x + _layernorm(_L0_attn_ref(_layernorm(x, axis=-1), L0_attn_gamma, L0_attn_beta, L0_attn_w_ih, L0_attn_w_hh, L0_attn_b_ih, L0_attn_b_hh, L0_attn_w_out, L0_attn_b_out), axis=-1)
    x = x + _layernorm(_L0_ffn_ref(_layernorm(x, axis=-1), L0_ffn_gate_W, L0_ffn_gate_b, L0_ffn_wi_W, L0_ffn_wi_b, L0_ffn_wo_W, L0_ffn_wo_b, L0_ffn_lora_A, L0_ffn_lora_B), axis=-1)
    x = x + _layernorm(_L1_attn_ref(_layernorm(x, axis=-1), L1_attn_W_in, L1_attn_b_in, L1_attn_in_ln_w, L1_attn_in_ln_b, L1_attn_W_out, L1_attn_out_ln_w, L1_attn_out_ln_b, L1_attn_smear_factor, L1_attn_log_scale), axis=-1)
    x = x + _layernorm(_L1_ffn_ref(_layernorm(x, axis=-1), L1_ffn_w_gate, L1_ffn_w_up, L1_ffn_w_down), axis=-1)
    return x

_drawn_inputs = setup_inputs


def setup_inputs(seed=0):
    import zlib

    import numpy as np

    out = dict(_drawn_inputs(seed))
    spreads = {'L0_attn_gamma': (1.0, 0.6),
     'L0_attn_beta': (0.0, 0.459),
     'L0_ffn_gate_b': (0.0, 0.8),
     'L0_ffn_wi_b': (0.0, 0.1),
     'L0_ffn_wo_b': (0.0, 0.1),
     'L1_attn_in_ln_w': (1.0, 0.2),
     'L1_attn_in_ln_b': (0.0, 0.1),
     'L1_attn_out_ln_w': (1.0, 0.2),
     'L1_attn_out_ln_b': (0.0, 0.1),
     'L1_attn_log_scale': (0.0, 0.8)}
    factors = {'L0_attn_b_ih': 3.567,
     'L0_attn_b_hh': 6.439,
     'L0_ffn_gate_W': 3.085,
     'L0_ffn_lora_A': 2.872,
     'L0_ffn_lora_B': 2.889,
     'L1_attn_smear_factor': 5.517}
    for name, (base, spread) in spreads.items():
        noise = np.random.default_rng([zlib.crc32(name.encode()), seed]).standard_normal(out[name].shape)
        drawn = base * np.exp(spread * noise) if base else spread * noise
        out[name] = jnp.asarray(drawn.astype(out[name].dtype))
    for name, factor in factors.items():
        out[name] = (out[name] * factor).astype(out[name].dtype)
    return out
```

```python
from contextlib import ExitStack

import concourse.bass as bass
from concourse import mybir

F32 = mybir.dt.float32
BF16 = mybir.dt.bfloat16
FP16 = mybir.dt.float16
I32 = mybir.dt.int32
U32 = mybir.dt.uint32
ALU = mybir.AluOpType
ACT = mybir.ActivationFunctionType
AX = mybir.AxisListType

P = 128
B, S, D = 8, 512, 128
NT = S // P
H = 256
HC = H // P
F, E, R = 512, 8, 4
FC = F // P
HEADS, DH = 16, 16
DE = HEADS * DH
HID = 384
NH = HID // P
EPS = 1e-5
NEG_BIG = -1e10
U = 4
NSTEP = HC * B


class Signal:

    def __init__(self, sem, per=1, credit=0):
        self.sem, self.per, self.credit = sem, per, credit

    def value(self, eng, b, k=None):
        v = b * self.per + (self.credit + (self.per if k is None else k))
        return v if isinstance(v, int) else eng.snap(v)

    def before(self, eng, b):
        return self.value(eng, b, 0)


def build(nc, x_d, gamma_d, beta_d, w_ih_d, w_hh_d, b_ih_d, b_hh_d, w_out_d, b_out_d,
          gate_w_d, gate_b_d, wi_d, wi_b_d, wo_d, wo_b_d, lora_a_d, lora_b_d,
          w_in_d, b_in_d, in_ln_w_d, in_ln_b_d, w_aout_d, out_ln_w_d, out_ln_b_d, smear_d, log_scale_d,
          w_gate_d, w_up_d, w_down_d, out_d):
    top = ExitStack()
    with top:
        def sb(ctx, name, shape, dt=F32):
            return ctx.enter_context(nc.sbuf_tensor(name, shape, dt))

        X = sb(top, "X", [P, B * NT, D])
        MV = sb(top, "MV", [P, B * NT, 2])
        R1 = sb(top, "R1", [P, B * NT])
        RR = sb(top, "RR", [P, B * NT])
        half = sb(top, "half", [P, B * NT])
        eps = sb(top, "eps", [P, NT])
        ident = sb(top, "ident", [P, P])
        identb = sb(top, "identb", [P, P], BF16)
        wihT = sb(top, "wihT", [P, 3 * H])
        woutT = sb(top, "woutT", [P, HC, D])
        wiT = sb(top, "wiT", [P, F])
        woT = sb(top, "woT", [P, FC, D])
        gaT = sb(top, "gaT", [P, E + E * R])
        lbT = sb(top, "lbT", [E * R, F])
        winT = sb(top, "winT", [P, 4 * DE + HEADS])
        waoT = sb(top, "waoT", [P, DE // P, D])
        wguT = sb(top, "wguT", [P, 2 * HID])
        wdT = sb(top, "wdT", [P, NH, D])
        gam = sb(top, "gam", [P, 1])
        bet = sb(top, "bet", [P, 1])
        bih = sb(top, "bih", [P, 6])
        bhh = sb(top, "bhh", [P, 6])
        wib = sb(top, "wib", [P, FC])
        bqk = sb(top, "bqk", [P, 4])
        ilw = sb(top, "ilw", [P, 1])
        ilb = sb(top, "ilb", [P, 1])
        bout = sb(top, "bout", [P, D])
        gateb = sb(top, "gateb", [P, E])
        wob = sb(top, "wob", [P, D])
        bvpy = sb(top, "bvpy", [P, 2 * DE + HEADS])
        olw = sb(top, "olw", [P, D])
        olb = sb(top, "olb", [P, D])
        iota_e = sb(top, "iota_e", [P, E, R])
        hs8 = sb(top, "hs8", [8, 6])
        qsc = sb(top, "qsc", [P, 6])
        kscale = sb(top, "kscale", [P, 4])
        S_gru = kscale[:, 2:3]
        bX = sb(top, "bX", [P, 6])
        W1 = sb(top, "W1", [P, HC, 3 * H], FP16)
        W2 = sb(top, "W2", [P, HC, 3 * H], FP16)
        PS = top.enter_context(nc.psum_tensor("PS", [P, 8, 512], F32))

        def signal(name, per=1, credit=0):
            return Signal(top.enter_context(nc.semaphore(name)), per, credit)

        passed = signal("passed").sem

        def hold(eng, sem, value):
            eng.wait_ge(sem, value)
            eng.sem_inc(passed, 1)

        def x_moments(dve, s_t, m, st, mv, kept):
            with dve.Fori(0, B) as b:
                for t in range(NT):
                    dve.bn_stats(s_t[:, t, :], X[:, bass.ds(dve.snap(b * NT + t), 1), :].rearrange("p o d -> p (o d)")).then_inc(st.sem, 1)
                hold(dve, st.sem, st.value(dve, b))
                for t in range(NT):
                    dve.bn_aggr(m[:, t, :], s_t[:, t, :]).then_inc(mv.sem, 1)
                dve.wait_ge(mv.sem, mv.value(dve, b))
                dve.tensor_scalar(MV[:, bass.ds(dve.snap(b * NT), NT), :], m[:, :, :], 1.0, None, ALU.mult).then_inc(kept.sem, 1)

        gru_scope = ExitStack()
        top.enter_context(gru_scope)
        HS = sb(gru_scope, "HS", [P, S, HC, B])
        xi_scope = ExitStack()
        gru_scope.enter_context(xi_scope)
        XI = sb(xi_scope, "XI", [P, S + 2 * U, 6, B])

        ctx = ExitStack()
        with ctx:
            staging = HS[:, :, :, :].rearrange("p s c b -> p (s c b)")
            taken = [0]

            def stage(shape, dt=F32):
                n = 1
                for k in shape:
                    n *= k
                at = staging[:, taken[0]:taken[0] + n]
                taken[0] += n
                at = at if dt == F32 else at.bitcast(dt)
                return at if len(shape) == 1 else at.rearrange("p (c k) -> p c k", c=shape[0])
            s_ih = stage((6, D))
            s_hh = stage((6, H))
            s_out = stage((H,))
            s_wi = stage((FC, D))
            s_wo = stage((F,))
            s_lb = stage((FC, E * R))
            s_in = stage((8, D))
            s_ao = stage((DE,))
            s_gi = stage((2 * NH, D), I32)
            s_di = stage((HID,), I32)
            s_g = stage((2 * NH, D))
            s_d = stage((HID,))
            s_ga = sb(ctx, "s_ga", [E + E * R, D])
            s_iny = sb(ctx, "s_iny", [HEADS, D])
            whhT = sb(ctx, "whhT", [P, HC, 3 * H])
            mx = sb(ctx, "mx", [P, 1])
            mrow = sb(ctx, "mrow", [1, 1])
            onesr = sb(ctx, "onesr", [1, P])
            sel8 = sb(ctx, "sel8", [8, P])
            STb = sb(ctx, "STb", [P, NT, 6])
            MVb = sb(ctx, "MVb", [P, NT, 2])
            rt = sb(ctx, "rt", [P, B * NT])
            YN = sb(ctx, "YN", [P, NT, D])
            YT = sb(ctx, "YT", [P, S])
            warm = sb(ctx, "warm", [P, 1])

            loads_x = signal("loads_x")
            loads_gru = signal("loads_gru")
            loads_rest = signal("loads_rest")
            consts = signal("consts")
            turned = signal("weights_turned")
            kept = signal("weights_kept")
            casts = signal("int_weights_cast")
            sc_v = signal("scale_step_v")
            sc_p = signal("scale_step_p")
            sc_a = signal("head_scalar_exps")
            hv = signal("head_scalars_ready")
            bx = signal("input_bias_ready")
            pool_step = signal("x_rstd_steps").sem
            stats = signal("x_stats", NT)
            aggr = signal("x_aggr", NT)
            mv_kept = signal("x_moments_kept")
            rstd = signal("x_rstd")
            y_ready = signal("y_ready", NT)
            yT_ps = signal("yT_ps", 1, 1)
            yT_ready = signal("yT_ready", 1, 1)
            xi_ps = signal("xi_ps", 6, 6)
            xi_v = signal("xi_by_vector", 3, 3)
            xi_a = signal("xi_by_scalar", 3, 3)

            gru_jobs = [(s_hh[:, c, kc * P:(kc + 1) * P], whhT[:, kc, c * P:(c + 1) * P], 0.25 if c >= 4 else 0.5)
                        for c in range(6) for kc in range(HC)]
            gru_jobs += [(s_ih[:, c, :], wihT[:, c * P:(c + 1) * P], 1.0) for c in range(6)]
            jobs = [(s_out[:, c * P:(c + 1) * P], woutT[:, c, :], 0.5) for c in range(HC)]
            jobs += [(s_wi[:, c, :], wiT[:, c * P:(c + 1) * P], 1.0) for c in range(FC)]
            jobs += [(s_wo[:, c * P:(c + 1) * P], woT[:, c, :], 1.0) for c in range(FC)]
            jobs += [(s_ga[:, :], gaT[:, :], 1.0)]
            jobs += [(s_lb[:, c, :], lbT[:, c * P:(c + 1) * P], 1.0) for c in range(FC)]
            jobs += [(s_in[:, c, :], winT[:, c * P:(c + 1) * P], 1.0) for c in range(8)]
            jobs += [(s_iny[:, :], winT[:, 4 * DE:4 * DE + HEADS], 1.0)]
            jobs += [(s_ao[:, c * P:(c + 1) * P], waoT[:, c, :], 0.5) for c in range(DE // P)]
            jobs += [(s_g[:, c, :], wguT[:, c * P:(c + 1) * P], 1.0) for c in range(2 * NH)]
            jobs += [(s_d[:, c * P:(c + 1) * P], wdT[:, c, :], 0.5) for c in range(NH)]
            NG = len(gru_jobs)
            alljobs = gru_jobs + jobs
            NJ = len(alljobs)

            block = ctx.enter_context(nc.Block())

            @block.sync
            def _(sp):
                sp.dma_start(s_hh, w_hh_d.rearrange("(c p) k -> p c k", p=P)).then_inc(loads_gru.sem, 16)
                sp.dma_start(s_ih, w_ih_d.rearrange("(c p) k -> p c k", p=P)).then_inc(loads_gru.sem, 16)
                for b in range(B):
                    sp.dma_start(X[:, b * NT:(b + 1) * NT, :],
                                 x_d[b].rearrange("(t p) d -> p t d", p=P)).then_inc(loads_x.sem, 16)
                sp.dma_start(s_out[:, :], w_out_d).then_inc(loads_rest.sem, 16)
                sp.dma_start(s_wi[:, :, :], wi_d.rearrange("(c p) k -> p c k", p=P)).then_inc(loads_rest.sem, 16)
                sp.dma_start(s_wo[:, :], wo_d).then_inc(loads_rest.sem, 16)
                sp.dma_start(s_ga[0:E, :], gate_w_d).then_inc(loads_rest.sem, 16)
                sp.dma_start(s_ga[E:E + E * R, :], lora_a_d.rearrange("e r d -> (e r) d")).then_inc(loads_rest.sem, 16)
                for c in range(FC):
                    sp.dma_start(s_lb[:, c, :].rearrange("p (e r) -> p e r", e=E),
                                 lora_b_d[:, c * P:(c + 1) * P, :].rearrange("e p r -> p e r")).then_inc(loads_rest.sem, 16)
                sp.dma_start(s_in[:, :, :], w_in_d[0:4 * DE, :].rearrange("(c p) k -> p c k", p=P)).then_inc(loads_rest.sem, 16)
                sp.dma_start(s_iny[:, :], w_in_d[4 * DE:, :]).then_inc(loads_rest.sem, 16)
                sp.dma_start(s_ao[:, :], w_aout_d).then_inc(loads_rest.sem, 16)
                sp.dma_start(s_gi[:, 0:NH, :], w_gate_d.rearrange("(c p) k -> p c k", p=P)).then_inc(loads_rest.sem, 16)
                sp.dma_start(s_gi[:, NH:, :], w_up_d.rearrange("(c p) k -> p c k", p=P)).then_inc(loads_rest.sem, 16)
                sp.dma_start(s_di[:, :], w_down_d).then_inc(loads_rest.sem, 16)

            N_REST = 11 + FC + 16

            @block.gpsimd
            def _(pool):
                pool.memset(ident[:, :], 0.0).then_inc(consts.sem, 1)
                pool.memset(half[:, :], -0.5).then_inc(consts.sem, 1)
                pool.memset(eps[:, :], EPS).then_inc(consts.sem, 1)
                pool.memset(sel8[:, :], 1.0).then_inc(consts.sem, 1)
                pool.memset(onesr[:, :], 1.0).then_inc(consts.sem, 1)
                pool.iota(iota_e[:, :, :], [[1, E], [0, R]], base=0, channel_multiplier=0,
                          allow_small_or_imprecise_dtypes=True).then_inc(consts.sem, 1)
                pool.memset(XI[:, S:, :, :], 0.0).then_inc(consts.sem, 1)
                pool.wait_ge(consts.sem, 7)
                pool.affine_select(out=ident[:, :], in_=ident[:, :], compare_op=ALU.not_equal, fill=1.0, base=0,
                                   pattern=[[-1, P]], channel_multiplier=1).then_inc(consts.sem, 1)
                pool.affine_select(out=sel8[:, :], in_=sel8[:, :], compare_op=ALU.is_ge, fill=0.0, base=0,
                                   pattern=[[1, P]], channel_multiplier=-DH).then_inc(consts.sem, 1)
                pool.wait_ge(consts.sem, 9)
                pool.tensor_copy(identb[:, :], ident[:, :]).then_inc(consts.sem, 1)
                pool.affine_select(out=sel8[:, :], in_=sel8[:, :], compare_op=ALU.is_ge, fill=0.0, base=DH - 1,
                                   pattern=[[-1, P]], channel_multiplier=DH).then_inc(consts.sem, 1)
                pool.wait_ge(loads_rest.sem, 16 * N_REST)
                pool.tensor_scalar(s_g[:, :, :], s_gi[:, :, :], 1.0 / 127.0, None, ALU.mult).then_inc(casts.sem, 1)
                pool.tensor_scalar(s_d[:, :], s_di[:, :], 1.0 / 127.0, None, ALU.mult).then_inc(casts.sem, 1)
                pool.wait_ge(mv_kept.sem, B)
                pool.tensor_scalar(rt[:, :], MV[:, :, 1], EPS, None, ALU.add).then_inc(pool_step, 1)
                pool.wait_ge(pool_step, 1)
                pool.tensor_tensor(R1[:, :], rt[:, :], half[:, :], ALU.pow).then_inc(pool_step, 1)
                pool.wait_ge(pool_step, 2)
                pool.tensor_tensor(rt[:, :], R1[:, :], R1[:, :], ALU.mult).then_inc(pool_step, 1)
                pool.wait_ge(pool_step, 3)
                pool.tensor_tensor(rt[:, :], rt[:, :], MV[:, :, 1], ALU.mult).then_inc(pool_step, 1)
                pool.wait_ge(pool_step, 4)
                pool.tensor_scalar(rt[:, :], rt[:, :], EPS, None, ALU.add).then_inc(pool_step, 1)
                pool.wait_ge(pool_step, 5)
                pool.tensor_tensor(rt[:, :], rt[:, :], half[:, :], ALU.pow).then_inc(pool_step, 1)
                pool.wait_ge(pool_step, 6)
                pool.tensor_tensor(RR[:, :], rt[:, :], R1[:, :], ALU.mult).then_inc(rstd.sem, 1)

            @block.tensor
            def _(pe):
                def turn(i):
                    src, dst, _ = alljobs[i]
                    k, m = src.shape[0], src.shape[1]
                    if i >= 8:
                        pe.wait_ge(kept.sem, i - 7)
                    pe.transpose(PS[0:m, i % 8, 0:k], src, ident[0:k, 0:k]).then_inc(turned.sem, 1)
                pe.wait_ge(consts.sem, 11)
                pe.wait_ge(loads_gru.sem, 32)
                for i in range(NG):
                    turn(i)
                pe.wait_ge(loads_rest.sem, 16 * N_REST)
                pe.wait_ge(casts.sem, 2)
                for i in range(NG, NJ):
                    turn(i)
                pe.wait_ge(kept.sem, NJ)
                pe.wait_ge(sc_v.sem, 1)
                pe.transpose(PS[0:1, 0, 0:P], mx[:, :], ident[:, :]).then_inc(sc_p.sem, 1)
                pe.wait_ge(sc_v.sem, 4)
                pe.matmul(PS[:, 1, 0:1], onesr[:, :], mrow[:, :], start=True, stop=True).then_inc(sc_p.sem, 1)
                pe.wait_ge(hv.sem, 3)
                pe.matmul(PS[:, 2, 0:6], sel8[:, :], hs8[:, :], start=True, stop=True).then_inc(sc_p.sem, 1)
                pe.wait_ge(sc_v.sem, 12)
                for s in (yT_ps, xi_ps):
                    pe.sem_inc(s.sem, s.credit)
                with pe.Fori(0, B) as b:
                    pe.wait_ge(y_ready.sem, y_ready.value(pe, b))
                    pe.wait_ge(yT_ready.sem, yT_ready.before(pe, b))
                    for t in range(NT):
                        last = pe.transpose(PS[:, 0, t * P:(t + 1) * P], YN[:, t, :], ident[:, :])
                    last.then_inc(yT_ps.sem, 1)
                    pe.wait_ge(yT_ready.sem, yT_ready.value(pe, b))
                    for c in range(6):
                        s, k = (xi_v, c // 2) if c % 2 else (xi_a, c // 2)
                        pe.wait_ge(s.sem, pe.snap(b * 3 + (k + 1)))
                        pe.matmul(PS[:, 1 + c, :], wihT[:, c * P:(c + 1) * P], YT[:, :],
                                  start=True, stop=True).then_inc(xi_ps.sem, 1)

            @block.scalar
            def _(act):
                def col(dst, src, c):
                    act.dma_start(dst, src.rearrange("(c p) -> p c", c=c),
                                   allow_slow_non_contiguous=True).then_inc(loads_rest.sem, 16)

                def row(dst, src):
                    act.dma_start(dst, src.partition_broadcast(P)).then_inc(loads_rest.sem, 16)
                col(gam[:, :], gamma_d, 1)
                col(bet[:, :], beta_d, 1)
                col(bih[:, :], b_ih_d, 6)
                col(bhh[:, :], b_hh_d, 6)
                col(wib[:, :], wi_b_d, FC)
                col(bqk[:, :], b_in_d[0:2 * DE], 4)
                col(ilw[:, :], in_ln_w_d, 1)
                col(ilb[:, :], in_ln_b_d, 1)
                row(bout[:, :], b_out_d)
                row(gateb[:, :], gate_b_d)
                row(wob[:, :], wo_b_d)
                row(bvpy[:, :], b_in_d[2 * DE:])
                row(olw[:, :], out_ln_w_d)
                row(olb[:, :], out_ln_b_d)
                act.dma_start(hs8[:, 0:2], smear_d.rearrange("(c h) -> h c", c=2),
                               allow_slow_non_contiguous=True).then_inc(loads_rest.sem, 16)
                act.dma_start(hs8[:, 2:4], log_scale_d.rearrange("(c h) -> h c", c=2),
                               allow_slow_non_contiguous=True).then_inc(loads_rest.sem, 16)
                act.wait_ge(consts.sem, 11)
                act.activation(warm[:, :], half[:, 0:1], ACT.Tanh).then_inc(sc_a.sem, 1)
                act.wait_ge(loads_rest.sem, 16 * N_REST)
                act.activation(hs8[:, 4:6], hs8[:, 2:4], ACT.Exp, scale=-2.0).then_inc(sc_a.sem, 1)
                act.wait_ge(sc_a.sem, 2)
                act.activation(hs8[:, 2:4], hs8[:, 0:2], ACT.Exp, scale=-1.0).then_inc(sc_a.sem, 1)
                act.wait_ge(sc_a.sem, 3)
                act.activation(hs8[:, 0:2], hs8[:, 0:2], ACT.Exp).then_inc(sc_a.sem, 1)
                for s in (yT_ready, xi_a):
                    act.sem_inc(s.sem, s.credit)
                act.wait_ge(bx.sem, 1)
                with act.Fori(0, B) as b:
                    act.wait_ge(yT_ps.sem, yT_ps.value(act, b))
                    act.wait_ge(xi_ps.sem, xi_ps.before(act, b))
                    act.activation(YT[:, :], PS[:, 0, :], ACT.Identity, scale=gam[:, 0:1],
                                   bias=bet[:, 0:1]).then_inc(yT_ready.sem, 1)
                    for c in (0, 2, 4):
                        act.wait_ge(xi_ps.sem, xi_ps.value(act, b, c + 1))
                        act.activation(XI[:, 0:S, c, bass.ds(b, 1)].rearrange("p s o -> p (s o)"), PS[:, 1 + c, :], ACT.Identity,
                                       scale=S_gru, bias=bX[:, c:c + 1]).then_inc(xi_a.sem, 1)

            @block.vector
            def _(dve):
                dve.wait_ge(loads_x.sem, 16 * B)

                def keep(i):
                    src, dst, f = alljobs[i]
                    dve.wait_ge(turned.sem, i + 1)
                    dve.tensor_scalar(dst, PS[0:src.shape[1], i % 8, 0:src.shape[0]], f, None,
                                      ALU.mult).then_inc(kept.sem, 1)
                x_moments(dve, STb, MVb, stats, aggr, mv_kept)
                for i in range(NJ):
                    keep(i)
                dve.wait_ge(kept.sem, NJ)
                dve.tensor_reduce(mx[:, :], whhT[:, :, :].rearrange("p a b -> p (a b)"), AX.X, ALU.max,
                                  apply_absolute_value=True).then_inc(sc_v.sem, 1)
                dve.wait_ge(sc_p.sem, 1)
                dve.tensor_reduce(mrow[:, :], PS[0:1, 0, 0:P], AX.X, ALU.max).then_inc(sc_v.sem, 1)
                dve.wait_ge(sc_v.sem, 2)
                dve.tensor_scalar(mrow[:, :], mrow[:, :], 2.0 ** -60, None, ALU.max).then_inc(sc_v.sem, 1)
                dve.wait_ge(sc_v.sem, 3)
                dve.tensor_scalar(mrow[:, :].bitcast(I32), mrow[:, :].bitcast(I32), 0x7f800000, None,
                                  ALU.bitwise_and).then_inc(sc_v.sem, 1)
                dve.wait_ge(sc_p.sem, 2)
                dve.tensor_scalar(kscale[:, 0:1], PS[:, 1, 0:1], 2.0 ** -15, None, ALU.mult).then_inc(sc_v.sem, 1)
                dve.tensor_scalar(kscale[:, 1:2], PS[:, 1, 0:1], 2.0 ** -14, None, ALU.mult).then_inc(sc_v.sem, 1)
                dve.wait_ge(sc_v.sem, 6)
                dve.reciprocal(kscale[:, 2:3], kscale[:, 1:2]).then_inc(sc_v.sem, 1)
                dve.wait_ge(sc_a.sem, 4)
                dve.tensor_scalar(hs8[:, 0:4], hs8[:, 0:4], 1.0, None, ALU.add).then_inc(hv.sem, 1)
                dve.tensor_scalar(hs8[:, 4:6], hs8[:, 4:6], float(DH) ** -0.5, None, ALU.mult).then_inc(hv.sem, 1)
                dve.wait_ge(hv.sem, 2)
                dve.reciprocal(hs8[:, 0:4], hs8[:, 0:4]).then_inc(hv.sem, 1)
                dve.wait_ge(sc_p.sem, 3)
                dve.tensor_copy(qsc[:, :], PS[:, 2, 0:6]).then_inc(sc_v.sem, 1)
                dve.wait_ge(sc_v.sem, 8)
                flat = lambda w: w[:, :, :].rearrange("p a b -> p (a b)")
                dve.tensor_scalar(flat(whhT), flat(whhT), S_gru, None, ALU.mult).then_inc(sc_v.sem, 1)
                dve.wait_ge(sc_v.sem, 9)
                dve.tensor_copy(flat(W1), flat(whhT)).then_inc(sc_v.sem, 1)
                dve.wait_ge(sc_v.sem, 10)
                dve.tensor_tensor(flat(W2), flat(whhT), flat(W1), ALU.subtract).then_inc(sc_v.sem, 1)
                dve.tensor_tensor(bih[:, 0:4], bih[:, 0:4], bhh[:, 0:4], ALU.add).then_inc(sc_v.sem, 1)
                dve.wait_ge(sc_v.sem, 12)
                dve.tensor_scalar(bX[:, :], bih[:, :], S_gru, None, ALU.mult).then_inc(bx.sem, 1)
                dve.wait_ge(rstd.sem, 1)
                dve.wait_ge(bx.sem, 1)
                dve.sem_inc(xi_v.sem, xi_v.credit)
                with dve.Fori(0, B) as b:
                    dve.wait_ge(yT_ps.sem, yT_ps.before(dve, b))
                    for t in range(NT):
                        i = dve.snap(b * NT + t)
                        dve.tensor_scalar(YN[:, t, :], X[:, bass.ds(i, 1), :].rearrange("p o d -> p (o d)"),
                                          MV[:, bass.ds(i, 1), 0:1].rearrange("p o k -> p (o k)"), RR[:, bass.ds(i, 1)],
                                          ALU.subtract, ALU.mult).then_inc(y_ready.sem, 1)
                    for c in (1, 3, 5):
                        dve.wait_ge(xi_ps.sem, xi_ps.value(dve, b, c + 1))
                        dve.tensor_scalar(XI[:, 0:S, c, bass.ds(b, 1)].rearrange("p s o -> p (s o)"), PS[:, 1 + c, :], S_gru,
                                          bX[:, c:c + 1], ALU.mult, ALU.add).then_inc(xi_v.sem, 1)

        ctx = ExitStack()
        with ctx:
            bh = sb(ctx, "bh", [P, U, NSTEP])
            XS = sb(ctx, "XS", [P, 2, U, 6, B])
            HR = sb(ctx, "HR", [P, 2, U, NSTEP])
            G1 = sb(ctx, "G1", [P, HC, B], FP16)
            G2 = sb(ctx, "G2", [P, HC, B], FP16)
            tr = sb(ctx, "tr", [P, NSTEP])
            tz = sb(ctx, "tz", [P, NSTEP])
            u_ = sb(ctx, "u_", [P, NSTEP])
            v_ = sb(ctx, "v_", [P, NSTEP])
            n_ = sb(ctx, "n_", [P, NSTEP])
            zg = sb(ctx, "zg", [P, NSTEP])
            zn = sb(ctx, "zn", [P, NSTEP])
            warm = sb(ctx, "warm2", [P, 1])
            free = sb(ctx, "free", [P, 2])
            pR = PS[:, 0:2, :]
            pZ = PS[:, 2:4, :]
            pN = PS[:, 4:6, :]

            xs_in = [signal(f"xs_in{p}") for p in range(2)]
            hr_out = [signal(f"hr_out{p}") for p in range(2)]
            bh_start = signal("bh_start")
            bh_ready = signal("bh_ready")
            injected = signal("injected")
            r_ps = signal("r_ps")
            hn_tr = signal("hn_ps_and_tr")
            z_ps = signal("z_ps")
            tz_ready = signal("tz_ready")
            u_ready = signal("u_ready")
            v_ready = signal("v_ready")
            n_ready = signal("n_ready")
            zg_ready = signal("zg_ready")
            zn_ready = signal("zn_ready")
            g1_ready = signal("g1_ready")
            g_ready = signal("g_ready")
            g2_ready = signal("g2_ready")
            warmed = signal("gru_warm")

            block = ctx.enter_context(nc.Block())

            @block.sync
            def _(sp):
                for p in range(2):
                    sp.dma_start(XS[:, p], XI[:, p * U:(p + 1) * U]).then_inc(xs_in[p].sem, 16)
                with sp.Fori(0, S // (2 * U)) as q:
                    for p in range(2):
                        sp.wait_ge(g_ready.sem, sp.snap(q * (2 * U) + U * (p + 1)))
                        at = sp.snap(q * (2 * U) + U * p)
                        sp.dma_start(HS[:, bass.ds(at, U)].rearrange("p u c b -> p u (c b)"),
                                     HR[:, p]).then_inc(hr_out[p].sem, 16)
                        sp.dma_start(XS[:, p], XI[:, bass.ds(sp.snap(q * (2 * U) + U * (p + 2)), U)]).then_inc(xs_in[p].sem, 16)
                for p in range(2):
                    sp.wait_ge(hr_out[p].sem, 16 * (S // (2 * U) + 1))
                    sp.wait_ge(xs_in[p].sem, 16 * (S // (2 * U) + 1))

            @block.tensor
            def _(pe):
                gates = {"r": (pR, 0), "z": (pZ, 1), "n": (pN, 2)}
                by_g1 = [(mc, kc, W) for mc in range(HC) for kc in range(HC) for W in (W1, W2)]
                by_g2 = [(mc, kc, W1) for mc in range(HC) for kc in range(HC)]

                def product(gate, p, k, mc, kc, W, G):
                    bank, g = gates[gate]
                    w = (HC * g + mc) * P
                    o = NSTEP * k + B * mc
                    return pe.matmul(bank[:, p, o:o + B], W[:, kc, w:w + P], G[:, kc, :],
                                     start=False, stop=True, skip_group_check=True)

                def inject(gate, p):
                    src = {"r": XS[:, p, :, 0:2, :], "z": XS[:, p, :, 2:4, :], "n": bh[:, :, :]}[gate]
                    return pe.matmul(gates[gate][0][:, p, 0:U * NSTEP], ident[:, :], src,
                                     start=True, stop=False, skip_group_check=True)
                pe.wait_ge(bh_ready.sem, 2)
                pe.wait_ge(xs_in[0].sem, 16)
                for gate in "rnz":
                    inject(gate, 0)
                with pe.Fori(0, S // (2 * U)) as q:
                    for p in range(2):
                        for k in range(U):
                            n = pe.snap(q * (2 * U) + (p * U + k + 1))
                            pe.wait_ge(g1_ready.sem, n)
                            for w in by_g1:
                                product("r", p, k, *w, G1)
                            for w in by_g1[:3]:
                                product("n", p, k, *w, G1)
                            pe.wait_ge(g2_ready.sem, n)
                            for w in by_g2:
                                last = product("r", p, k, *w, G2)
                            last.then_inc(r_ps.sem, 1)
                            for w in by_g1[3:]:
                                product("n", p, k, *w, G1)
                            for w in by_g2:
                                last = product("n", p, k, *w, G2)
                            last.then_inc(hn_tr.sem, 1)
                            for w in by_g1:
                                product("z", p, k, *w, G1)
                            for w in by_g2:
                                last = product("z", p, k, *w, G2)
                            last.then_inc(z_ps.sem, 1)
                            if k == 1:
                                pe.wait_ge(xs_in[1 - p].sem, pe.snap(q * 16 + 16 * (p + 1)))
                            if 1 <= k <= 3:
                                inject("rnz"[k - 1], 1 - p).then_inc(injected.sem, 1)

            @block.scalar
            def _(act):
                act.activation(warm[:, :], half[:, 0:1], ACT.Tanh).then_inc(warmed.sem, 1)
                gate_scale = act.alloc_register("gate_scale")
                n_scale = act.alloc_register("n_scale")
                act.load(gate_scale, kscale[0:1, 0:1].bitcast(I32))
                act.load(n_scale, kscale[0:1, 1:2].bitcast(I32))
                with act.Fori(0, S // (2 * U)) as q:
                    for p in range(2):
                        for k in range(U):
                            n = act.snap(q * (2 * U) + (p * U + k + 1))
                            o = NSTEP * k
                            act.wait_ge(r_ps.sem, n)
                            act.activation(tr[:, :], pR[:, p, o:o + NSTEP], ACT.Tanh, scale=gate_scale).then_inc(hn_tr.sem, 1)
                            act.wait_ge(z_ps.sem, n)
                            act.activation(tz[:, :], pZ[:, p, o:o + NSTEP], ACT.Tanh, scale=gate_scale).then_inc(tz_ready.sem, 1)
                            act.wait_ge(v_ready.sem, n)
                            act.activation(n_[:, :], v_[:, :], ACT.Tanh, scale=n_scale).then_inc(n_ready.sem, 1)

            @block.vector
            def _(dve):
                dve.memset(bh[:, :, :], 0.0).then_inc(bh_start.sem, 1)
                dve.memset(HR[:, :, :, :], 0.0).then_inc(bh_start.sem, 1)
                dve.memset(G1[:, :, :], 0.0).then_inc(g1_ready.sem, 1)
                dve.memset(G2[:, :, :], 0.0).then_inc(g2_ready.sem, 1)
                dve.tensor_scalar(bhh[:, 4:6], bhh[:, 4:6], S_gru, 0.5, ALU.mult, ALU.mult).then_inc(bh_start.sem, 1)
                dve.wait_ge(bh_start.sem, 3)
                for c in range(HC):
                    x = bh[:, :, c * B:(c + 1) * B]
                    dve.tensor_scalar(x, x, bhh[:, 4 + c:5 + c], None, ALU.add).then_inc(bh_ready.sem, 1)
                for p in range(2):
                    dve.memset(free[:, p:p + 1], 0.0).then_inc(hr_out[p].sem, 16)
                flat = lambda g: g[:, :, :].rearrange("p c b -> p (c b)")

                def step(q, p, k):
                    n = dve.snap(q * (2 * U) + (p * U + k + 1))
                    n2 = dve.snap(q * (4 * U) + 2 * (p * U + k + 1))
                    o = NSTEP * k
                    before = HR[:, p, k - 1, :] if k else HR[:, 1 - p, U - 1, :]
                    dve.wait_ge(hn_tr.sem, n2)
                    dve.scalar_tensor_tensor(u_[:, :], tr[:, :], 1.0, pN[:, p, o:o + NSTEP],
                                             ALU.add, ALU.mult).then_inc(u_ready.sem, 1)
                    dve.wait_ge(u_ready.sem, n)
                    dve.tensor_tensor(v_[:, :], u_[:, :], XS[:, p, k, 4:6, :].rearrange("p c b -> p (c b)"),
                                      ALU.add).then_inc(v_ready.sem, 1)
                    dve.wait_ge(tz_ready.sem, n)
                    dve.scalar_tensor_tensor(zg[:, :], tz[:, :], 1.0, before, ALU.add, ALU.mult).then_inc(zg_ready.sem, 1)
                    dve.wait_ge(n_ready.sem, n)
                    dve.scalar_tensor_tensor(zn[:, :], tz[:, :], 1.0, n_[:, :], ALU.subtract, ALU.mult).then_inc(zn_ready.sem, 1)
                    dve.wait_ge(zn_ready.sem, n)
                    dve.scalar_tensor_tensor(flat(G1), zg[:, :], 0.5, zn[:, :], ALU.mult, ALU.subtract).then_inc(g1_ready.sem, 1)
                    dve.scalar_tensor_tensor(HR[:, p, k, :], zg[:, :], 0.5, zn[:, :], ALU.mult, ALU.subtract).then_inc(g_ready.sem, 1)
                    dve.wait_ge(g_ready.sem, n)
                    dve.tensor_tensor(flat(G2), HR[:, p, k, :], flat(G1), ALU.subtract).then_inc(g2_ready.sem, 1)
                with dve.Fori(0, S // (2 * U)) as q:
                    for p in range(2):
                        for k in range(U):
                            if k == 0:
                                dve.wait_ge(hr_out[p].sem, dve.snap(q * 16 + 16))
                            step(q, p, k)
        xi_scope.close()

        def layer_norm_scale(eng, mv, rt, rs, step, b, k):
            eng.tensor_tensor(rt[:, :], mv[:, :, 1], eps[:, :], ALU.add).then_inc(step.sem, 1)
            eng.wait_ge(step.sem, step.value(eng, b, k + 1))
            eng.tensor_tensor(rs[:, :], rt[:, :], half[:, 0:NT], ALU.pow).then_inc(step.sem, 1)

        ctx = ExitStack()
        with ctx:
            HB = sb(ctx, "HB", [P, HC, S])
            X0 = sb(ctx, "X0", [P, NT, D])
            X0b = sb(ctx, "X0b", [P, NT, D])
            T = sb(ctx, "T", [P, NT, D])
            N1 = sb(ctx, "N1", [P, NT, D])
            XF = sb(ctx, "XF", [P, NT, D])
            XFT = sb(ctx, "XFT", [P, S])
            LG = sb(ctx, "LG", [P, NT, E])
            LM = sb(ctx, "LM", [P, NT, 8])
            LI = sb(ctx, "LI", [P, NT, 8], U32)
            LF = sb(ctx, "LF", [P, NT])
            LA = sb(ctx, "LA", [P, NT, E * R])
            ML = sb(ctx, "ML", [P, NT, E * R])
            LAT = sb(ctx, "LAT", [E * R, S])
            INT = sb(ctx, "INT", [P, FC, S])
            T2 = sb(ctx, "T2", [P, NT, D])
            N2 = sb(ctx, "N2", [P, NT, D])
            sets = []
            for i in range(3):
                sets.append((sb(ctx, f"st{i}", [P, NT, 6]), sb(ctx, f"mv{i}", [P, NT, 2]),
                             sb(ctx, f"rt{i}", [P, NT]), sb(ctx, f"rs{i}", [P, NT])))
            warm = sb(ctx, "warm3", [P, 1])
            p_gy = PS[:, 0, :].rearrange("p (t d) -> p t d", t=NT)
            p_xfT = PS[:, 1, :]
            p_ga = PS[:, 2, 0:NT * (E + E * R)].rearrange("p (t c) -> p t c", t=NT)
            p_laT = PS[0:E * R, 3, :]
            p_base = PS[:, 4:7, :]
            p_dn = PS[:, 7, :].rearrange("p (t d) -> p t d", t=NT)

            warmed = signal("ffn_warm")
            hb = signal("hb_copied", HC)
            x0 = signal("x0_ready", NT)
            x0b = signal("x0b_ready")
            gy = signal("gru_out_ps", 1, 1)
            t_sum = signal("gru_sum_ready")
            st = [signal(f"c_stats{i}", NT) for i in range(3)]
            mv = [signal(f"c_moments{i}", NT) for i in range(3)]
            rs = [signal(f"c_scale{i}", 2) for i in range(3)]
            nn = signal("n1_ready", NT)
            x1 = signal("x1_ready")
            xf = signal("xf_ready", NT)
            xfT_ps = signal("xfT_ps")
            xfT = signal("xfT_ready")
            ga = signal("gate_lora_ps")
            lg = signal("logits_ready", 2)
            lm = signal("logit_max_ready", NT)
            li = signal("expert_index_ready", NT)
            lf = signal("expert_number_ready")
            ml = signal("masked_lora_ready", NT)
            laT_ps = signal("loraT_ps")
            laT = signal("loraT_ready")
            base = signal("base_ps", FC)
            inter = signal("inter_ready", FC, FC)
            dn = signal("ffn_out_ps")
            t2 = signal("ffn_sum_ready")
            n2 = signal("n2_ready", NT)
            x2 = signal("x2_ready")

            block = ctx.enter_context(nc.Block())

            @block.gpsimd
            def _(pool):
                with pool.Fori(0, B) as b:
                    pool.wait_ge(x0.sem, x0.value(pool, b))
                    for t in range(NT):
                        last = pool.tensor_tensor(X0b[:, t, :], X0[:, t, :], bout[:, :], ALU.add)
                    last.then_inc(x0b.sem, 1)
                    for i in range(3):
                        _, m, r_t, r_s = sets[i]
                        pool.wait_ge(mv[i].sem, mv[i].value(pool, b))
                        layer_norm_scale(pool, m, r_t, r_s, rs[i], b, 0)

            @block.tensor
            def _(pe):
                pe.sem_inc(gy.sem, gy.credit)
                with pe.Fori(0, B) as b:
                    pe.wait_ge(hb.sem, hb.value(pe, b))
                    for t in range(NT):
                        for c in range(HC):
                            last = pe.matmul(p_gy[:, t, :], HB[:, c, t * P:(t + 1) * P], woutT[:, c, :],
                                             start=(c == 0), stop=(c == HC - 1))
                    last.then_inc(gy.sem, 1)
                    pe.wait_ge(xf.sem, xf.value(pe, b))
                    for t in range(NT):
                        last = pe.transpose(p_xfT[:, t * P:(t + 1) * P], XF[:, t, :], ident[:, :])
                    last.then_inc(xfT_ps.sem, 1)
                    pe.wait_ge(xfT.sem, xfT.value(pe, b))
                    for t in range(NT):
                        last = pe.matmul(p_ga[:, t, :], XFT[:, t * P:(t + 1) * P], gaT[:, :], start=True, stop=True)
                    last.then_inc(ga.sem, 1)
                    for c in range(FC):
                        if c in (0, 3):
                            pe.wait_ge(inter.sem, inter.value(pe, b, c // 3))
                        pe.matmul(p_base[:, c % 3, :], wiT[:, c * P:(c + 1) * P], XFT[:, :], start=True, stop=False)
                        if c == 0:
                            pe.wait_ge(ml.sem, ml.value(pe, b))
                            for t in range(NT):
                                last = pe.transpose(p_laT[:, t * P:(t + 1) * P], ML[:, t, :], ident[:, :])
                            last.then_inc(laT_ps.sem, 1)
                            pe.wait_ge(laT.sem, laT.value(pe, b))
                        pe.matmul(p_base[:, c % 3, :], lbT[:, c * P:(c + 1) * P], LAT[:, :],
                                  start=False, stop=True).then_inc(base.sem, 1)
                    for t in range(NT):
                        for c in range(FC):
                            if t == 0:
                                pe.wait_ge(inter.sem, inter.value(pe, b, c + 1))
                            last = pe.matmul(p_dn[:, t, :], INT[:, c, t * P:(t + 1) * P], woT[:, c, :],
                                             start=(c == 0), stop=(c == FC - 1))
                    last.then_inc(dn.sem, 1)

            @block.scalar
            def _(act):
                act.activation(warm[:, :], half[:, 0:1], ACT.Tanh).then_inc(warmed.sem, 1)
                act.sem_inc(inter.sem, inter.credit)
                with act.Fori(0, B) as b:
                    act.wait_ge(gy.sem, gy.before(act, b))
                    for c in range(HC):
                        act.activation(HB[:, c, :], HS[:, :, c, bass.ds(b, 1)].rearrange("p s o -> p (s o)"),
                                       ACT.Copy).then_inc(hb.sem, 1)
                    act.wait_ge(xfT_ps.sem, xfT_ps.value(act, b))
                    act.activation(XFT[:, :], p_xfT, ACT.Copy).then_inc(xfT.sem, 1)
                    act.wait_ge(laT_ps.sem, laT_ps.value(act, b))
                    act.activation(LAT[:, :], p_laT, ACT.Copy).then_inc(laT.sem, 1)
                    for c in range(FC):
                        act.wait_ge(base.sem, base.value(act, b, c + 1))
                        act.activation(INT[:, c, :], p_base[:, c % 3, :], ACT.Relu,
                                       bias=wib[:, c:c + 1]).then_inc(inter.sem, 1)

            @block.vector
            def _(dve):
                def moments(i, src, b):
                    s_t, m, _, _ = sets[i]
                    for t in range(NT):
                        dve.bn_stats(s_t[:, t, :], src(t)).then_inc(st[i].sem, 1)
                    hold(dve, st[i].sem, st[i].value(dve, b))
                    for t in range(NT):
                        dve.bn_aggr(m[:, t, :], s_t[:, t, :]).then_inc(mv[i].sem, 1)

                def normal(i, dst, src, b, done):
                    _, m, _, r_s = sets[i]
                    dve.wait_ge(rs[i].sem, rs[i].value(dve, b))
                    for t in range(NT):
                        dve.tensor_scalar(dst[:, t, :], src(t), m[:, t, 0:1], r_s[:, t:t + 1],
                                          ALU.subtract, ALU.mult).then_inc(done.sem, 1)
                with dve.Fori(0, B) as b:
                    tiles = lambda: X[:, bass.ds(dve.snap(b * NT), NT), :]
                    tile = lambda t: X[:, bass.ds(dve.snap(b * NT + t), 1), :].rearrange("p o d -> p (o d)")
                    for t in range(NT):
                        i = dve.snap(b * NT + t)
                        dve.tensor_scalar(X0[:, t, :], tile(t), MV[:, bass.ds(i, 1), 0:1].rearrange("p o k -> p (o k)"),
                                          R1[:, bass.ds(i, 1)], ALU.subtract, ALU.mult).then_inc(x0.sem, 1)
                    dve.wait_ge(x0b.sem, x0b.value(dve, b))
                    dve.wait_ge(gy.sem, gy.value(dve, b))
                    dve.tensor_tensor(T[:, :, :], X0b[:, :, :], p_gy, ALU.add).then_inc(t_sum.sem, 1)
                    dve.wait_ge(t_sum.sem, t_sum.value(dve, b))
                    moments(0, lambda t: T[:, t, :], b)
                    normal(0, N1, lambda t: T[:, t, :], b, nn)
                    dve.wait_ge(nn.sem, nn.value(dve, b))
                    dve.tensor_tensor(tiles(), tiles(), N1[:, :, :], ALU.add).then_inc(x1.sem, 1)
                    hold(dve, x1.sem, x1.value(dve, b))
                    moments(1, tile, b)
                    normal(1, XF, tile, b, xf)
                    dve.wait_ge(ga.sem, ga.value(dve, b))
                    dve.tensor_tensor(LG[:, :, :], p_ga[:, :, 0:E], gateb[:, :].unsqueeze(1).to_broadcast([P, NT, E]),
                                      ALU.add).then_inc(lg.sem, 1)
                    dve.tensor_copy(LA[:, :, :], p_ga[:, :, E:]).then_inc(lg.sem, 1)
                    hold(dve, lg.sem, lg.value(dve, b))
                    for t in range(NT):
                        dve.max(LM[:, t, :], LG[:, t, :]).then_inc(lm.sem, 1)
                    hold(dve, lm.sem, lm.value(dve, b))
                    for t in range(NT):
                        dve.max_index(LI[:, t, :], LM[:, t, :], LG[:, t, :]).then_inc(li.sem, 1)
                    dve.wait_ge(li.sem, li.value(dve, b))
                    dve.tensor_copy(LF[:, :], LI[:, :, 0]).then_inc(lf.sem, 1)
                    dve.wait_ge(lf.sem, lf.value(dve, b))
                    for t in range(NT):
                        dve.scalar_tensor_tensor(ML[:, t, :], iota_e[:, :, :].rearrange("p e r -> p (e r)"), LF[:, t:t + 1],
                                                 LA[:, t, :], ALU.is_equal, ALU.mult).then_inc(ml.sem, 1)
                    dve.wait_ge(dn.sem, dn.value(dve, b))
                    dve.tensor_tensor(T2[:, :, :], p_dn, wob[:, :].unsqueeze(1).to_broadcast([P, NT, D]),
                                      ALU.add).then_inc(t2.sem, 1)
                    dve.wait_ge(t2.sem, t2.value(dve, b))
                    moments(2, lambda t: T2[:, t, :], b)
                    normal(2, N2, lambda t: T2[:, t, :], b, n2)
                    dve.wait_ge(n2.sem, n2.value(dve, b))
                    dve.tensor_tensor(tiles(), tiles(), N2[:, :, :], ALU.add).then_inc(x2.sem, 1)

        gru_scope.close()

        KM, KF = 99, 102
        NG4 = HEADS // 4
        ctx = ExitStack()
        with ctx:
            qd = nc.dram_tensor("q_parts", (B, 3, DE, S), BF16).ap()
            kd = nc.dram_tensor("k_parts", (B, 3, DE, S), BF16).ap()
            ad = nc.dram_tensor("k_extra", (B, HEADS * 6, S), BF16).ap()
            QS = sb(ctx, "QS", [KF, HEADS, S], BF16)
            KS = sb(ctx, "KS", [KF, HEADS, S], BF16)
            VV = sb(ctx, "VV", [P, NT, HEADS, 32])
            SP = sb(ctx, "SP", [P, NT, DE])
            PT = sb(ctx, "PT", [P, 2, 4, S])
            XN = sb(ctx, "XN", [P, NT, D])
            XT = sb(ctx, "XT", [P, S])
            QF = sb(ctx, "QF", [P, 2, S])
            KF_ = sb(ctx, "KF_", [P, 2, S])
            KK = sb(ctx, "KK", [P, 2, S])
            PQ = sb(ctx, "PQ", [P, 2, 3, S], BF16)
            PK = sb(ctx, "PK", [P, 2, 3, S], BF16)
            RES = sb(ctx, "RES", [P, 4, S])
            YB = sb(ctx, "YB", [P, NT, HEADS])
            SG = sb(ctx, "SG", [P, NT, HEADS])
            PR = sb(ctx, "PR", [P, NT, HEADS])
            KA = sb(ctx, "KA", [P, NT, HEADS, 6], BF16)
            KAT = sb(ctx, "KAT", [HEADS * 6, S], BF16)
            PB = sb(ctx, "PB", [P, DE])
            TH = sb(ctx, "TH", [P, DE])
            MX = sb(ctx, "MX", [P, 4, NT])
            MR = sb(ctx, "MR", [P, 4, NT])
            QA = sb(ctx, "QA", [P, 4, NT, 6], BF16)
            OT = sb(ctx, "OT", [P, S])
            RS_ = sb(ctx, "RS_", [P, NT, 4])
            ON = sb(ctx, "ON", [P, NT, HEADS, DH])
            GT = sb(ctx, "GT", [P, 2, S])
            T = sb(ctx, "T_a", [P, NT, D])
            N1 = sb(ctx, "N1_a", [P, NT, D])
            N2 = sb(ctx, "N2_a", [P, NT, D])
            STa = sb(ctx, "STa", [P, NT, 6])
            MVa = sb(ctx, "MVa", [P, NT, 2])
            rta = sb(ctx, "rta", [P, B * NT])
            sets = []
            for i in range(2):
                sets.append((sb(ctx, f"sta{i}", [P, NT, 6]), sb(ctx, f"mva{i}", [P, NT, 2]),
                             sb(ctx, f"rt_a{i}", [P, NT]), sb(ctx, f"rs_a{i}", [P, NT])))
            tri = sb(ctx, "tri", [P, P])
            ones = sb(ctx, "ones_a", [P, P])
            maskU = sb(ctx, "maskU", [P, P], BF16)
            maskL = sb(ctx, "maskL", [P, P], BF16)
            bqs = sb(ctx, "bqs", [P, 2])
            warm = sb(ctx, "warm4", [P, 1])

            p_s = [PS[:, 0:2, :], PS[:, 2:4, :]]
            p_o = PS[:, 4, :]
            p_m = PS[:, 5, :]
            p_a = PS[:, 6, :]
            p_b = PS[:, 7, :]

            warmed = signal("att_warm")
            acon = signal("att_consts")
            acon2 = signal("q_bias_ready")
            astats = signal("att_x_stats", NT)
            aaggr = signal("att_x_aggr", NT)
            amv_kept = signal("att_x_moments_kept")
            arst = signal("att_rstd_steps")
            xn = signal("xn_ready", NT)
            xnT_ps = signal("xnT_ps")
            xnT = signal("xnT_ready")
            y_ps = signal("y_ps")
            yb = signal("yb_ready")
            th = signal("gate_tanh_ready")
            sg = signal("gate_sigmoid_ready")
            qk_ps = signal("qk_ps", 4)
            qk = signal("qk_ready", 4)
            kk1 = signal("k_scaled", 2)
            kk2 = signal("k_smeared", 2)
            part1 = signal("part1_ready", 4)
            rest1 = signal("rest1_ready", 4)
            part2 = signal("part2_ready", 4)
            part3 = signal("part3_ready", 4)
            vp_ps = signal("vp_ps", NT)
            v_kept = signal("v_kept", NT)
            pb = signal("pb_ready", NT)
            pth = signal("silu_tanh_ready", NT)
            sp_ = signal("silu_ready", NT)
            pos_ps = signal("pos_ps")
            ka = signal("ka_ready", 5)
            kaT_ps = signal("kaT_ps")
            kaT = signal("kaT_ready")
            parts_out = signal("parts_to_dram", 16 * 5)
            stack_in = signal("stacks_in", 16 * 13)
            s_ps = signal("score_ps", 8 * NG4)
            mx_ = signal("max_ready", 8 * NG4)
            qa = signal("max_parts_ready", 5 * NG4)
            m_ps = signal("max_rows_ps", 2 * NG4)
            m_in = signal("max_rows_ready", 2 * NG4)
            e_ps = signal("score_minus_max_ps", 8 * NG4)
            ex = signal("exp_ready", 8 * NG4)
            o_ps = signal("o_ps", NG4)
            o_kept = signal("o_kept", NG4)
            oT_ps = signal("oT_ps", NG4)
            rden = signal("inverse_sum_ready", NG4)
            on = signal("o_normal", NG4)
            gated = signal("gated_ready")
            gT_ps = signal("gatedT_ps", 2)
            gT = signal("gatedT_ready", 2)
            w_ps = signal("att_out_ps")
            t_kept = signal("att_out_kept")
            st = [signal(f"a_stats{i}", NT) for i in range(2)]
            mv = [signal(f"a_moments{i}", NT) for i in range(2)]
            rs = [signal(f"a_scale{i}", 2) for i in range(2)]
            n1 = signal("a_n1_ready", NT)
            n1w = signal("a_n1w_ready", 2)
            n2 = signal("a_n2_ready", NT)
            x3 = signal("x3_ready")

            block = ctx.enter_context(nc.Block())

            def over_batches(eng, project, attend):
                with eng.Fori(0, B) as b:
                    project(b)
                    attend(b)

            @block.sync
            def _(sp):
                def project(b):
                    at = bass.ds(b, 1)
                    one = lambda ap: ap.rearrange("o a n -> (o a) n") if len(ap.shape) == 3 else ap.rearrange("o s a n -> (o s) a n")
                    for i, (parts, dram) in enumerate(((PQ, qd), (PQ, qd), (PK, kd), (PK, kd))):
                        c = i % 2
                        sp.wait_ge(part3.sem, part3.value(sp, b, i + 1))
                        sp.dma_start(one(dram[at])[:, c * P:(c + 1) * P, :].rearrange("s p n -> p s n"),
                                     parts[:, c, :, :]).then_inc(parts_out.sem, 16)
                    sp.wait_ge(kaT.sem, kaT.value(sp, b))
                    sp.dma_start(one(ad[at]), KAT[:, :]).then_inc(parts_out.sem, 16)
                    sp.wait_ge(parts_out.sem, parts_out.value(sp, b))
                    def head_rows(dram, s):
                        return one(dram[at])[s, :, :].rearrange("(h d) n -> d h n", d=DH)
                    for r, (qp, kp) in enumerate(((0, 0), (0, 1), (0, 2), (1, 0), (1, 1), (2, 0))):
                        sp.dma_start(QS[r * DH:(r + 1) * DH, :, :], head_rows(qd, qp)).then_inc(stack_in.sem, 16)
                        sp.dma_start(KS[r * DH:(r + 1) * DH, :, :], head_rows(kd, kp)).then_inc(stack_in.sem, 16)
                    sp.dma_start(KS[96:KF, :, :], one(ad[at]).rearrange("(h r) n -> r h n", r=6)).then_inc(stack_in.sem, 16)

                with sp.Fori(0, B) as b:
                    project(b)

            @block.gpsimd
            def _(pool):
                pool.memset(tri[:, :], 1.0).then_inc(acon.sem, 1)
                pool.memset(ones[:, :], 1.0).then_inc(acon.sem, 1)
                pool.memset(maskU[:, :], 0.0).then_inc(acon.sem, 1)
                pool.memset(maskL[:, :], 0.0).then_inc(acon.sem, 1)
                pool.memset(VV[:, :, :, DH:32], 0.0).then_inc(acon.sem, 1)
                pool.memset(KA[:, :, :, :], 1.0).then_inc(acon.sem, 1)
                pool.memset(QA[:, :, :, :], 1.0).then_inc(acon.sem, 1)
                pool.wait_ge(acon.sem, 7)
                pool.memset(VV[:, :, :, DH:DH + 1], 1.0).then_inc(acon.sem, 1)
                pool.affine_select(out=tri[:, :], in_=tri[:, :], compare_op=ALU.is_ge, fill=0.0, base=0,
                                   pattern=[[1, P]], channel_multiplier=-1).then_inc(acon.sem, 1)
                pool.affine_select(out=maskU[:, :], in_=maskU[:, :], compare_op=ALU.is_ge, fill=NEG_BIG, base=0,
                                   pattern=[[-1, P]], channel_multiplier=1).then_inc(acon.sem, 1)
                pool.affine_select(out=maskL[:, :], in_=maskL[:, :], compare_op=ALU.is_ge, fill=NEG_BIG, base=0,
                                   pattern=[[1, P]], channel_multiplier=-1).then_inc(acon.sem, 1)
                pool.wait_ge(amv_kept.sem, B)
                pool.tensor_scalar(rta[:, :], MV[:, :, 1], EPS, None, ALU.add).then_inc(arst.sem, 1)
                pool.wait_ge(arst.sem, 1)
                pool.tensor_tensor(R1[:, :], rta[:, :], half[:, :], ALU.pow).then_inc(arst.sem, 1)
                pool.wait_ge(arst.sem, 2)
                pool.tensor_tensor(rta[:, :], R1[:, :], R1[:, :], ALU.mult).then_inc(arst.sem, 1)
                pool.wait_ge(arst.sem, 3)
                pool.tensor_tensor(rta[:, :], rta[:, :], MV[:, :, 1], ALU.mult).then_inc(arst.sem, 1)
                pool.wait_ge(arst.sem, 4)
                pool.tensor_scalar(rta[:, :], rta[:, :], EPS, None, ALU.add).then_inc(arst.sem, 1)
                pool.wait_ge(arst.sem, 5)
                pool.tensor_tensor(rta[:, :], rta[:, :], half[:, :], ALU.pow).then_inc(arst.sem, 1)
                pool.wait_ge(arst.sem, 6)
                pool.tensor_tensor(RR[:, :], rta[:, :], R1[:, :], ALU.mult).then_inc(arst.sem, 1)

                def attend(b):
                    for i in range(2):
                        _, m, r_t, r_s = sets[i]
                        pool.wait_ge(mv[i].sem, mv[i].value(pool, b))
                        layer_norm_scale(pool, m, r_t, r_s, rs[i], b, 0)
                with pool.Fori(0, B) as b:
                    attend(b)

            @block.tensor
            def _(pe):
                pe.wait_ge(acon.sem, 11)
                pe.wait_ge(acon2.sem, 2)

                def project(b):
                    pe.wait_ge(xn.sem, xn.value(pe, b))
                    for t in range(NT):
                        last = pe.transpose(p_a[:, t * P:(t + 1) * P], XN[:, t, :], ident[:, :])
                    last.then_inc(xnT_ps.sem, 1)
                    pe.wait_ge(xnT.sem, xnT.value(pe, b))
                    p_y = p_b[:, 0:NT * HEADS].rearrange("p (t h) -> p t h", t=NT)
                    for t in range(NT):
                        last = pe.matmul(p_y[:, t, :], XT[:, t * P:(t + 1) * P], winT[:, 4 * DE:], start=True, stop=True)
                    last.then_inc(y_ps.sem, 1)
                    for c in range(4):
                        if c == 1:
                            pe.wait_ge(yb.sem, yb.value(pe, b))
                        if c >= 2:
                            pe.wait_ge(qk.sem, qk.value(pe, b, c - 1))
                        pe.matmul(PS[:, 6 + c % 2, :], winT[:, c * P:(c + 1) * P], XT[:, :],
                                  start=True, stop=True).then_inc(qk_ps.sem, 1)
                    for t in range(NT):
                        if t < 2:
                            pe.wait_ge(qk.sem, qk.value(pe, b, t + 3))
                        else:
                            pe.wait_ge(pb.sem, pb.value(pe, b, t - 1))
                        pe.matmul(PS[:, 6 + t % 2, :], XT[:, t * P:(t + 1) * P], winT[:, 2 * DE:4 * DE],
                                  start=True, stop=True).then_inc(vp_ps.sem, 1)
                    pe.wait_ge(pb.sem, pb.value(pe, b, NT - 1))
                    pe.wait_ge(sg.sem, sg.value(pe, b))
                    p_p = p_a[:, 0:NT * HEADS].rearrange("p (t h) -> p t h", t=NT)
                    for t in range(NT):
                        for i in range(t + 1):
                            last = pe.matmul(p_p[:, t, :], (tri if i == t else ones)[:, :], SG[:, i, :],
                                             start=(i == 0), stop=(i == t))
                    last.then_inc(pos_ps.sem, 1)
                    pe.wait_ge(pb.sem, pb.value(pe, b))
                    pe.wait_ge(ka.sem, ka.value(pe, b))
                    p_k = p_b.bitcast(BF16)[0:HEADS * 6, 0:S]
                    for t in range(NT):
                        last = pe.transpose(p_k[:, t * P:(t + 1) * P], KA[:, t, :, :].rearrange("p h r -> p (h r)"), identb[:, :])
                    last.then_inc(kaT_ps.sem, 1)

                def attend(b):
                    pe.wait_ge(stack_in.sem, stack_in.value(pe, b))
                    for g in range(NG4):
                        for it in range(NT):
                            n = (it + 1) * P
                            for pair in range(2):
                                u = 2 * it + pair
                                if u >= 2:
                                    pe.wait_ge(mx_.sem, mx_.value(pe, b, 8 * g + u - 1))
                                for i in range(2):
                                    h = 4 * g + 2 * pair + i
                                    q = QS[0:KM, h, it * P:(it + 1) * P]
                                    pe.matmul(p_s[pair][:, i, 0:n], q, KS[0:KM, h, 0:n], start=True, stop=False)
                                    last = pe.matmul(p_s[pair][:, i, n - P:n], identb[:, :], maskU[:, :], start=False, stop=True)
                                last.then_inc(s_ps.sem, 1)
                        pe.wait_ge(qa.sem, qa.value(pe, b, 5 * (g + 1)))
                        for pair in range(2):
                            p_r = p_m.bitcast(BF16)[96:KF, :].rearrange("p (i n) -> p i n", i=2)
                            if pair == 1:
                                pe.wait_ge(m_in.sem, m_in.value(pe, b, 2 * g + 1))
                            for i in range(2):
                                for t in range(NT):
                                    last = pe.transpose(p_r[:, i, t * P:(t + 1) * P], QA[:, 2 * pair + i, t, :], identb[:, :],
                                                        tile_position=(0, 96))
                            last.then_inc(m_ps.sem, 1)
                        pe.wait_ge(m_in.sem, m_in.value(pe, b, 2 * g + 2))
                        for jt in range(NT + 1):
                            if jt < NT:
                                n = S - jt * P
                                for pair in range(2):
                                    u = 2 * jt + pair
                                    if u >= 2:
                                        pe.wait_ge(ex.sem, ex.value(pe, b, 8 * g + u - 1))
                                    for i in range(2):
                                        h = 4 * g + 2 * pair + i
                                        pe.matmul(p_s[pair][:, i, 0:n], KS[0:KF, h, jt * P:(jt + 1) * P],
                                                  QS[0:KF, h, jt * P:S], start=True, stop=False)
                                        last = pe.matmul(p_s[pair][:, i, 0:P], identb[:, :], maskL[:, :], start=False, stop=True)
                                    last.then_inc(e_ps.sem, 1)
                            if jt >= 1:
                                j = jt - 1
                                pe.wait_ge(ex.sem, ex.value(pe, b, 8 * g + 2 * j + 2))
                                for i in range(4):
                                    h = 4 * g + i
                                    last = pe.matmul(p_o[32 * i:32 * i + 32, j * P:S], VV[:, j, h, :], PT[:, j % 2, i, 0:S - j * P],
                                                     start=(j == 0), stop=(j == NT - 1), tile_position=(0, 32 * i),
                                                     skip_group_check=True)
                        last.then_inc(o_ps.sem, 1)
                        pe.wait_ge(o_kept.sem, o_kept.value(pe, b, g + 1))
                        for t in range(NT):
                            last = pe.transpose(p_m[:, t * P:(t + 1) * P], OT[:, t * P:(t + 1) * P], ident[:, :])
                        last.then_inc(oT_ps.sem, 1)
                        pe.wait_ge(on.sem, on.value(pe, b, g + 1))
                    pe.wait_ge(gated.sem, gated.value(pe, b))
                    for c in range(2):
                        for t in range(NT):
                            last = pe.transpose(PS[:, 6 + c, t * P:(t + 1) * P],
                                                ON[:, t, 8 * c:8 * c + 8, :].rearrange("p h d -> p (h d)"), ident[:, :])
                        last.then_inc(gT_ps.sem, 1)
                    pe.wait_ge(gT.sem, gT.value(pe, b))
                    p_w = p_a.rearrange("p (t d) -> p t d", t=NT)
                    for t in range(NT):
                        for c in range(2):
                            last = pe.matmul(p_w[:, t, :], GT[:, c, t * P:(t + 1) * P], waoT[:, c, :], start=(c == 0), stop=(c == 1))
                    last.then_inc(w_ps.sem, 1)
                    pe.wait_ge(t_kept.sem, t_kept.value(pe, b))
                over_batches(pe, project, attend)

            @block.scalar
            def _(act):
                act.activation(warm[:, :], half[:, 0:1], ACT.Tanh).then_inc(warmed.sem, 1)

                act.wait_ge(acon2.sem, 2)

                def project(b):
                    act.wait_ge(xnT_ps.sem, xnT_ps.value(act, b))
                    act.activation(XT[:, :], p_a, ACT.Identity, scale=ilw[:, 0:1], bias=ilb[:, 0:1]).then_inc(xnT.sem, 1)
                    act.wait_ge(yb.sem, yb.value(act, b))
                    act.activation(SG[:, :, :], YB[:, :, :], ACT.Tanh, scale=0.5).then_inc(th.sem, 1)
                    for c in range(4):
                        act.wait_ge(qk_ps.sem, qk_ps.value(act, b, c + 1))
                        if c < 2:
                            act.activation(QF[:, c, :], PS[:, 6 + c, :], ACT.Identity, scale=qsc[:, 4 + c:5 + c],
                                           bias=bqs[:, c:c + 1]).then_inc(qk.sem, 1)
                        else:
                            act.activation(KF_[:, c - 2, :], PS[:, 4 + c, :], ACT.Identity, bias=bqk[:, c:c + 1]).then_inc(qk.sem, 1)
                    act.wait_ge(parts_out.sem, parts_out.before(act, b))
                    for i in range(4):
                        src, dst = (QF, PQ) if i < 2 else (KK, PK)
                        if i < 2:
                            act.wait_ge(qk.sem, qk.value(act, b, i + 1))
                        else:
                            act.wait_ge(kk2.sem, kk2.value(act, b, i - 1))
                        act.activation(dst[:, i % 2, 0, :], src[:, i % 2, :], ACT.Copy).then_inc(part1.sem, 1)
                    for t in range(NT):
                        act.wait_ge(pb.sem, pb.value(act, b, t + 1))
                        act.activation(TH[:, :], PB[:, :], ACT.Tanh, scale=0.5).then_inc(pth.sem, 1)
                    act.wait_ge(kaT_ps.sem, kaT_ps.value(act, b))
                    act.activation(KAT[:, :], p_b.bitcast(BF16)[0:HEADS * 6, 0:S], ACT.Copy).then_inc(kaT.sem, 1)

                def attend(b):
                    for g in range(NG4):
                        for pair in range(2):
                            act.wait_ge(m_ps.sem, m_ps.value(act, b, 2 * g + pair + 1))
                            h = 4 * g + 2 * pair
                            act.activation(QS[96:KF, h:h + 2, :], p_m.bitcast(BF16)[96:KF, :].rearrange("p (i n) -> p i n", i=2),
                                           ACT.Copy).then_inc(m_in.sem, 1)
                        for jt in range(NT):
                            n = S - jt * P
                            for pair in range(2):
                                act.wait_ge(e_ps.sem, e_ps.value(act, b, 8 * g + 2 * jt + pair + 1))
                                act.activation(PT[:, jt % 2, 2 * pair:2 * pair + 2, 0:n], p_s[pair][:, :, 0:n],
                                               ACT.Exp).then_inc(ex.sem, 1)
                        act.wait_ge(o_ps.sem, o_ps.value(act, b, g + 1))
                        act.activation(OT[:, :], p_o, ACT.Copy).then_inc(o_kept.sem, 1)
                    for c in range(2):
                        act.wait_ge(gT_ps.sem, gT_ps.value(act, b, c + 1))
                        act.activation(GT[:, c, :], PS[:, 6 + c, :], ACT.Copy).then_inc(gT.sem, 1)
                over_batches(act, project, attend)

            @block.vector
            def _(dve):
                dve.memset(QS[96:KF, :, :], 1.0).then_inc(acon2.sem, 1)
                dve.tensor_tensor(bqs[:, :], bqk[:, 0:2], qsc[:, 4:6], ALU.mult).then_inc(acon2.sem, 1)
                x_moments(dve, STa, MVa, astats, aaggr, amv_kept)
                dve.wait_ge(arst.sem, 7)

                def tiles(b):
                    return X[:, bass.ds(dve.snap(b * NT), NT), :]

                def project(b):
                    for t in range(NT):
                        at = bass.ds(dve.snap(b * NT + t), 1)
                        dve.tensor_scalar(XN[:, t, :], X[:, at, :].rearrange("p o d -> p (o d)"),
                                          MV[:, at, 0:1].rearrange("p o k -> p (o k)"), RR[:, at],
                                          ALU.subtract, ALU.mult).then_inc(xn.sem, 1)
                    dve.wait_ge(y_ps.sem, y_ps.value(dve, b))
                    dve.tensor_tensor(YB[:, :, :], p_b[:, 0:NT * HEADS].rearrange("p (t h) -> p t h", t=NT),
                                      bvpy[:, 2 * DE:].unsqueeze(1).to_broadcast([P, NT, HEADS]), ALU.add).then_inc(yb.sem, 1)
                    dve.wait_ge(th.sem, th.value(dve, b))
                    dve.tensor_scalar(SG[:, :, :], SG[:, :, :], 0.5, 0.5, ALU.mult, ALU.add).then_inc(sg.sem, 1)

                    def rests(i):
                        src, dst = (QF, PQ) if i < 2 else (KK, PK)
                        c = i % 2
                        dve.wait_ge(part1.sem, part1.value(dve, b, i + 1))
                        dve.tensor_tensor(RES[:, i, :], src[:, c, :], dst[:, c, 0, :], ALU.subtract).then_inc(rest1.sem, 1)
                        dve.wait_ge(rest1.sem, rest1.value(dve, b, i + 1))
                        dve.tensor_copy(dst[:, c, 1, :], RES[:, i, :]).then_inc(part2.sem, 1)
                        dve.wait_ge(part2.sem, part2.value(dve, b, i + 1))
                        dve.tensor_tensor(dst[:, c, 2, :], RES[:, i, :], dst[:, c, 1, :], ALU.subtract).then_inc(part3.sem, 1)
                    for c in range(2):
                        dve.wait_ge(qk.sem, qk.value(dve, b, 3 + c))
                        dve.tensor_scalar(KK[:, c, :], KF_[:, c, :], qsc[:, c:c + 1], None, ALU.mult).then_inc(kk1.sem, 1)
                        dve.wait_ge(kk1.sem, kk1.value(dve, b, c + 1))
                        dve.scalar_tensor_tensor(KK[:, c, 1:S], KF_[:, c, 0:S - 1], qsc[:, 2 + c:3 + c], KK[:, c, 1:S],
                                                 ALU.mult, ALU.add).then_inc(kk2.sem, 1)
                    for t in range(NT):
                        dve.wait_ge(vp_ps.sem, vp_ps.value(dve, b, t + 1))
                        bank = PS[:, 6 + t % 2, :]
                        dve.tensor_tensor(VV[:, t, :, 0:DH], bank[:, 0:DE].rearrange("p (h d) -> p h d", d=DH),
                                          bvpy[:, 0:DE].rearrange("p (h d) -> p h d", d=DH), ALU.add).then_inc(v_kept.sem, 1)
                        dve.tensor_tensor(PB[:, :], bank[:, DE:], bvpy[:, DE:2 * DE], ALU.add).then_inc(pb.sem, 1)
                        dve.wait_ge(pth.sem, pth.value(dve, b, t + 1))
                        dve.scalar_tensor_tensor(SP[:, t, :], TH[:, :], 1.0, PB[:, :], ALU.add, ALU.mult).then_inc(sp_.sem, 1)
                        dve.wait_ge(sp_.sem, sp_.value(dve, b, t + 1))
                        rests(t)
                    p_p = p_a[:, 0:NT * HEADS].rearrange("p (t h) -> p t h", t=NT)
                    dve.wait_ge(pos_ps.sem, pos_ps.value(dve, b))
                    dve.tensor_copy(KA[:, :, :, 0], p_p).then_inc(ka.sem, 1)
                    dve.wait_ge(ka.sem, ka.value(dve, b, 1))
                    dve.tensor_tensor(PR[:, :, :], p_p, KA[:, :, :, 0], ALU.subtract).then_inc(ka.sem, 1)
                    dve.wait_ge(ka.sem, ka.value(dve, b, 2))
                    dve.tensor_copy(KA[:, :, :, 1], PR[:, :, :]).then_inc(ka.sem, 1)
                    dve.wait_ge(ka.sem, ka.value(dve, b, 3))
                    dve.tensor_tensor(KA[:, :, :, 2], PR[:, :, :], KA[:, :, :, 1], ALU.subtract).then_inc(ka.sem, 2)

                def attend(b):
                    for g in range(NG4):
                        for it in range(NT):
                            n = (it + 1) * P
                            for pair in range(2):
                                dve.wait_ge(s_ps.sem, s_ps.value(dve, b, 8 * g + 2 * it + pair + 1))
                                dve.tensor_reduce(MX[:, 2 * pair:2 * pair + 2, it], p_s[pair][:, :, 0:n], AX.X, ALU.max,
                                                  negate=True).then_inc(mx_.sem, 1)
                        dve.wait_ge(mx_.sem, mx_.value(dve, b, 8 * (g + 1)))
                        dve.tensor_copy(QA[:, :, :, 3], MX[:, :, :]).then_inc(qa.sem, 1)
                        dve.wait_ge(qa.sem, qa.value(dve, b, 5 * g + 1))
                        dve.tensor_tensor(MR[:, :, :], MX[:, :, :], QA[:, :, :, 3], ALU.subtract).then_inc(qa.sem, 1)
                        dve.wait_ge(qa.sem, qa.value(dve, b, 5 * g + 2))
                        dve.tensor_copy(QA[:, :, :, 4], MR[:, :, :]).then_inc(qa.sem, 1)
                        dve.wait_ge(qa.sem, qa.value(dve, b, 5 * g + 3))
                        dve.tensor_tensor(QA[:, :, :, 5], MR[:, :, :], QA[:, :, :, 4], ALU.subtract).then_inc(qa.sem, 2)
                        dve.wait_ge(oT_ps.sem, oT_ps.value(dve, b, g + 1))
                        o4 = p_m.rearrange("p (t h d) -> p t h d", t=NT, h=4)
                        dve.reciprocal(RS_[:, :, :], o4[:, :, :, DH]).then_inc(rden.sem, 1)
                        dve.wait_ge(rden.sem, rden.value(dve, b, g + 1))
                        dve.tensor_tensor(ON[:, :, 4 * g:4 * g + 4, :], o4[:, :, :, 0:DH],
                                          RS_[:, :, :].unsqueeze(3).to_broadcast([P, NT, 4, DH]), ALU.mult).then_inc(on.sem, 1)
                    dve.wait_ge(on.sem, on.value(dve, b))
                    dve.tensor_tensor(ON[:, :, :, :].rearrange("p t h d -> p (t h d)"), ON[:, :, :, :].rearrange("p t h d -> p (t h d)"),
                                      SP[:, :, :].rearrange("p t n -> p (t n)"), ALU.mult).then_inc(gated.sem, 1)
                    dve.wait_ge(w_ps.sem, w_ps.value(dve, b))
                    dve.tensor_copy(T[:, :, :], p_a.rearrange("p (t d) -> p t d", t=NT)).then_inc(t_kept.sem, 1)
                    dve.wait_ge(t_kept.sem, t_kept.value(dve, b))

                    def norm(i, dst, src, done):
                        s_t, m, _, r_s = sets[i]
                        for t in range(NT):
                            dve.bn_stats(s_t[:, t, :], src[:, t, :]).then_inc(st[i].sem, 1)
                        hold(dve, st[i].sem, st[i].value(dve, b))
                        for t in range(NT):
                            dve.bn_aggr(m[:, t, :], s_t[:, t, :]).then_inc(mv[i].sem, 1)
                        dve.wait_ge(rs[i].sem, rs[i].value(dve, b))
                        for t in range(NT):
                            dve.tensor_scalar(dst[:, t, :], src[:, t, :], m[:, t, 0:1], r_s[:, t:t + 1],
                                              ALU.subtract, ALU.mult).then_inc(done.sem, 1)
                        dve.wait_ge(done.sem, done.value(dve, b))
                    norm(0, N1, T, n1)
                    dve.tensor_tensor(N1[:, :, :], N1[:, :, :], olw[:, :].unsqueeze(1).to_broadcast([P, NT, D]), ALU.mult).then_inc(n1w.sem, 1)
                    dve.wait_ge(n1w.sem, n1w.value(dve, b, 1))
                    dve.tensor_tensor(N1[:, :, :], N1[:, :, :], olb[:, :].unsqueeze(1).to_broadcast([P, NT, D]), ALU.add).then_inc(n1w.sem, 1)
                    dve.wait_ge(n1w.sem, n1w.value(dve, b))
                    norm(1, N2, N1, n2)
                    dve.tensor_tensor(tiles(b), tiles(b), N2[:, :, :], ALU.add).then_inc(x3.sem, 1)
                over_batches(dve, project, attend)

        ctx = ExitStack()
        with ctx:
            XF = sb(ctx, "XF_e", [P, NT, D])
            XT = sb(ctx, "XT_e", [P, S])
            TG = sb(ctx, "TG", [P, NH, S])
            SGU = sb(ctx, "SGU", [P, NH, S])
            HU = sb(ctx, "HU", [P, NH, S])
            T = sb(ctx, "T_e", [P, NT, D])
            N1 = sb(ctx, "N1_e", [P, NT, D])
            sets = []
            for i in range(2):
                sets.append((sb(ctx, f"ste{i}", [P, NT, 6]), sb(ctx, f"mve{i}", [P, NT, 2]),
                             sb(ctx, f"rt_e{i}", [P, NT]), sb(ctx, f"rs_e{i}", [P, NT])))
            warm = sb(ctx, "warm5", [P, 1])
            warmed = signal("swiglu_warm")
            st = [signal(f"e_stats{i}", NT) for i in range(2)]
            mv = [signal(f"e_moments{i}", NT) for i in range(2)]
            rs = [signal(f"e_scale{i}", 2) for i in range(2)]
            xg = signal("xg_ready", NT)
            xgT_ps = signal("xgT_ps")
            xgT = signal("xgT_ready")
            gu_ps = signal("gate_up_ps", 2 * NH)
            tg = signal("swiglu_tanh_ready", NH)
            sgr = signal("swiglu_gate_ready", NH)
            hu = signal("hidden_ready", NH)
            dn = signal("down_ps")
            tk = signal("down_kept")
            n1 = signal("e_n1_ready", NT)
            x4 = signal("x4_ready")
            stored = signal("stored", 16)
            block = ctx.enter_context(nc.Block())

            @block.sync
            def _(sp):
                for b in range(B):
                    sp.wait_ge(x4.sem, b + 1)
                    sp.dma_start(out_d[b].rearrange("(t p) d -> p t d", p=P), X[:, b * NT:(b + 1) * NT, :]).then_inc(stored.sem, 16)
                sp.wait_ge(stored.sem, 16 * B)

            @block.gpsimd
            def _(pool):
                with pool.Fori(0, B) as b:
                    for i in range(2):
                        _, m, r_t, r_s = sets[i]
                        pool.wait_ge(mv[i].sem, mv[i].value(pool, b))
                        layer_norm_scale(pool, m, r_t, r_s, rs[i], b, 0)

            @block.tensor
            def _(pe):
                with pe.Fori(0, B) as b:
                    pe.wait_ge(xg.sem, xg.value(pe, b))
                    for t in range(NT):
                        last = pe.transpose(PS[:, 0, t * P:(t + 1) * P], XF[:, t, :], ident[:, :])
                    last.then_inc(xgT_ps.sem, 1)
                    pe.wait_ge(xgT.sem, xgT.value(pe, b))
                    for c in range(NH):
                        for o in range(2):
                            pe.matmul(PS[:, 1 + NH * o + c, :], wguT[:, o * HID + c * P:o * HID + (c + 1) * P], XT[:, :],
                                      start=True, stop=True).then_inc(gu_ps.sem, 1)
                    p_dn = PS[:, 7, :].rearrange("p (t d) -> p t d", t=NT)
                    for t in range(NT):
                        for c in range(NH):
                            if t == 0:
                                pe.wait_ge(hu.sem, hu.value(pe, b, c + 1))
                            last = pe.matmul(p_dn[:, t, :], HU[:, c, t * P:(t + 1) * P], wdT[:, c, :],
                                             start=(c == 0), stop=(c == NH - 1))
                    last.then_inc(dn.sem, 1)

            @block.scalar
            def _(act):
                act.activation(warm[:, :], half[:, 0:1], ACT.Tanh).then_inc(warmed.sem, 1)
                with act.Fori(0, B) as b:
                    act.wait_ge(xgT_ps.sem, xgT_ps.value(act, b))
                    act.activation(XT[:, :], PS[:, 0, :], ACT.Copy).then_inc(xgT.sem, 1)
                    for c in range(NH):
                        act.wait_ge(gu_ps.sem, gu_ps.value(act, b, 2 * c + 1))
                        act.activation(TG[:, c, :], PS[:, 1 + c, :], ACT.Tanh, scale=0.5).then_inc(tg.sem, 1)

            @block.vector
            def _(dve):
                def moments(i, src, b):
                    s_t, m, _, _ = sets[i]
                    for t in range(NT):
                        dve.bn_stats(s_t[:, t, :], src(t)).then_inc(st[i].sem, 1)
                    hold(dve, st[i].sem, st[i].value(dve, b))
                    for t in range(NT):
                        dve.bn_aggr(m[:, t, :], s_t[:, t, :]).then_inc(mv[i].sem, 1)

                def normal(i, dst, src, b, done):
                    _, m, _, r_s = sets[i]
                    dve.wait_ge(rs[i].sem, rs[i].value(dve, b))
                    for t in range(NT):
                        dve.tensor_scalar(dst[:, t, :], src(t), m[:, t, 0:1], r_s[:, t:t + 1],
                                          ALU.subtract, ALU.mult).then_inc(done.sem, 1)
                with dve.Fori(0, B) as b:
                    tiles = lambda: X[:, bass.ds(dve.snap(b * NT), NT), :]
                    tile = lambda t: X[:, bass.ds(dve.snap(b * NT + t), 1), :].rearrange("p o d -> p (o d)")
                    moments(0, tile, b)
                    normal(0, XF, tile, b, xg)
                    for c in range(NH):
                        dve.wait_ge(tg.sem, tg.value(dve, b, c + 1))
                        dve.scalar_tensor_tensor(SGU[:, c, :], TG[:, c, :], 1.0, PS[:, 1 + c, :], ALU.add, ALU.mult).then_inc(sgr.sem, 1)
                        dve.wait_ge(gu_ps.sem, gu_ps.value(dve, b, 2 * c + 2))
                        dve.wait_ge(sgr.sem, sgr.value(dve, b, c + 1))
                        dve.tensor_tensor(HU[:, c, :], SGU[:, c, :], PS[:, 1 + NH + c, :], ALU.mult).then_inc(hu.sem, 1)
                    dve.wait_ge(dn.sem, dn.value(dve, b))
                    dve.tensor_copy(T[:, :, :], PS[:, 7, :].rearrange("p (t d) -> p t d", t=NT)).then_inc(tk.sem, 1)
                    dve.wait_ge(tk.sem, tk.value(dve, b))
                    moments(1, lambda t: T[:, t, :], b)
                    normal(1, N1, lambda t: T[:, t, :], b, n1)
                    dve.wait_ge(n1.sem, n1.value(dve, b))
                    dve.tensor_tensor(tiles(), tiles(), N1[:, :, :], ALU.add).then_inc(x4.sem, 1)


_INS = ["L0_attn_x", "L0_attn_gamma", "L0_attn_beta", "L0_attn_w_ih", "L0_attn_w_hh", "L0_attn_b_ih", "L0_attn_b_hh",
        "L0_attn_w_out", "L0_attn_b_out", "L0_ffn_gate_W", "L0_ffn_gate_b", "L0_ffn_wi_W", "L0_ffn_wi_b", "L0_ffn_wo_W",
        "L0_ffn_wo_b", "L0_ffn_lora_A", "L0_ffn_lora_B", "L1_attn_W_in", "L1_attn_b_in", "L1_attn_in_ln_w",
        "L1_attn_in_ln_b", "L1_attn_W_out", "L1_attn_out_ln_w", "L1_attn_out_ln_b", "L1_attn_smear_factor",
        "L1_attn_log_scale", "L1_ffn_w_gate", "L1_ffn_w_up", "L1_ffn_w_down"]


def kernel(**inputs):
    import numpy as _np
    import concourse.bacc as _bacc
    from concourse import mybir as _mybir
    from concourse.bass_utils import run_bass_kernel_spmd as _run

    nc = _bacc.Bacc("TRN2", target_bir_lowering=False, num_devices=1)
    arrays, args = {}, []
    for name in _INS:
        a = _np.ascontiguousarray(inputs[name])
        arrays[f"in_{name}_dram"] = a
        args.append(nc.dram_tensor(f"in_{name}_dram", a.shape, _mybir.dt.from_np(a.dtype), kind="ExternalInput").ap())
    args.append(nc.dram_tensor("out_0_dram", (B, S, D), F32, kind="ExternalOutput").ap())
    build(nc, *args)
    r = _run(nc, [arrays], core_ids=[0])
    return r.results[0]["out_0_dram"]
```

```python
from contextlib import ExitStack

import concourse.bass as bass
from concourse import mybir

F32 = mybir.dt.float32
BF16 = mybir.dt.bfloat16
FP16 = mybir.dt.float16
I32 = mybir.dt.int32
U32 = mybir.dt.uint32
ALU = mybir.AluOpType
ACT = mybir.ActivationFunctionType
AX = mybir.AxisListType

P = 128
B, S, D = 8, 512, 128
NT = S // P
H = 256
HC = H // P
F, E, R = 512, 8, 4
FC = F // P
HEADS, DH = 16, 16
DE = HEADS * DH
HID = 384
NH = HID // P
EPS = 1e-5
NEG_BIG = -1e10
U = 4
NSTEP = HC * B


class Signal:

    def __init__(self, sem, per=1, credit=0):
        self.sem, self.per, self.credit = sem, per, credit

    def value(self, eng, b, k=None):
        v = b * self.per + (self.credit + (self.per if k is None else k))
        return v if isinstance(v, int) else eng.snap(v)

    def before(self, eng, b):
        return self.value(eng, b, 0)


def build(nc, x_d, gamma_d, beta_d, w_ih_d, w_hh_d, b_ih_d, b_hh_d, w_out_d, b_out_d,
          gate_w_d, gate_b_d, wi_d, wi_b_d, wo_d, wo_b_d, lora_a_d, lora_b_d,
          w_in_d, b_in_d, in_ln_w_d, in_ln_b_d, w_aout_d, out_ln_w_d, out_ln_b_d, smear_d, log_scale_d,
          w_gate_d, w_up_d, w_down_d, out_d):
    top = ExitStack()
    with top:
        def sb(ctx, name, shape, dt=F32):
            return ctx.enter_context(nc.sbuf_tensor(name, shape, dt))

        X = sb(top, "X", [P, B * NT, D])
        MV = sb(top, "MV", [P, B * NT, 2])
        R1 = sb(top, "R1", [P, B * NT])
        RR = sb(top, "RR", [P, B * NT])
        half = sb(top, "half", [P, B * NT])
        eps = sb(top, "eps", [P, NT])
        ident = sb(top, "ident", [P, P])
        identb = sb(top, "identb", [P, P], BF16)
        wihT = sb(top, "wihT", [P, 3 * H])
        woutT = sb(top, "woutT", [P, HC, D])
        wiT = sb(top, "wiT", [P, F])
        woT = sb(top, "woT", [P, FC, D])
        gaT = sb(top, "gaT", [P, E + E * R])
        lbT = sb(top, "lbT", [E * R, F])
        winT = sb(top, "winT", [P, 4 * DE + HEADS])
        waoT = sb(top, "waoT", [P, DE // P, D])
        wguT = sb(top, "wguT", [P, 2 * HID])
        wdT = sb(top, "wdT", [P, NH, D])
        gam = sb(top, "gam", [P, 1])
        bet = sb(top, "bet", [P, 1])
        bih = sb(top, "bih", [P, 6])
        bhh = sb(top, "bhh", [P, 6])
        wib = sb(top, "wib", [P, FC])
        bqk = sb(top, "bqk", [P, 4])
        ilw = sb(top, "ilw", [P, 1])
        ilb = sb(top, "ilb", [P, 1])
        bout = sb(top, "bout", [P, D])
        gateb = sb(top, "gateb", [P, E])
        wob = sb(top, "wob", [P, D])
        bvpy = sb(top, "bvpy", [P, 2 * DE + HEADS])
        olw = sb(top, "olw", [P, D])
        olb = sb(top, "olb", [P, D])
        iota_e = sb(top, "iota_e", [P, E, R])
        hs8 = sb(top, "hs8", [8, 6])
        qsc = sb(top, "qsc", [P, 6])
        kscale = sb(top, "kscale", [P, 4])
        S_gru = kscale[:, 2:3]
        bX = sb(top, "bX", [P, 6])
        PS = top.enter_context(nc.psum_tensor("PS", [P, 8, 512], F32))

        def signal(name, per=1, credit=0):
            return Signal(top.enter_context(nc.semaphore(name)), per, credit)

        passed = signal("passed").sem

        def hold(eng, sem, value):
            eng.wait_ge(sem, value)
            eng.sem_inc(passed, 1)

        def x_moments(dve, s_t, m, st, mv, kept):
            with dve.Fori(0, B) as b:
                for t in range(NT):
                    dve.bn_stats(s_t[:, t, :], X[:, bass.ds(dve.snap(b * NT + t), 1), :].rearrange("p o d -> p (o d)")).then_inc(st.sem, 1)
                hold(dve, st.sem, st.value(dve, b))
                for t in range(NT):
                    dve.bn_aggr(m[:, t, :], s_t[:, t, :]).then_inc(mv.sem, 1)
                dve.wait_ge(mv.sem, mv.value(dve, b))
                dve.tensor_scalar(MV[:, bass.ds(dve.snap(b * NT), NT), :], m[:, :, :], 1.0, None, ALU.mult).then_inc(kept.sem, 1)

        gru_scope = ExitStack()
        top.enter_context(gru_scope)
        W1 = sb(gru_scope, "W1", [P, HC, 3 * H], FP16)
        W2 = sb(gru_scope, "W2", [P, HC, 3 * H], FP16)
        HS = sb(gru_scope, "HS", [P, S, HC, B])
        xi_scope = ExitStack()
        gru_scope.enter_context(xi_scope)
        XI = sb(xi_scope, "XI", [P, S + 2 * U, 6, B])

        ctx = ExitStack()
        with ctx:
            staging = HS[:, :, :, :].rearrange("p s c b -> p (s c b)")
            taken = [0]

            def stage(shape, dt=F32):
                n = 1
                for k in shape:
                    n *= k
                at = staging[:, taken[0]:taken[0] + n]
                taken[0] += n
                at = at if dt == F32 else at.bitcast(dt)
                return at if len(shape) == 1 else at.rearrange("p (c k) -> p c k", c=shape[0])
            s_ih = stage((6, D))
            s_hh = stage((6, H))
            s_out = stage((H,))
            s_wi = stage((FC, D))
            s_wo = stage((F,))
            s_lb = stage((FC, E * R))
            s_in = stage((8, D))
            s_ao = stage((DE,))
            s_gi = stage((2 * NH, D), I32)
            s_di = stage((HID,), I32)
            s_g = stage((2 * NH, D))
            s_d = stage((HID,))
            s_ga = sb(ctx, "s_ga", [E + E * R, D])
            s_iny = sb(ctx, "s_iny", [HEADS, D])
            whhT = sb(ctx, "whhT", [P, HC, 3 * H])
            mx = sb(ctx, "mx", [P, 1])
            mrow = sb(ctx, "mrow", [1, 1])
            onesr = sb(ctx, "onesr", [1, P])
            sel8 = sb(ctx, "sel8", [8, P])
            STb = sb(ctx, "STb", [P, NT, 6])
            MVb = sb(ctx, "MVb", [P, NT, 2])
            rt = sb(ctx, "rt", [P, B * NT])
            YN = sb(ctx, "YN", [P, NT, D])
            YT = sb(ctx, "YT", [P, S])
            warm = sb(ctx, "warm", [P, 1])

            loads_x = signal("loads_x")
            loads_gru = signal("loads_gru")
            loads_rest = signal("loads_rest")
            consts = signal("consts")
            turned = signal("weights_turned")
            kept = signal("weights_kept")
            casts = signal("int_weights_cast")
            sc_v = signal("scale_step_v")
            sc_p = signal("scale_step_p")
            sc_a = signal("head_scalar_exps")
            hv = signal("head_scalars_ready")
            bx = signal("input_bias_ready")
            pool_step = signal("x_rstd_steps").sem
            stats = signal("x_stats", NT)
            aggr = signal("x_aggr", NT)
            mv_kept = signal("x_moments_kept")
            rstd = signal("x_rstd")
            y_ready = signal("y_ready", NT)
            yT_ps = signal("yT_ps", 1, 1)
            yT_ready = signal("yT_ready", 1, 1)
            xi_ps = signal("xi_ps", 6, 6)
            xi_v = signal("xi_by_vector", 3, 3)
            xi_a = signal("xi_by_scalar", 3, 3)

            gru_jobs = [(s_hh[:, c, kc * P:(kc + 1) * P], whhT[:, kc, c * P:(c + 1) * P], 0.25 if c >= 4 else 0.5)
                        for c in range(6) for kc in range(HC)]
            gru_jobs += [(s_ih[:, c, :], wihT[:, c * P:(c + 1) * P], 1.0) for c in range(6)]
            jobs = [(s_out[:, c * P:(c + 1) * P], woutT[:, c, :], 0.5) for c in range(HC)]
            jobs += [(s_wi[:, c, :], wiT[:, c * P:(c + 1) * P], 1.0) for c in range(FC)]
            jobs += [(s_wo[:, c * P:(c + 1) * P], woT[:, c, :], 1.0) for c in range(FC)]
            jobs += [(s_ga[:, :], gaT[:, :], 1.0)]
            jobs += [(s_lb[:, c, :], lbT[:, c * P:(c + 1) * P], 1.0) for c in range(FC)]
            jobs += [(s_in[:, c, :], winT[:, c * P:(c + 1) * P], 1.0) for c in range(8)]
            jobs += [(s_iny[:, :], winT[:, 4 * DE:4 * DE + HEADS], 1.0)]
            jobs += [(s_ao[:, c * P:(c + 1) * P], waoT[:, c, :], 0.5) for c in range(DE // P)]
            jobs += [(s_g[:, c, :], wguT[:, c * P:(c + 1) * P], 1.0) for c in range(2 * NH)]
            jobs += [(s_d[:, c * P:(c + 1) * P], wdT[:, c, :], 0.5) for c in range(NH)]
            NG = len(gru_jobs)
            alljobs = gru_jobs + jobs
            NJ = len(alljobs)

            block = ctx.enter_context(nc.Block())

            @block.sync
            def _(sp):
                sp.dma_start(s_hh, w_hh_d.rearrange("(c p) k -> p c k", p=P)).then_inc(loads_gru.sem, 16)
                sp.dma_start(s_ih, w_ih_d.rearrange("(c p) k -> p c k", p=P)).then_inc(loads_gru.sem, 16)
                for b in range(B):
                    sp.dma_start(X[:, b * NT:(b + 1) * NT, :],
                                 x_d[b].rearrange("(t p) d -> p t d", p=P)).then_inc(loads_x.sem, 16)
                sp.dma_start(s_out[:, :], w_out_d).then_inc(loads_rest.sem, 16)
                sp.dma_start(s_wi[:, :, :], wi_d.rearrange("(c p) k -> p c k", p=P)).then_inc(loads_rest.sem, 16)
                sp.dma_start(s_wo[:, :], wo_d).then_inc(loads_rest.sem, 16)
                sp.dma_start(s_ga[0:E, :], gate_w_d).then_inc(loads_rest.sem, 16)
                sp.dma_start(s_ga[E:E + E * R, :], lora_a_d.rearrange("e r d -> (e r) d")).then_inc(loads_rest.sem, 16)
                for c in range(FC):
                    sp.dma_start(s_lb[:, c, :].rearrange("p (e r) -> p e r", e=E),
                                 lora_b_d[:, c * P:(c + 1) * P, :].rearrange("e p r -> p e r")).then_inc(loads_rest.sem, 16)
                sp.dma_start(s_in[:, :, :], w_in_d[0:4 * DE, :].rearrange("(c p) k -> p c k", p=P)).then_inc(loads_rest.sem, 16)
                sp.dma_start(s_iny[:, :], w_in_d[4 * DE:, :]).then_inc(loads_rest.sem, 16)
                sp.dma_start(s_ao[:, :], w_aout_d).then_inc(loads_rest.sem, 16)
                sp.dma_start(s_gi[:, 0:NH, :], w_gate_d.rearrange("(c p) k -> p c k", p=P)).then_inc(loads_rest.sem, 16)
                sp.dma_start(s_gi[:, NH:, :], w_up_d.rearrange("(c p) k -> p c k", p=P)).then_inc(loads_rest.sem, 16)
                sp.dma_start(s_di[:, :], w_down_d).then_inc(loads_rest.sem, 16)

            N_REST = 11 + FC + 16

            @block.gpsimd
            def _(pool):
                pool.memset(ident[:, :], 0.0).then_inc(consts.sem, 1)
                pool.memset(half[:, :], -0.5).then_inc(consts.sem, 1)
                pool.memset(eps[:, :], EPS).then_inc(consts.sem, 1)
                pool.memset(sel8[:, :], 1.0).then_inc(consts.sem, 1)
                pool.memset(onesr[:, :], 1.0).then_inc(consts.sem, 1)
                pool.iota(iota_e[:, :, :], [[1, E], [0, R]], base=0, channel_multiplier=0,
                          allow_small_or_imprecise_dtypes=True).then_inc(consts.sem, 1)
                pool.memset(XI[:, S:, :, :], 0.0).then_inc(consts.sem, 1)
                pool.wait_ge(consts.sem, 7)
                pool.affine_select(out=ident[:, :], in_=ident[:, :], compare_op=ALU.not_equal, fill=1.0, base=0,
                                   pattern=[[-1, P]], channel_multiplier=1).then_inc(consts.sem, 1)
                pool.affine_select(out=sel8[:, :], in_=sel8[:, :], compare_op=ALU.is_ge, fill=0.0, base=0,
                                   pattern=[[1, P]], channel_multiplier=-DH).then_inc(consts.sem, 1)
                pool.wait_ge(consts.sem, 9)
                pool.tensor_copy(identb[:, :], ident[:, :]).then_inc(consts.sem, 1)
                pool.affine_select(out=sel8[:, :], in_=sel8[:, :], compare_op=ALU.is_ge, fill=0.0, base=DH - 1,
                                   pattern=[[-1, P]], channel_multiplier=DH).then_inc(consts.sem, 1)
                pool.wait_ge(loads_rest.sem, 16 * N_REST)
                pool.tensor_scalar(s_g[:, :, :], s_gi[:, :, :], 1.0 / 127.0, None, ALU.mult).then_inc(casts.sem, 1)
                pool.tensor_scalar(s_d[:, :], s_di[:, :], 1.0 / 127.0, None, ALU.mult).then_inc(casts.sem, 1)
                pool.wait_ge(mv_kept.sem, B)
                pool.tensor_scalar(rt[:, :], MV[:, :, 1], EPS, None, ALU.add).then_inc(pool_step, 1)
                pool.wait_ge(pool_step, 1)
                pool.tensor_tensor(R1[:, :], rt[:, :], half[:, :], ALU.pow).then_inc(pool_step, 1)
                pool.wait_ge(pool_step, 2)
                pool.tensor_tensor(rt[:, :], R1[:, :], R1[:, :], ALU.mult).then_inc(pool_step, 1)
                pool.wait_ge(pool_step, 3)
                pool.tensor_tensor(rt[:, :], rt[:, :], MV[:, :, 1], ALU.mult).then_inc(pool_step, 1)
                pool.wait_ge(pool_step, 4)
                pool.tensor_scalar(rt[:, :], rt[:, :], EPS, None, ALU.add).then_inc(pool_step, 1)
                pool.wait_ge(pool_step, 5)
                pool.tensor_tensor(rt[:, :], rt[:, :], half[:, :], ALU.pow).then_inc(pool_step, 1)
                pool.wait_ge(pool_step, 6)
                pool.tensor_tensor(RR[:, :], rt[:, :], R1[:, :], ALU.mult).then_inc(rstd.sem, 1)

            @block.tensor
            def _(pe):
                def turn(i):
                    src, dst, _ = alljobs[i]
                    k, m = src.shape[0], src.shape[1]
                    if i >= 8:
                        pe.wait_ge(kept.sem, i - 7)
                    pe.transpose(PS[0:m, i % 8, 0:k], src, ident[0:k, 0:k]).then_inc(turned.sem, 1)
                pe.wait_ge(consts.sem, 11)
                pe.wait_ge(loads_gru.sem, 32)
                for i in range(NG):
                    turn(i)
                pe.wait_ge(loads_rest.sem, 16 * N_REST)
                pe.wait_ge(casts.sem, 2)
                for i in range(NG, NJ):
                    turn(i)
                pe.wait_ge(kept.sem, NJ)
                pe.wait_ge(sc_v.sem, 1)
                pe.transpose(PS[0:1, 0, 0:P], mx[:, :], ident[:, :]).then_inc(sc_p.sem, 1)
                pe.wait_ge(sc_v.sem, 4)
                pe.matmul(PS[:, 1, 0:1], onesr[:, :], mrow[:, :], start=True, stop=True).then_inc(sc_p.sem, 1)
                pe.wait_ge(hv.sem, 3)
                pe.matmul(PS[:, 2, 0:6], sel8[:, :], hs8[:, :], start=True, stop=True).then_inc(sc_p.sem, 1)
                pe.wait_ge(sc_v.sem, 12)
                for s in (yT_ps, xi_ps):
                    pe.sem_inc(s.sem, s.credit)
                with pe.Fori(0, B) as b:
                    pe.wait_ge(y_ready.sem, y_ready.value(pe, b))
                    pe.wait_ge(yT_ready.sem, yT_ready.before(pe, b))
                    for t in range(NT):
                        last = pe.transpose(PS[:, 0, t * P:(t + 1) * P], YN[:, t, :], ident[:, :])
                    last.then_inc(yT_ps.sem, 1)
                    pe.wait_ge(yT_ready.sem, yT_ready.value(pe, b))
                    for c in range(6):
                        s, k = (xi_v, c // 2) if c % 2 else (xi_a, c // 2)
                        pe.wait_ge(s.sem, pe.snap(b * 3 + (k + 1)))
                        pe.matmul(PS[:, 1 + c, :], wihT[:, c * P:(c + 1) * P], YT[:, :],
                                  start=True, stop=True).then_inc(xi_ps.sem, 1)

            @block.scalar
            def _(act):
                def col(dst, src, c):
                    act.dma_start(dst, src.rearrange("(c p) -> p c", c=c),
                                   allow_slow_non_contiguous=True).then_inc(loads_rest.sem, 16)

                def row(dst, src):
                    act.dma_start(dst, src.partition_broadcast(P)).then_inc(loads_rest.sem, 16)
                col(gam[:, :], gamma_d, 1)
                col(bet[:, :], beta_d, 1)
                col(bih[:, :], b_ih_d, 6)
                col(bhh[:, :], b_hh_d, 6)
                col(wib[:, :], wi_b_d, FC)
                col(bqk[:, :], b_in_d[0:2 * DE], 4)
                col(ilw[:, :], in_ln_w_d, 1)
                col(ilb[:, :], in_ln_b_d, 1)
                row(bout[:, :], b_out_d)
                row(gateb[:, :], gate_b_d)
                row(wob[:, :], wo_b_d)
                row(bvpy[:, :], b_in_d[2 * DE:])
                row(olw[:, :], out_ln_w_d)
                row(olb[:, :], out_ln_b_d)
                act.dma_start(hs8[:, 0:2], smear_d.rearrange("(c h) -> h c", c=2),
                               allow_slow_non_contiguous=True).then_inc(loads_rest.sem, 16)
                act.dma_start(hs8[:, 2:4], log_scale_d.rearrange("(c h) -> h c", c=2),
                               allow_slow_non_contiguous=True).then_inc(loads_rest.sem, 16)
                act.wait_ge(consts.sem, 11)
                act.activation(warm[:, :], half[:, 0:1], ACT.Tanh).then_inc(sc_a.sem, 1)
                act.wait_ge(loads_rest.sem, 16 * N_REST)
                act.activation(hs8[:, 4:6], hs8[:, 2:4], ACT.Exp, scale=-2.0).then_inc(sc_a.sem, 1)
                act.wait_ge(sc_a.sem, 2)
                act.activation(hs8[:, 2:4], hs8[:, 0:2], ACT.Exp, scale=-1.0).then_inc(sc_a.sem, 1)
                act.wait_ge(sc_a.sem, 3)
                act.activation(hs8[:, 0:2], hs8[:, 0:2], ACT.Exp).then_inc(sc_a.sem, 1)
                for s in (yT_ready, xi_a):
                    act.sem_inc(s.sem, s.credit)
                act.wait_ge(bx.sem, 1)
                with act.Fori(0, B) as b:
                    act.wait_ge(yT_ps.sem, yT_ps.value(act, b))
                    act.wait_ge(xi_ps.sem, xi_ps.before(act, b))
                    act.activation(YT[:, :], PS[:, 0, :], ACT.Identity, scale=gam[:, 0:1],
                                   bias=bet[:, 0:1]).then_inc(yT_ready.sem, 1)
                    for c in (0, 2, 4):
                        act.wait_ge(xi_ps.sem, xi_ps.value(act, b, c + 1))
                        act.activation(XI[:, 0:S, c, bass.ds(b, 1)].rearrange("p s o -> p (s o)"), PS[:, 1 + c, :], ACT.Identity,
                                       scale=S_gru, bias=bX[:, c:c + 1]).then_inc(xi_a.sem, 1)

            @block.vector
            def _(dve):
                dve.wait_ge(loads_x.sem, 16 * B)

                def keep(i):
                    src, dst, f = alljobs[i]
                    dve.wait_ge(turned.sem, i + 1)
                    dve.tensor_scalar(dst, PS[0:src.shape[1], i % 8, 0:src.shape[0]], f, None,
                                      ALU.mult).then_inc(kept.sem, 1)
                x_moments(dve, STb, MVb, stats, aggr, mv_kept)
                for i in range(NJ):
                    keep(i)
                dve.wait_ge(kept.sem, NJ)
                dve.tensor_reduce(mx[:, :], whhT[:, :, :].rearrange("p a b -> p (a b)"), AX.X, ALU.max,
                                  apply_absolute_value=True).then_inc(sc_v.sem, 1)
                dve.wait_ge(sc_p.sem, 1)
                dve.tensor_reduce(mrow[:, :], PS[0:1, 0, 0:P], AX.X, ALU.max).then_inc(sc_v.sem, 1)
                dve.wait_ge(sc_v.sem, 2)
                dve.tensor_scalar(mrow[:, :], mrow[:, :], 2.0 ** -60, None, ALU.max).then_inc(sc_v.sem, 1)
                dve.wait_ge(sc_v.sem, 3)
                dve.tensor_scalar(mrow[:, :].bitcast(I32), mrow[:, :].bitcast(I32), 0x7f800000, None,
                                  ALU.bitwise_and).then_inc(sc_v.sem, 1)
                dve.wait_ge(sc_p.sem, 2)
                dve.tensor_scalar(kscale[:, 0:1], PS[:, 1, 0:1], 2.0 ** -15, None, ALU.mult).then_inc(sc_v.sem, 1)
                dve.tensor_scalar(kscale[:, 1:2], PS[:, 1, 0:1], 2.0 ** -14, None, ALU.mult).then_inc(sc_v.sem, 1)
                dve.wait_ge(sc_v.sem, 6)
                dve.reciprocal(kscale[:, 2:3], kscale[:, 1:2]).then_inc(sc_v.sem, 1)
                dve.wait_ge(sc_a.sem, 4)
                dve.tensor_scalar(hs8[:, 0:4], hs8[:, 0:4], 1.0, None, ALU.add).then_inc(hv.sem, 1)
                dve.tensor_scalar(hs8[:, 4:6], hs8[:, 4:6], float(DH) ** -0.5, None, ALU.mult).then_inc(hv.sem, 1)
                dve.wait_ge(hv.sem, 2)
                dve.reciprocal(hs8[:, 0:4], hs8[:, 0:4]).then_inc(hv.sem, 1)
                dve.wait_ge(sc_p.sem, 3)
                dve.tensor_copy(qsc[:, :], PS[:, 2, 0:6]).then_inc(sc_v.sem, 1)
                dve.wait_ge(sc_v.sem, 8)
                flat = lambda w: w[:, :, :].rearrange("p a b -> p (a b)")
                dve.tensor_scalar(flat(whhT), flat(whhT), S_gru, None, ALU.mult).then_inc(sc_v.sem, 1)
                dve.wait_ge(sc_v.sem, 9)
                dve.tensor_copy(flat(W1), flat(whhT)).then_inc(sc_v.sem, 1)
                dve.wait_ge(sc_v.sem, 10)
                dve.tensor_tensor(flat(W2), flat(whhT), flat(W1), ALU.subtract).then_inc(sc_v.sem, 1)
                dve.tensor_tensor(bih[:, 0:4], bih[:, 0:4], bhh[:, 0:4], ALU.add).then_inc(sc_v.sem, 1)
                dve.wait_ge(sc_v.sem, 12)
                dve.tensor_scalar(bX[:, :], bih[:, :], S_gru, None, ALU.mult).then_inc(bx.sem, 1)
                dve.wait_ge(rstd.sem, 1)
                dve.wait_ge(bx.sem, 1)
                dve.sem_inc(xi_v.sem, xi_v.credit)
                with dve.Fori(0, B) as b:
                    dve.wait_ge(yT_ps.sem, yT_ps.before(dve, b))
                    for t in range(NT):
                        i = dve.snap(b * NT + t)
                        dve.tensor_scalar(YN[:, t, :], X[:, bass.ds(i, 1), :].rearrange("p o d -> p (o d)"),
                                          MV[:, bass.ds(i, 1), 0:1].rearrange("p o k -> p (o k)"), RR[:, bass.ds(i, 1)],
                                          ALU.subtract, ALU.mult).then_inc(y_ready.sem, 1)
                    for c in (1, 3, 5):
                        dve.wait_ge(xi_ps.sem, xi_ps.value(dve, b, c + 1))
                        dve.tensor_scalar(XI[:, 0:S, c, bass.ds(b, 1)].rearrange("p s o -> p (s o)"), PS[:, 1 + c, :], S_gru,
                                          bX[:, c:c + 1], ALU.mult, ALU.add).then_inc(xi_v.sem, 1)

        ctx = ExitStack()
        with ctx:
            bh = sb(ctx, "bh", [P, U, NSTEP])
            XS = sb(ctx, "XS", [P, 2, U, 6, B])
            HR = sb(ctx, "HR", [P, 2, U, NSTEP])
            G1 = sb(ctx, "G1", [P, HC, B], FP16)
            G2 = sb(ctx, "G2", [P, HC, B], FP16)
            tr = sb(ctx, "tr", [P, NSTEP])
            tz = sb(ctx, "tz", [P, NSTEP])
            u_ = sb(ctx, "u_", [P, NSTEP])
            v_ = sb(ctx, "v_", [P, NSTEP])
            n_ = sb(ctx, "n_", [P, NSTEP])
            zg = sb(ctx, "zg", [P, NSTEP])
            zn = sb(ctx, "zn", [P, NSTEP])
            warm = sb(ctx, "warm2", [P, 1])
            free = sb(ctx, "free", [P, 2])
            pR = PS[:, 0:2, :]
            pZ = PS[:, 2:4, :]
            pN = PS[:, 4:6, :]

            xs_in = [signal(f"xs_in{p}") for p in range(2)]
            hr_out = [signal(f"hr_out{p}") for p in range(2)]
            bh_start = signal("bh_start")
            bh_ready = signal("bh_ready")
            injected = signal("injected")
            r_ps = signal("r_ps")
            hn_tr = signal("hn_ps_and_tr")
            z_ps = signal("z_ps")
            tz_ready = signal("tz_ready")
            u_ready = signal("u_ready")
            v_ready = signal("v_ready")
            n_ready = signal("n_ready")
            zg_ready = signal("zg_ready")
            zn_ready = signal("zn_ready")
            g1_ready = signal("g1_ready")
            g_ready = signal("g_ready")
            g2_ready = signal("g2_ready")
            warmed = signal("gru_warm")

            block = ctx.enter_context(nc.Block())

            @block.sync
            def _(sp):
                for p in range(2):
                    sp.dma_start(XS[:, p], XI[:, p * U:(p + 1) * U]).then_inc(xs_in[p].sem, 16)
                with sp.Fori(0, S // (2 * U)) as q:
                    for p in range(2):
                        sp.wait_ge(g_ready.sem, sp.snap(q * (2 * U) + U * (p + 1)))
                        at = sp.snap(q * (2 * U) + U * p)
                        sp.dma_start(HS[:, bass.ds(at, U)].rearrange("p u c b -> p u (c b)"),
                                     HR[:, p]).then_inc(hr_out[p].sem, 16)
                        sp.dma_start(XS[:, p], XI[:, bass.ds(sp.snap(q * (2 * U) + U * (p + 2)), U)]).then_inc(xs_in[p].sem, 16)
                for p in range(2):
                    sp.wait_ge(hr_out[p].sem, 16 * (S // (2 * U) + 1))
                    sp.wait_ge(xs_in[p].sem, 16 * (S // (2 * U) + 1))

            @block.tensor
            def _(pe):
                gates = {"r": (pR, 0), "z": (pZ, 1), "n": (pN, 2)}
                by_g1 = [(mc, kc, W) for mc in range(HC) for kc in range(HC) for W in (W1, W2)]
                by_g2 = [(mc, kc, W1) for mc in range(HC) for kc in range(HC)]

                def product(gate, p, k, mc, kc, W, G):
                    bank, g = gates[gate]
                    w = (HC * g + mc) * P
                    o = NSTEP * k + B * mc
                    return pe.matmul(bank[:, p, o:o + B], W[:, kc, w:w + P], G[:, kc, :],
                                     start=False, stop=True, skip_group_check=True)

                def inject(gate, p):
                    src = {"r": XS[:, p, :, 0:2, :], "z": XS[:, p, :, 2:4, :], "n": bh[:, :, :]}[gate]
                    return pe.matmul(gates[gate][0][:, p, 0:U * NSTEP], ident[:, :], src,
                                     start=True, stop=False, skip_group_check=True)
                pe.wait_ge(bh_ready.sem, 2)
                pe.wait_ge(xs_in[0].sem, 16)
                for gate in "rnz":
                    inject(gate, 0)
                with pe.Fori(0, S // (2 * U)) as q:
                    for p in range(2):
                        for k in range(U):
                            n = pe.snap(q * (2 * U) + (p * U + k + 1))
                            pe.wait_ge(g1_ready.sem, n)
                            for w in by_g1:
                                product("r", p, k, *w, G1)
                            for w in by_g1[:3]:
                                product("n", p, k, *w, G1)
                            pe.wait_ge(g2_ready.sem, n)
                            for w in by_g2:
                                last = product("r", p, k, *w, G2)
                            last.then_inc(r_ps.sem, 1)
                            for w in by_g1[3:]:
                                product("n", p, k, *w, G1)
                            for w in by_g2:
                                last = product("n", p, k, *w, G2)
                            last.then_inc(hn_tr.sem, 1)
                            for w in by_g1:
                                product("z", p, k, *w, G1)
                            for w in by_g2:
                                last = product("z", p, k, *w, G2)
                            last.then_inc(z_ps.sem, 1)
                            if k == 1:
                                pe.wait_ge(xs_in[1 - p].sem, pe.snap(q * 16 + 16 * (p + 1)))
                            if 1 <= k <= 3:
                                inject("rnz"[k - 1], 1 - p).then_inc(injected.sem, 1)

            @block.scalar
            def _(act):
                act.activation(warm[:, :], half[:, 0:1], ACT.Tanh).then_inc(warmed.sem, 1)
                gate_scale = act.alloc_register("gate_scale")
                n_scale = act.alloc_register("n_scale")
                act.load(gate_scale, kscale[0:1, 0:1].bitcast(I32))
                act.load(n_scale, kscale[0:1, 1:2].bitcast(I32))
                with act.Fori(0, S // (2 * U)) as q:
                    for p in range(2):
                        for k in range(U):
                            n = act.snap(q * (2 * U) + (p * U + k + 1))
                            o = NSTEP * k
                            act.wait_ge(r_ps.sem, n)
                            act.activation(tr[:, :], pR[:, p, o:o + NSTEP], ACT.Tanh, scale=gate_scale).then_inc(hn_tr.sem, 1)
                            act.wait_ge(z_ps.sem, n)
                            act.activation(tz[:, :], pZ[:, p, o:o + NSTEP], ACT.Tanh, scale=gate_scale).then_inc(tz_ready.sem, 1)
                            act.wait_ge(v_ready.sem, n)
                            act.activation(n_[:, :], v_[:, :], ACT.Tanh, scale=n_scale).then_inc(n_ready.sem, 1)

            @block.vector
            def _(dve):
                dve.memset(bh[:, :, :], 0.0).then_inc(bh_start.sem, 1)
                dve.memset(HR[:, :, :, :], 0.0).then_inc(bh_start.sem, 1)
                dve.memset(G1[:, :, :], 0.0).then_inc(g1_ready.sem, 1)
                dve.memset(G2[:, :, :], 0.0).then_inc(g2_ready.sem, 1)
                dve.tensor_scalar(bhh[:, 4:6], bhh[:, 4:6], S_gru, 0.5, ALU.mult, ALU.mult).then_inc(bh_start.sem, 1)
                dve.wait_ge(bh_start.sem, 3)
                for c in range(HC):
                    x = bh[:, :, c * B:(c + 1) * B]
                    dve.tensor_scalar(x, x, bhh[:, 4 + c:5 + c], None, ALU.add).then_inc(bh_ready.sem, 1)
                for p in range(2):
                    dve.memset(free[:, p:p + 1], 0.0).then_inc(hr_out[p].sem, 16)
                flat = lambda g: g[:, :, :].rearrange("p c b -> p (c b)")

                def step(q, p, k):
                    n = dve.snap(q * (2 * U) + (p * U + k + 1))
                    n2 = dve.snap(q * (4 * U) + 2 * (p * U + k + 1))
                    o = NSTEP * k
                    before = HR[:, p, k - 1, :] if k else HR[:, 1 - p, U - 1, :]
                    dve.wait_ge(hn_tr.sem, n2)
                    dve.scalar_tensor_tensor(u_[:, :], tr[:, :], 1.0, pN[:, p, o:o + NSTEP],
                                             ALU.add, ALU.mult).then_inc(u_ready.sem, 1)
                    dve.wait_ge(u_ready.sem, n)
                    dve.tensor_tensor(v_[:, :], u_[:, :], XS[:, p, k, 4:6, :].rearrange("p c b -> p (c b)"),
                                      ALU.add).then_inc(v_ready.sem, 1)
                    dve.wait_ge(tz_ready.sem, n)
                    dve.scalar_tensor_tensor(zg[:, :], tz[:, :], 1.0, before, ALU.add, ALU.mult).then_inc(zg_ready.sem, 1)
                    dve.wait_ge(n_ready.sem, n)
                    dve.scalar_tensor_tensor(zn[:, :], tz[:, :], 1.0, n_[:, :], ALU.subtract, ALU.mult).then_inc(zn_ready.sem, 1)
                    dve.wait_ge(zn_ready.sem, n)
                    dve.scalar_tensor_tensor(flat(G1), zg[:, :], 0.5, zn[:, :], ALU.mult, ALU.subtract).then_inc(g1_ready.sem, 1)
                    dve.scalar_tensor_tensor(HR[:, p, k, :], zg[:, :], 0.5, zn[:, :], ALU.mult, ALU.subtract).then_inc(g_ready.sem, 1)
                    dve.wait_ge(g_ready.sem, n)
                    dve.tensor_tensor(flat(G2), HR[:, p, k, :], flat(G1), ALU.subtract).then_inc(g2_ready.sem, 1)
                with dve.Fori(0, S // (2 * U)) as q:
                    for p in range(2):
                        for k in range(U):
                            if k == 0:
                                dve.wait_ge(hr_out[p].sem, dve.snap(q * 16 + 16))
                            step(q, p, k)
        xi_scope.close()

        def layer_norm_scale(eng, mv, rt, rs, step, b, k):
            eng.tensor_tensor(rt[:, :], mv[:, :, 1], eps[:, :], ALU.add).then_inc(step.sem, 1)
            eng.wait_ge(step.sem, step.value(eng, b, k + 1))
            eng.tensor_tensor(rs[:, :], rt[:, :], half[:, 0:NT], ALU.pow).then_inc(step.sem, 1)

        ctx = ExitStack()
        with ctx:
            HB = sb(ctx, "HB", [P, HC, S])
            X0 = sb(ctx, "X0", [P, NT, D])
            X0b = sb(ctx, "X0b", [P, NT, D])
            T = sb(ctx, "T", [P, NT, D])
            N1 = sb(ctx, "N1", [P, NT, D])
            XF = sb(ctx, "XF", [P, NT, D])
            XFT = sb(ctx, "XFT", [P, S])
            LG = sb(ctx, "LG", [P, NT, E])
            LM = sb(ctx, "LM", [P, NT, 8])
            LI = sb(ctx, "LI", [P, NT, 8], U32)
            LF = sb(ctx, "LF", [P, NT])
            LA = sb(ctx, "LA", [P, NT, E * R])
            ML = sb(ctx, "ML", [P, NT, E * R])
            LAT = sb(ctx, "LAT", [E * R, S])
            INT = sb(ctx, "INT", [P, FC, S])
            T2 = sb(ctx, "T2", [P, NT, D])
            N2 = sb(ctx, "N2", [P, NT, D])
            sets = []
            for i in range(3):
                sets.append((sb(ctx, f"st{i}", [P, NT, 6]), sb(ctx, f"mv{i}", [P, NT, 2]),
                             sb(ctx, f"rt{i}", [P, NT]), sb(ctx, f"rs{i}", [P, NT])))
            warm = sb(ctx, "warm3", [P, 1])
            p_gy = PS[:, 0, :].rearrange("p (t d) -> p t d", t=NT)
            p_xfT = PS[:, 1, :]
            p_ga = PS[:, 2, 0:NT * (E + E * R)].rearrange("p (t c) -> p t c", t=NT)
            p_laT = PS[0:E * R, 3, :]
            p_base = PS[:, 4:7, :]
            p_dn = PS[:, 7, :].rearrange("p (t d) -> p t d", t=NT)

            warmed = signal("ffn_warm")
            hb = signal("hb_copied", HC)
            x0 = signal("x0_ready", NT)
            x0b = signal("x0b_ready")
            gy = signal("gru_out_ps", 1, 1)
            t_sum = signal("gru_sum_ready")
            st = [signal(f"c_stats{i}", NT) for i in range(3)]
            mv = [signal(f"c_moments{i}", NT) for i in range(3)]
            rs = [signal(f"c_scale{i}", 2) for i in range(3)]
            nn = signal("n1_ready", NT)
            x1 = signal("x1_ready")
            xf = signal("xf_ready", NT)
            xfT_ps = signal("xfT_ps")
            xfT = signal("xfT_ready")
            ga = signal("gate_lora_ps")
            lg = signal("logits_ready", 2)
            lm = signal("logit_max_ready", NT)
            li = signal("expert_index_ready", NT)
            lf = signal("expert_number_ready")
            ml = signal("masked_lora_ready", NT)
            laT_ps = signal("loraT_ps")
            laT = signal("loraT_ready")
            base = signal("base_ps", FC)
            inter = signal("inter_ready", FC, FC)
            dn = signal("ffn_out_ps")
            t2 = signal("ffn_sum_ready")
            n2 = signal("n2_ready", NT)
            x2 = signal("x2_ready")

            block = ctx.enter_context(nc.Block())

            @block.gpsimd
            def _(pool):
                with pool.Fori(0, B) as b:
                    pool.wait_ge(x0.sem, x0.value(pool, b))
                    for t in range(NT):
                        last = pool.tensor_tensor(X0b[:, t, :], X0[:, t, :], bout[:, :], ALU.add)
                    last.then_inc(x0b.sem, 1)
                    for i in range(3):
                        _, m, r_t, r_s = sets[i]
                        pool.wait_ge(mv[i].sem, mv[i].value(pool, b))
                        layer_norm_scale(pool, m, r_t, r_s, rs[i], b, 0)

            @block.tensor
            def _(pe):
                pe.sem_inc(gy.sem, gy.credit)
                with pe.Fori(0, B) as b:
                    pe.wait_ge(hb.sem, hb.value(pe, b))
                    for t in range(NT):
                        for c in range(HC):
                            last = pe.matmul(p_gy[:, t, :], HB[:, c, t * P:(t + 1) * P], woutT[:, c, :],
                                             start=(c == 0), stop=(c == HC - 1))
                    last.then_inc(gy.sem, 1)
                    pe.wait_ge(xf.sem, xf.value(pe, b))
                    for t in range(NT):
                        last = pe.transpose(p_xfT[:, t * P:(t + 1) * P], XF[:, t, :], ident[:, :])
                    last.then_inc(xfT_ps.sem, 1)
                    pe.wait_ge(xfT.sem, xfT.value(pe, b))
                    for t in range(NT):
                        last = pe.matmul(p_ga[:, t, :], XFT[:, t * P:(t + 1) * P], gaT[:, :], start=True, stop=True)
                    last.then_inc(ga.sem, 1)
                    for c in range(FC):
                        if c in (0, 3):
                            pe.wait_ge(inter.sem, inter.value(pe, b, c // 3))
                        pe.matmul(p_base[:, c % 3, :], wiT[:, c * P:(c + 1) * P], XFT[:, :], start=True, stop=False)
                        if c == 0:
                            pe.wait_ge(ml.sem, ml.value(pe, b))
                            for t in range(NT):
                                last = pe.transpose(p_laT[:, t * P:(t + 1) * P], ML[:, t, :], ident[:, :])
                            last.then_inc(laT_ps.sem, 1)
                            pe.wait_ge(laT.sem, laT.value(pe, b))
                        pe.matmul(p_base[:, c % 3, :], lbT[:, c * P:(c + 1) * P], LAT[:, :],
                                  start=False, stop=True).then_inc(base.sem, 1)
                    for t in range(NT):
                        for c in range(FC):
                            if t == 0:
                                pe.wait_ge(inter.sem, inter.value(pe, b, c + 1))
                            last = pe.matmul(p_dn[:, t, :], INT[:, c, t * P:(t + 1) * P], woT[:, c, :],
                                             start=(c == 0), stop=(c == FC - 1))
                    last.then_inc(dn.sem, 1)

            @block.scalar
            def _(act):
                act.activation(warm[:, :], half[:, 0:1], ACT.Tanh).then_inc(warmed.sem, 1)
                act.sem_inc(inter.sem, inter.credit)
                with act.Fori(0, B) as b:
                    act.wait_ge(gy.sem, gy.before(act, b))
                    for c in range(HC):
                        act.activation(HB[:, c, :], HS[:, :, c, bass.ds(b, 1)].rearrange("p s o -> p (s o)"),
                                       ACT.Copy).then_inc(hb.sem, 1)
                    act.wait_ge(xfT_ps.sem, xfT_ps.value(act, b))
                    act.activation(XFT[:, :], p_xfT, ACT.Copy).then_inc(xfT.sem, 1)
                    act.wait_ge(laT_ps.sem, laT_ps.value(act, b))
                    act.activation(LAT[:, :], p_laT, ACT.Copy).then_inc(laT.sem, 1)
                    for c in range(FC):
                        act.wait_ge(base.sem, base.value(act, b, c + 1))
                        act.activation(INT[:, c, :], p_base[:, c % 3, :], ACT.Relu,
                                       bias=wib[:, c:c + 1]).then_inc(inter.sem, 1)

            @block.vector
            def _(dve):
                def moments(i, src, b):
                    s_t, m, _, _ = sets[i]
                    for t in range(NT):
                        dve.bn_stats(s_t[:, t, :], src(t)).then_inc(st[i].sem, 1)
                    hold(dve, st[i].sem, st[i].value(dve, b))
                    for t in range(NT):
                        dve.bn_aggr(m[:, t, :], s_t[:, t, :]).then_inc(mv[i].sem, 1)

                def normal(i, dst, src, b, done):
                    _, m, _, r_s = sets[i]
                    dve.wait_ge(rs[i].sem, rs[i].value(dve, b))
                    for t in range(NT):
                        dve.tensor_scalar(dst[:, t, :], src(t), m[:, t, 0:1], r_s[:, t:t + 1],
                                          ALU.subtract, ALU.mult).then_inc(done.sem, 1)
                with dve.Fori(0, B) as b:
                    tiles = lambda: X[:, bass.ds(dve.snap(b * NT), NT), :]
                    tile = lambda t: X[:, bass.ds(dve.snap(b * NT + t), 1), :].rearrange("p o d -> p (o d)")
                    for t in range(NT):
                        i = dve.snap(b * NT + t)
                        dve.tensor_scalar(X0[:, t, :], tile(t), MV[:, bass.ds(i, 1), 0:1].rearrange("p o k -> p (o k)"),
                                          R1[:, bass.ds(i, 1)], ALU.subtract, ALU.mult).then_inc(x0.sem, 1)
                    dve.wait_ge(x0b.sem, x0b.value(dve, b))
                    dve.wait_ge(gy.sem, gy.value(dve, b))
                    dve.tensor_tensor(T[:, :, :], X0b[:, :, :], p_gy, ALU.add).then_inc(t_sum.sem, 1)
                    dve.wait_ge(t_sum.sem, t_sum.value(dve, b))
                    moments(0, lambda t: T[:, t, :], b)
                    normal(0, N1, lambda t: T[:, t, :], b, nn)
                    dve.wait_ge(nn.sem, nn.value(dve, b))
                    dve.tensor_tensor(tiles(), tiles(), N1[:, :, :], ALU.add).then_inc(x1.sem, 1)
                    hold(dve, x1.sem, x1.value(dve, b))
                    moments(1, tile, b)
                    normal(1, XF, tile, b, xf)
                    dve.wait_ge(ga.sem, ga.value(dve, b))
                    dve.tensor_tensor(LG[:, :, :], p_ga[:, :, 0:E], gateb[:, :].unsqueeze(1).to_broadcast([P, NT, E]),
                                      ALU.add).then_inc(lg.sem, 1)
                    dve.tensor_copy(LA[:, :, :], p_ga[:, :, E:]).then_inc(lg.sem, 1)
                    hold(dve, lg.sem, lg.value(dve, b))
                    for t in range(NT):
                        dve.max(LM[:, t, :], LG[:, t, :]).then_inc(lm.sem, 1)
                    hold(dve, lm.sem, lm.value(dve, b))
                    for t in range(NT):
                        dve.max_index(LI[:, t, :], LM[:, t, :], LG[:, t, :]).then_inc(li.sem, 1)
                    dve.wait_ge(li.sem, li.value(dve, b))
                    dve.tensor_copy(LF[:, :], LI[:, :, 0]).then_inc(lf.sem, 1)
                    dve.wait_ge(lf.sem, lf.value(dve, b))
                    for t in range(NT):
                        dve.scalar_tensor_tensor(ML[:, t, :], iota_e[:, :, :].rearrange("p e r -> p (e r)"), LF[:, t:t + 1],
                                                 LA[:, t, :], ALU.is_equal, ALU.mult).then_inc(ml.sem, 1)
                    dve.wait_ge(dn.sem, dn.value(dve, b))
                    dve.tensor_tensor(T2[:, :, :], p_dn, wob[:, :].unsqueeze(1).to_broadcast([P, NT, D]),
                                      ALU.add).then_inc(t2.sem, 1)
                    dve.wait_ge(t2.sem, t2.value(dve, b))
                    moments(2, lambda t: T2[:, t, :], b)
                    normal(2, N2, lambda t: T2[:, t, :], b, n2)
                    dve.wait_ge(n2.sem, n2.value(dve, b))
                    dve.tensor_tensor(tiles(), tiles(), N2[:, :, :], ALU.add).then_inc(x2.sem, 1)

        gru_scope.close()

        KM, KF = 99, 102
        NG4 = HEADS // 4
        ctx = ExitStack()
        with ctx:
            qd = nc.dram_tensor("q_parts", (B, 3, DE, S), BF16).ap()
            kd = nc.dram_tensor("k_parts", (B, 3, DE, S), BF16).ap()
            ad = nc.dram_tensor("k_extra", (B, HEADS * 6, S), BF16).ap()
            QS = sb(ctx, "QS", [KF, 2, HEADS, S], BF16)
            KS = sb(ctx, "KS", [KF, 2, HEADS, S], BF16)
            VV = sb(ctx, "VV", [P, 2, NT, HEADS, 32])
            SP = sb(ctx, "SP", [P, 2, NT, DE])
            PT = sb(ctx, "PT", [P, 2, 4, S])
            XN = sb(ctx, "XN", [P, NT, D])
            XT = sb(ctx, "XT", [P, S])
            QF = sb(ctx, "QF", [P, 2, S])
            KF_ = sb(ctx, "KF_", [P, 2, S])
            KK = sb(ctx, "KK", [P, 2, S])
            PQ = sb(ctx, "PQ", [P, 2, 3, S], BF16)
            PK = sb(ctx, "PK", [P, 2, 3, S], BF16)
            RES = sb(ctx, "RES", [P, 2, S])
            YB = sb(ctx, "YB", [P, NT, HEADS])
            SG = sb(ctx, "SG", [P, NT, HEADS])
            PR = sb(ctx, "PR", [P, NT, HEADS])
            KA = sb(ctx, "KA", [P, NT, HEADS, 6], BF16)
            KAT = sb(ctx, "KAT", [HEADS * 6, S], BF16)
            PB = sb(ctx, "PB", [P, 2, DE])
            TH = sb(ctx, "TH", [P, 2, DE])
            MX = sb(ctx, "MX", [P, 4, NT])
            MR = sb(ctx, "MR", [P, 4, NT])
            QA = sb(ctx, "QA", [P, 4, NT, 6], BF16)
            OT = sb(ctx, "OT", [P, S])
            RS_ = sb(ctx, "RS_", [P, NT, 4])
            ON = sb(ctx, "ON", [P, NT, HEADS, DH])
            GT = sb(ctx, "GT", [P, 2, S])
            T = sb(ctx, "T_a", [P, NT, D])
            N1 = sb(ctx, "N1_a", [P, NT, D])
            STa = sb(ctx, "STa", [P, NT, 6])
            MVa = sb(ctx, "MVa", [P, NT, 2])
            rta = sb(ctx, "rta", [P, B * NT])
            sets = []
            for i in range(2):
                sets.append((sb(ctx, f"sta{i}", [P, NT, 6]), sb(ctx, f"mva{i}", [P, NT, 2]),
                             sb(ctx, f"rt_a{i}", [P, NT]), sb(ctx, f"rs_a{i}", [P, NT])))
            tri = sb(ctx, "tri", [P, P])
            ones = sb(ctx, "ones_a", [P, P])
            maskU = sb(ctx, "maskU", [P, P], BF16)
            maskL = sb(ctx, "maskL", [P, P], BF16)
            bqs = sb(ctx, "bqs", [P, 2])
            warm = sb(ctx, "warm4", [P, 1])

            p_x = PS[:, 0:2, :]
            p_e = PS[:, 2:4, :]
            p_o = PS[:, 4, :]
            p_m = PS[:, 5, :]
            p_a = PS[:, 6, :]
            p_b = PS[:, 7, :]

            warmed = signal("att_warm")
            acon = signal("att_consts")
            acon2 = signal("q_bias_ready")
            astats = signal("att_x_stats", NT)
            aaggr = signal("att_x_aggr", NT)
            amv_kept = signal("att_x_moments_kept")
            arst = signal("att_rstd_steps")
            xn = signal("xn_ready", NT)
            xnT_ps = signal("xnT_ps")
            xnT = signal("xnT_ready")
            y_ps = signal("y_ps")
            yb = signal("yb_ready")
            th = signal("gate_tanh_ready")
            sg = signal("gate_sigmoid_ready")
            qk_ps = signal("qk_ps", 4)
            qk = signal("qk_ready", 4)
            kk1 = signal("k_scaled", 2)
            kk2 = signal("k_smeared", 2)
            part1 = signal("part1_ready", 4)
            rest1 = signal("rest1_ready", 4)
            part2 = signal("part2_ready", 4)
            part3 = signal("part3_ready", 4)
            vp_ps = signal("vp_ps", NT)
            v_kept = signal("v_kept", NT)
            pb = signal("pb_ready", NT)
            pth = signal("silu_tanh_ready", NT)
            sp_ = signal("silu_ready", NT)
            pos_ps = signal("pos_ps")
            ka = signal("ka_ready", 5)
            kaT_ps = signal("kaT_ps")
            kaT = signal("kaT_ready")
            parts_out = signal("parts_to_dram", 16 * 5)
            stack_in = signal("stacks_in", 16 * 13)
            s_ps = signal("score_ps", 16 * NG4)
            mx_ = signal("max_ready", 16 * NG4)
            qa = signal("max_parts_ready", 5 * NG4)
            m_ps = signal("max_rows_ps", NG4)
            m_in = signal("max_rows_ready", 4 * NG4)
            e_ps = signal("score_minus_max_ps", 16 * NG4)
            ex = signal("exp_ready", 16 * NG4)
            o_ps = signal("o_ps", NG4)
            o_kept = signal("o_kept", NG4)
            oT_ps = signal("oT_ps", NG4)
            rden = signal("inverse_sum_ready", NG4)
            on = signal("o_normal", NG4)
            gated = signal("gated_ready")
            gT_ps = signal("gatedT_ps", 2)
            gT = signal("gatedT_ready", 2)
            w_ps = signal("att_out_ps")
            t_kept = signal("att_out_kept")
            st = [signal(f"a_stats{i}", NT) for i in range(2)]
            mv = [signal(f"a_moments{i}", NT) for i in range(2)]
            rs = [signal(f"a_scale{i}", 2) for i in range(2)]
            n1 = signal("a_n1_ready", NT)
            n1w = signal("a_n1w_ready", 2)
            n2 = signal("a_n2_ready", NT)
            x3 = signal("x3_ready")

            block = ctx.enter_context(nc.Block())

            def sequences(eng, project, maxima, slot, output):
                for s in range(9):
                    project(0, 0, s)
                for j in range(NT):
                    maxima(0, 0, 0, j)

                def body(b, p, before, after):
                    for g in range(NG4):
                        for j in range(NT):
                            s = NT * g + j
                            more = (b, p, g + 1) if g + 1 < NG4 else None if after is None else (after, 1 - p, 0)
                            slot(b, p, g, j, more, before)
                            if after is not None and s < 9:
                                project(after, 1 - p, s)
                            if before is not None and s < 11:
                                output(before, 1 - p, s)
                            if j == NT - 1:
                                slot(b, p, g, NT, more, before)
                body(0, 0, None, 1)
                with eng.Fori(0, B // 2 - 1) as q:
                    for k in range(2):
                        body(eng.snap(q * 2 + (k + 1)), 1 - k, eng.snap(q * 2 + k), eng.snap(q * 2 + (k + 2)))
                body(B - 1, 1, B - 2, None)
                slot(B, 0, 0, 1, None, B - 1)
                for s in range(11):
                    output(B - 1, 1, s)

            def group_before(b, g, before):
                return (b, g - 1) if g else (before, NG4 - 1)

            @block.sync
            def _(sp):
                def project(b, p):
                    at = bass.ds(b, 1)
                    one = lambda ap: ap.rearrange("o a n -> (o a) n") if len(ap.shape) == 3 else ap.rearrange("o s a n -> (o s) a n")
                    for i, (parts, dram) in enumerate(((PQ, qd), (PQ, qd), (PK, kd), (PK, kd))):
                        c = i % 2
                        sp.wait_ge(part3.sem, part3.value(sp, b, i + 1))
                        sp.dma_start(one(dram[at])[:, c * P:(c + 1) * P, :].rearrange("s p n -> p s n"),
                                     parts[:, c, :, :]).then_inc(parts_out.sem, 16)
                    sp.wait_ge(kaT.sem, kaT.value(sp, b))
                    sp.dma_start(one(ad[at]), KAT[:, :]).then_inc(parts_out.sem, 16)
                    sp.wait_ge(parts_out.sem, parts_out.value(sp, b))
                    def head_rows(dram, s):
                        return one(dram[at])[s, :, :].rearrange("(h d) n -> d h n", d=DH)
                    for r, (qp, kp) in enumerate(((0, 0), (0, 1), (0, 2), (1, 0), (1, 1), (2, 0))):
                        sp.dma_start(QS[r * DH:(r + 1) * DH, p, :, :], head_rows(qd, qp)).then_inc(stack_in.sem, 16)
                        sp.dma_start(KS[r * DH:(r + 1) * DH, p, :, :], head_rows(kd, kp)).then_inc(stack_in.sem, 16)
                    sp.dma_start(KS[96:KF, p, :, :], one(ad[at]).rearrange("(h r) n -> r h n", r=6)).then_inc(stack_in.sem, 16)

                with sp.Fori(0, B // 2) as q:
                    for p in range(2):
                        project(sp.snap(q * 2 + p), p)

            @block.gpsimd
            def _(pool):
                pool.memset(tri[:, :], 1.0).then_inc(acon.sem, 1)
                pool.memset(ones[:, :], 1.0).then_inc(acon.sem, 1)
                pool.memset(maskU[:, :], 0.0).then_inc(acon.sem, 1)
                pool.memset(maskL[:, :], 0.0).then_inc(acon.sem, 1)
                pool.memset(VV[:, :, :, :, DH:32], 0.0).then_inc(acon.sem, 1)
                pool.memset(KA[:, :, :, :], 1.0).then_inc(acon.sem, 1)
                pool.memset(QA[:, :, :, :], 1.0).then_inc(acon.sem, 1)
                pool.wait_ge(acon.sem, 7)
                pool.memset(VV[:, :, :, :, DH:DH + 1], 1.0).then_inc(acon.sem, 1)
                pool.affine_select(out=tri[:, :], in_=tri[:, :], compare_op=ALU.is_ge, fill=0.0, base=0,
                                   pattern=[[1, P]], channel_multiplier=-1).then_inc(acon.sem, 1)
                pool.affine_select(out=maskU[:, :], in_=maskU[:, :], compare_op=ALU.is_ge, fill=NEG_BIG, base=0,
                                   pattern=[[-1, P]], channel_multiplier=1).then_inc(acon.sem, 1)
                pool.affine_select(out=maskL[:, :], in_=maskL[:, :], compare_op=ALU.is_ge, fill=NEG_BIG, base=0,
                                   pattern=[[1, P]], channel_multiplier=-1).then_inc(acon.sem, 1)
                pool.wait_ge(amv_kept.sem, B)
                pool.tensor_scalar(rta[:, :], MV[:, :, 1], EPS, None, ALU.add).then_inc(arst.sem, 1)
                pool.wait_ge(arst.sem, 1)
                pool.tensor_tensor(R1[:, :], rta[:, :], half[:, :], ALU.pow).then_inc(arst.sem, 1)
                pool.wait_ge(arst.sem, 2)
                pool.tensor_tensor(rta[:, :], R1[:, :], R1[:, :], ALU.mult).then_inc(arst.sem, 1)
                pool.wait_ge(arst.sem, 3)
                pool.tensor_tensor(rta[:, :], rta[:, :], MV[:, :, 1], ALU.mult).then_inc(arst.sem, 1)
                pool.wait_ge(arst.sem, 4)
                pool.tensor_scalar(rta[:, :], rta[:, :], EPS, None, ALU.add).then_inc(arst.sem, 1)
                pool.wait_ge(arst.sem, 5)
                pool.tensor_tensor(rta[:, :], rta[:, :], half[:, :], ALU.pow).then_inc(arst.sem, 1)
                pool.wait_ge(arst.sem, 6)
                pool.tensor_tensor(RR[:, :], rta[:, :], R1[:, :], ALU.mult).then_inc(arst.sem, 1)

                def attend(b):
                    for i in range(2):
                        _, m, r_t, r_s = sets[i]
                        pool.wait_ge(mv[i].sem, mv[i].value(pool, b))
                        layer_norm_scale(pool, m, r_t, r_s, rs[i], b, 0)
                with pool.Fori(0, B) as b:
                    attend(b)

            @block.tensor
            def _(pe):
                pe.wait_ge(acon.sem, 11)
                pe.wait_ge(acon2.sem, 2)

                def project(b, p, s):
                    if s == 0:
                        pe.wait_ge(xn.sem, xn.value(pe, b))
                        for t in range(NT):
                            last = pe.transpose(p_a[:, t * P:(t + 1) * P], XN[:, t, :], ident[:, :])
                        last.then_inc(xnT_ps.sem, 1)
                    if s == 1:
                        pe.wait_ge(xnT.sem, xnT.value(pe, b))
                        p_y = p_b[:, 0:NT * HEADS].rearrange("p (t h) -> p t h", t=NT)
                        for t in range(NT):
                            last = pe.matmul(p_y[:, t, :], XT[:, t * P:(t + 1) * P], winT[:, 4 * DE:], start=True, stop=True)
                        last.then_inc(y_ps.sem, 1)
                    for c in {1: (0,), 3: (1,), 4: (2, 3)}.get(s, ()):
                        if c == 1:
                            pe.wait_ge(yb.sem, yb.value(pe, b))
                        if c >= 2:
                            pe.wait_ge(qk.sem, qk.value(pe, b, c - 1))
                        if c == 2:
                            wait_output(b)
                        pe.matmul(PS[:, 6 + c % 2, :], winT[:, c * P:(c + 1) * P], XT[:, :],
                                  start=True, stop=True).then_inc(qk_ps.sem, 1)
                    for t in {5: (0, 1), 6: (2, 3)}.get(s, ()):
                        if t < 2:
                            pe.wait_ge(qk.sem, qk.value(pe, b, t + 3))
                        else:
                            pe.wait_ge(pb.sem, pb.value(pe, b, t - 1))
                        pe.matmul(PS[:, 6 + t % 2, :], XT[:, t * P:(t + 1) * P], winT[:, 2 * DE:4 * DE],
                                  start=True, stop=True).then_inc(vp_ps.sem, 1)
                    if s == 7:
                        pe.wait_ge(pb.sem, pb.value(pe, b, NT - 1))
                        pe.wait_ge(sg.sem, sg.value(pe, b))
                        p_p = p_a[:, 0:NT * HEADS].rearrange("p (t h) -> p t h", t=NT)
                        for t in range(NT):
                            for i in range(t + 1):
                                last = pe.matmul(p_p[:, t, :], (tri if i == t else ones)[:, :], SG[:, i, :],
                                                 start=(i == 0), stop=(i == t))
                        last.then_inc(pos_ps.sem, 1)
                    if s == 8:
                        pe.wait_ge(pb.sem, pb.value(pe, b))
                        pe.wait_ge(ka.sem, ka.value(pe, b))
                        p_k = p_b.bitcast(BF16)[0:HEADS * 6, 0:S]
                        for t in range(NT):
                            last = pe.transpose(p_k[:, t * P:(t + 1) * P], KA[:, t, :, :].rearrange("p h r -> p (h r)"), identb[:, :])
                        last.then_inc(kaT_ps.sem, 1)

                def wait_output(b):
                    if not isinstance(b, int):
                        pe.wait_ge(t_kept.sem, pe.snap(b - 1))
                    elif b >= 2:
                        pe.wait_ge(t_kept.sem, b - 1)

                def score_for_max(b, p, g, it, i):
                    n = (it + 1) * P
                    u, h = 4 * it + i, 4 * g + i
                    if u >= 2:
                        pe.wait_ge(mx_.sem, mx_.value(pe, b, 16 * g + u - 1))
                    pe.matmul(p_x[:, i % 2, 0:n], QS[0:KM, p, h, it * P:(it + 1) * P], KS[0:KM, p, h, 0:n], start=True, stop=False)
                    pe.matmul(p_x[:, i % 2, n - P:n], identb[:, :], maskU[:, :], start=False, stop=True).then_inc(s_ps.sem, 1)

                def rows_of_maxima(b, p, g):
                    pe.wait_ge(qa.sem, qa.value(pe, b, 5 * (g + 1)))
                    for i in range(4):
                        for t in range(NT):
                            last = pe.transpose(p_m.bitcast(BF16)[32 * i:32 * i + 6, t * P:(t + 1) * P], QA[:, i, t, :],
                                                identb[:, :], tile_position=(0, 32 * i))
                    last.then_inc(m_ps.sem, 1)

                def maxima(b, p, g, it):
                    if it == 0 and g == 0:
                        pe.wait_ge(stack_in.sem, stack_in.value(pe, b))
                    for i in range(4):
                        score_for_max(b, p, g, it, i)
                    if it == NT - 1:
                        rows_of_maxima(b, p, g)

                def times_v(b, p, g, j):
                    pe.wait_ge(ex.sem, ex.value(pe, b, 16 * g + 4 * j + 4))
                    for i in range(4):
                        last = pe.matmul(p_o[32 * i:32 * i + 32, j * P:S], VV[:, p, j, 4 * g + i, :], PT[:, j % 2, i, 0:S - j * P],
                                         start=(j == 0), stop=(j == NT - 1), tile_position=(0, 32 * i), skip_group_check=True)
                    return last

                def slot(b, p, g, j, more, before):
                    if j == NT:
                        times_v(b, p, g, NT - 1).then_inc(o_ps.sem, 1)
                        if more:
                            rows_of_maxima(*more)
                        return
                    if b is not B and not (isinstance(b, int) and b == B):
                        if j == 0:
                            pe.wait_ge(m_in.sem, m_in.value(pe, b, 4 * (g + 1)))
                        if more and j == 0 and more[2] == 0:
                            pe.wait_ge(stack_in.sem, stack_in.value(pe, more[0]))
                        n = S - j * P
                        for i in range(4):
                            u, h = 4 * j + i, 4 * g + i
                            if u >= 2:
                                pe.wait_ge(ex.sem, ex.value(pe, b, 16 * g + u - 1))
                            pe.matmul(p_e[:, i % 2, 0:n], KS[0:KF, p, h, j * P:(j + 1) * P],
                                      QS[0:KF, p, h, j * P:S], start=True, stop=False)
                            pe.matmul(p_e[:, i % 2, 0:P], identb[:, :], maskL[:, :], start=False, stop=True).then_inc(e_ps.sem, 1)
                            if more:
                                score_for_max(*more, j, i)
                        if j >= 1:
                            if j == 1:
                                o = group_before(b, g, before)
                                if o[0] is not None:
                                    pe.wait_ge(o_kept.sem, o_kept.value(pe, o[0], o[1] + 1))
                            times_v(b, p, g, j - 1)
                    if j == 1:
                        o = group_before(b, g, before)
                        if o[0] is not None:
                            pe.wait_ge(o_kept.sem, o_kept.value(pe, o[0], o[1] + 1))
                            for t in range(NT):
                                last = pe.transpose(p_m[:, t * P:(t + 1) * P], OT[:, t * P:(t + 1) * P], ident[:, :])
                            last.then_inc(oT_ps.sem, 1)
                    if j == 3:
                        o = group_before(b, g, before)
                        if o[0] is not None:
                            pe.wait_ge(on.sem, on.value(pe, o[0], o[1] + 1))

                def output(b, p, s):
                    if s == 2:
                        pe.wait_ge(gated.sem, gated.value(pe, b))
                        for c in range(2):
                            for t in range(NT):
                                last = pe.transpose(PS[:, 6 + c, t * P:(t + 1) * P],
                                                    ON[:, t, 8 * c:8 * c + 8, :].rearrange("p h d -> p (h d)"), ident[:, :])
                            last.then_inc(gT_ps.sem, 1)
                    if s == 3:
                        pe.wait_ge(gT.sem, gT.value(pe, b))
                        p_w = p_a.rearrange("p (t d) -> p t d", t=NT)
                        for t in range(NT):
                            for c in range(2):
                                last = pe.matmul(p_w[:, t, :], GT[:, c, t * P:(t + 1) * P], waoT[:, c, :], start=(c == 0), stop=(c == 1))
                        last.then_inc(w_ps.sem, 1)
                sequences(pe, project, maxima, slot, output)

            @block.scalar
            def _(act):
                act.activation(warm[:, :], half[:, 0:1], ACT.Tanh).then_inc(warmed.sem, 1)

                act.wait_ge(acon2.sem, 2)

                def project(b, p, s):
                    if s == 0:
                        act.wait_ge(xnT_ps.sem, xnT_ps.value(act, b))
                        act.activation(XT[:, :], p_a, ACT.Identity, scale=ilw[:, 0:1], bias=ilb[:, 0:1]).then_inc(xnT.sem, 1)
                    for c in {1: (0,), 3: (1,), 4: (2, 3)}.get(s, ()):
                        act.wait_ge(qk_ps.sem, qk_ps.value(act, b, c + 1))
                        if c < 2:
                            act.activation(QF[:, c, :], PS[:, 6 + c, :], ACT.Identity, scale=qsc[:, 4 + c:5 + c],
                                           bias=bqs[:, c:c + 1]).then_inc(qk.sem, 1)
                        else:
                            act.activation(KF_[:, c - 2, :], PS[:, 4 + c, :], ACT.Identity, bias=bqk[:, c:c + 1]).then_inc(qk.sem, 1)
                    if s == 3:
                        act.wait_ge(yb.sem, yb.value(act, b))
                        act.activation(SG[:, :, :], YB[:, :, :], ACT.Tanh, scale=0.5).then_inc(th.sem, 1)
                    if s == 4:
                        act.wait_ge(parts_out.sem, parts_out.before(act, b))
                    for i in {4: (0, 1), 5: (2, 3)}.get(s, ()):
                        src, dst = (QF, PQ) if i < 2 else (KK, PK)
                        if i < 2:
                            act.wait_ge(qk.sem, qk.value(act, b, i + 1))
                        else:
                            act.wait_ge(kk2.sem, kk2.value(act, b, i - 1))
                        act.activation(dst[:, i % 2, 0, :], src[:, i % 2, :], ACT.Copy).then_inc(part1.sem, 1)
                    for t in {5: (0, 1), 6: (2, 3)}.get(s, ()):
                        act.wait_ge(pb.sem, pb.value(act, b, t + 1))
                        act.activation(TH[:, t % 2, :], PB[:, t % 2, :], ACT.Tanh, scale=0.5).then_inc(pth.sem, 1)
                    if s == 8:
                        act.wait_ge(kaT_ps.sem, kaT_ps.value(act, b))
                        act.activation(KAT[:, :], p_b.bitcast(BF16)[0:HEADS * 6, 0:S], ACT.Copy).then_inc(kaT.sem, 1)

                def rows_of_maxima(b, p, g):
                    act.wait_ge(m_ps.sem, m_ps.value(act, b, g + 1))
                    for i in range(4):
                        act.activation(QS[96:KF, p, 4 * g + i, :], p_m.bitcast(BF16)[32 * i:32 * i + 6, 0:S],
                                       ACT.Copy).then_inc(m_in.sem, 1)

                def maxima(b, p, g, it):
                    if it == NT - 1:
                        rows_of_maxima(b, p, g)

                def slot(b, p, g, j, more, before):
                    if isinstance(b, int) and b == B:
                        return
                    if j == NT:
                        act.wait_ge(o_ps.sem, o_ps.value(act, b, g + 1))
                        act.activation(OT[:, :], p_o, ACT.Copy).then_inc(o_kept.sem, 1)
                        if more:
                            rows_of_maxima(*more)
                        return
                    n = S - j * P
                    for i in range(4):
                        act.wait_ge(e_ps.sem, e_ps.value(act, b, 16 * g + 4 * j + i + 1))
                        act.activation(PT[:, j % 2, i, 0:n], p_e[:, i % 2, 0:n], ACT.Exp).then_inc(ex.sem, 1)

                def output(b, p, s):
                    if s == 2:
                        for c in range(2):
                            act.wait_ge(gT_ps.sem, gT_ps.value(act, b, c + 1))
                            act.activation(GT[:, c, :], PS[:, 6 + c, :], ACT.Copy).then_inc(gT.sem, 1)
                sequences(act, project, maxima, slot, output)

            @block.vector
            def _(dve):
                dve.memset(QS[96:KF, :, :, :], 1.0).then_inc(acon2.sem, 1)
                dve.tensor_tensor(bqs[:, :], bqk[:, 0:2], qsc[:, 4:6], ALU.mult).then_inc(acon2.sem, 1)
                x_moments(dve, STa, MVa, astats, aaggr, amv_kept)
                dve.wait_ge(arst.sem, 7)

                def project(b, p, s):
                    if s == 0:
                        for t in range(NT):
                            if isinstance(b, int):
                                at = slice(b * NT + t, b * NT + t + 1)
                            else:
                                at = bass.ds(dve.snap(b * NT + t), 1)
                            dve.tensor_scalar(XN[:, t, :], X[:, at, :].rearrange("p o d -> p (o d)"),
                                              MV[:, at, 0:1].rearrange("p o k -> p (o k)"), RR[:, at],
                                              ALU.subtract, ALU.mult).then_inc(xn.sem, 1)
                    if s == 1:
                        dve.wait_ge(y_ps.sem, y_ps.value(dve, b))
                        dve.tensor_tensor(YB[:, :, :], p_b[:, 0:NT * HEADS].rearrange("p (t h) -> p t h", t=NT),
                                          bvpy[:, 2 * DE:].unsqueeze(1).to_broadcast([P, NT, HEADS]), ALU.add).then_inc(yb.sem, 1)
                    if s == 4:
                        dve.wait_ge(th.sem, th.value(dve, b))
                        dve.tensor_scalar(SG[:, :, :], SG[:, :, :], 0.5, 0.5, ALU.mult, ALU.add).then_inc(sg.sem, 1)
                    for c in {5: (0, 1)}.get(s, ()):
                        dve.wait_ge(qk.sem, qk.value(dve, b, 3 + c))
                        dve.tensor_scalar(KK[:, c, :], KF_[:, c, :], qsc[:, c:c + 1], None, ALU.mult).then_inc(kk1.sem, 1)
                        dve.wait_ge(kk1.sem, kk1.value(dve, b, c + 1))
                        dve.scalar_tensor_tensor(KK[:, c, 1:S], KF_[:, c, 0:S - 1], qsc[:, 2 + c:3 + c], KK[:, c, 1:S],
                                                 ALU.mult, ALU.add).then_inc(kk2.sem, 1)
                    for t in {6: (0, 1), 7: (2, 3)}.get(s, ()):
                        dve.wait_ge(pth.sem, pth.value(dve, b, t + 1))
                        dve.scalar_tensor_tensor(SP[:, p, t, :], TH[:, t % 2, :], 1.0, PB[:, t % 2, :], ALU.add, ALU.mult).then_inc(sp_.sem, 1)
                    for t in {5: (0, 1), 6: (2, 3)}.get(s, ()):
                        if t >= 2:
                            dve.wait_ge(sp_.sem, sp_.value(dve, b, t - 1))
                        dve.wait_ge(vp_ps.sem, vp_ps.value(dve, b, t + 1))
                        bank = PS[:, 6 + t % 2, :]
                        dve.tensor_tensor(VV[:, p, t, :, 0:DH], bank[:, 0:DE].rearrange("p (h d) -> p h d", d=DH),
                                          bvpy[:, 0:DE].rearrange("p (h d) -> p h d", d=DH), ALU.add).then_inc(v_kept.sem, 1)
                        dve.tensor_tensor(PB[:, t % 2, :], bank[:, DE:], bvpy[:, DE:2 * DE], ALU.add).then_inc(pb.sem, 1)
                    for i in {6: (0, 1), 7: (2, 3)}.get(s, ()):
                        src, dst = (QF, PQ) if i < 2 else (KK, PK)
                        c = i % 2
                        if i >= 2:
                            dve.wait_ge(part3.sem, part3.value(dve, b, i - 1))
                        dve.wait_ge(part1.sem, part1.value(dve, b, i + 1))
                        dve.tensor_tensor(RES[:, c, :], src[:, c, :], dst[:, c, 0, :], ALU.subtract).then_inc(rest1.sem, 1)
                        dve.wait_ge(rest1.sem, rest1.value(dve, b, i + 1))
                        dve.tensor_copy(dst[:, c, 1, :], RES[:, c, :]).then_inc(part2.sem, 1)
                        dve.wait_ge(part2.sem, part2.value(dve, b, i + 1))
                        dve.tensor_tensor(dst[:, c, 2, :], RES[:, c, :], dst[:, c, 1, :], ALU.subtract).then_inc(part3.sem, 1)
                    if s == 7:
                        p_p = p_a[:, 0:NT * HEADS].rearrange("p (t h) -> p t h", t=NT)
                        dve.wait_ge(pos_ps.sem, pos_ps.value(dve, b))
                        dve.tensor_copy(KA[:, :, :, 0], p_p).then_inc(ka.sem, 1)
                        dve.wait_ge(ka.sem, ka.value(dve, b, 1))
                        dve.tensor_tensor(PR[:, :, :], p_p, KA[:, :, :, 0], ALU.subtract).then_inc(ka.sem, 1)
                        dve.wait_ge(ka.sem, ka.value(dve, b, 2))
                        dve.tensor_copy(KA[:, :, :, 1], PR[:, :, :]).then_inc(ka.sem, 1)
                        dve.wait_ge(ka.sem, ka.value(dve, b, 3))
                        dve.tensor_tensor(KA[:, :, :, 2], PR[:, :, :], KA[:, :, :, 1], ALU.subtract).then_inc(ka.sem, 2)

                def maxima(b, p, g, it):
                    n = (it + 1) * P
                    for i in range(4):
                        dve.wait_ge(s_ps.sem, s_ps.value(dve, b, 16 * g + 4 * it + i + 1))
                        dve.tensor_reduce(MX[:, i, it:it + 1], p_x[:, i % 2, 0:n], AX.X, ALU.max,
                                          negate=True).then_inc(mx_.sem, 1)
                    if it == NT - 1:
                        dve.wait_ge(mx_.sem, mx_.value(dve, b, 16 * (g + 1)))
                        dve.tensor_copy(QA[:, :, :, 3], MX[:, :, :]).then_inc(qa.sem, 1)
                        dve.wait_ge(qa.sem, qa.value(dve, b, 5 * g + 1))
                        dve.tensor_tensor(MR[:, :, :], MX[:, :, :], QA[:, :, :, 3], ALU.subtract).then_inc(qa.sem, 1)
                        dve.wait_ge(qa.sem, qa.value(dve, b, 5 * g + 2))
                        dve.tensor_copy(QA[:, :, :, 4], MR[:, :, :]).then_inc(qa.sem, 1)
                        dve.wait_ge(qa.sem, qa.value(dve, b, 5 * g + 3))
                        dve.tensor_tensor(QA[:, :, :, 5], MR[:, :, :], QA[:, :, :, 4], ALU.subtract).then_inc(qa.sem, 2)

                def slot(b, p, g, j, more, before):
                    if j == NT:
                        return
                    if more:
                        maxima(*more, j)
                    o = group_before(b, g, before)
                    if j == 1 and o[0] is not None:
                        o_b, o_g = o
                        dve.wait_ge(oT_ps.sem, oT_ps.value(dve, o_b, o_g + 1))
                        o4 = p_m.rearrange("p (t h d) -> p t h d", t=NT, h=4)
                        dve.reciprocal(RS_[:, :, :], o4[:, :, :, DH]).then_inc(rden.sem, 1)
                        dve.wait_ge(rden.sem, rden.value(dve, o_b, o_g + 1))
                        dve.tensor_tensor(ON[:, :, 4 * o_g:4 * o_g + 4, :], o4[:, :, :, 0:DH],
                                          RS_[:, :, :].unsqueeze(3).to_broadcast([P, NT, 4, DH]), ALU.mult).then_inc(on.sem, 1)

                def moments(i, src, b):
                    s_t, m, _, _ = sets[i]
                    for t in range(NT):
                        dve.bn_stats(s_t[:, t, :], src[:, t, :]).then_inc(st[i].sem, 1)
                    hold(dve, st[i].sem, st[i].value(dve, b))
                    for t in range(NT):
                        dve.bn_aggr(m[:, t, :], s_t[:, t, :]).then_inc(mv[i].sem, 1)

                def normal(i, dst, src, b, done):
                    _, m, _, r_s = sets[i]
                    dve.wait_ge(rs[i].sem, rs[i].value(dve, b))
                    for t in range(NT):
                        dve.tensor_scalar(dst[:, t, :], src[:, t, :], m[:, t, 0:1], r_s[:, t:t + 1],
                                          ALU.subtract, ALU.mult).then_inc(done.sem, 1)
                    dve.wait_ge(done.sem, done.value(dve, b))

                def output(b, p, s):
                    if s == 1:
                        dve.wait_ge(on.sem, on.value(dve, b))
                        flat = ON[:, :, :, :].rearrange("p t h d -> p (t h d)")
                        dve.tensor_tensor(flat, flat, SP[:, p, :, :].rearrange("p t n -> p (t n)"), ALU.mult).then_inc(gated.sem, 1)
                    if s == 3:
                        dve.wait_ge(w_ps.sem, w_ps.value(dve, b))
                        dve.tensor_copy(T[:, :, :], p_a.rearrange("p (t d) -> p t d", t=NT)).then_inc(t_kept.sem, 1)
                        dve.wait_ge(t_kept.sem, t_kept.value(dve, b))
                        moments(0, T, b)
                    if s == 9:
                        normal(0, N1, T, b, n1)
                        dve.tensor_tensor(N1[:, :, :], N1[:, :, :], olw[:, :].unsqueeze(1).to_broadcast([P, NT, D]), ALU.mult).then_inc(n1w.sem, 1)
                        dve.wait_ge(n1w.sem, n1w.value(dve, b, 1))
                        dve.tensor_tensor(N1[:, :, :], N1[:, :, :], olb[:, :].unsqueeze(1).to_broadcast([P, NT, D]), ALU.add).then_inc(n1w.sem, 1)
                        dve.wait_ge(n1w.sem, n1w.value(dve, b))
                        moments(1, N1, b)
                    if s == 10:
                        normal(1, T, N1, b, n2)
                        x = X[:, b * NT:(b + 1) * NT, :] if isinstance(b, int) else X[:, bass.ds(dve.snap(b * NT), NT), :]
                        dve.tensor_tensor(x, x, T[:, :, :], ALU.add).then_inc(x3.sem, 1)
                sequences(dve, project, maxima, slot, output)

        ctx = ExitStack()
        with ctx:
            XF = sb(ctx, "XF_e", [P, NT, D])
            XT = sb(ctx, "XT_e", [P, S])
            TG = sb(ctx, "TG", [P, NH, S])
            SGU = sb(ctx, "SGU", [P, NH, S])
            HU = sb(ctx, "HU", [P, NH, S])
            T = sb(ctx, "T_e", [P, NT, D])
            N1 = sb(ctx, "N1_e", [P, NT, D])
            sets = []
            for i in range(2):
                sets.append((sb(ctx, f"ste{i}", [P, NT, 6]), sb(ctx, f"mve{i}", [P, NT, 2]),
                             sb(ctx, f"rt_e{i}", [P, NT]), sb(ctx, f"rs_e{i}", [P, NT])))
            warm = sb(ctx, "warm5", [P, 1])
            warmed = signal("swiglu_warm")
            st = [signal(f"e_stats{i}", NT) for i in range(2)]
            mv = [signal(f"e_moments{i}", NT) for i in range(2)]
            rs = [signal(f"e_scale{i}", 2) for i in range(2)]
            xg = signal("xg_ready", NT)
            xgT_ps = signal("xgT_ps")
            xgT = signal("xgT_ready")
            gu_ps = signal("gate_up_ps", 2 * NH)
            tg = signal("swiglu_tanh_ready", NH)
            sgr = signal("swiglu_gate_ready", NH)
            hu = signal("hidden_ready", NH)
            dn = signal("down_ps")
            tk = signal("down_kept")
            n1 = signal("e_n1_ready", NT)
            x4 = signal("x4_ready")
            stored = signal("stored", 16)
            block = ctx.enter_context(nc.Block())

            @block.sync
            def _(sp):
                for b in range(B):
                    sp.wait_ge(x4.sem, b + 1)
                    sp.dma_start(out_d[b].rearrange("(t p) d -> p t d", p=P), X[:, b * NT:(b + 1) * NT, :]).then_inc(stored.sem, 16)
                sp.wait_ge(stored.sem, 16 * B)

            @block.gpsimd
            def _(pool):
                with pool.Fori(0, B) as b:
                    for i in range(2):
                        _, m, r_t, r_s = sets[i]
                        pool.wait_ge(mv[i].sem, mv[i].value(pool, b))
                        layer_norm_scale(pool, m, r_t, r_s, rs[i], b, 0)

            @block.tensor
            def _(pe):
                with pe.Fori(0, B) as b:
                    pe.wait_ge(xg.sem, xg.value(pe, b))
                    for t in range(NT):
                        last = pe.transpose(PS[:, 0, t * P:(t + 1) * P], XF[:, t, :], ident[:, :])
                    last.then_inc(xgT_ps.sem, 1)
                    pe.wait_ge(xgT.sem, xgT.value(pe, b))
                    for c in range(NH):
                        for o in range(2):
                            pe.matmul(PS[:, 1 + NH * o + c, :], wguT[:, o * HID + c * P:o * HID + (c + 1) * P], XT[:, :],
                                      start=True, stop=True).then_inc(gu_ps.sem, 1)
                    p_dn = PS[:, 7, :].rearrange("p (t d) -> p t d", t=NT)
                    for t in range(NT):
                        for c in range(NH):
                            if t == 0:
                                pe.wait_ge(hu.sem, hu.value(pe, b, c + 1))
                            last = pe.matmul(p_dn[:, t, :], HU[:, c, t * P:(t + 1) * P], wdT[:, c, :],
                                             start=(c == 0), stop=(c == NH - 1))
                    last.then_inc(dn.sem, 1)

            @block.scalar
            def _(act):
                act.activation(warm[:, :], half[:, 0:1], ACT.Tanh).then_inc(warmed.sem, 1)
                with act.Fori(0, B) as b:
                    act.wait_ge(xgT_ps.sem, xgT_ps.value(act, b))
                    act.activation(XT[:, :], PS[:, 0, :], ACT.Copy).then_inc(xgT.sem, 1)
                    for c in range(NH):
                        act.wait_ge(gu_ps.sem, gu_ps.value(act, b, 2 * c + 1))
                        act.activation(TG[:, c, :], PS[:, 1 + c, :], ACT.Tanh, scale=0.5).then_inc(tg.sem, 1)

            @block.vector
            def _(dve):
                def moments(i, src, b):
                    s_t, m, _, _ = sets[i]
                    for t in range(NT):
                        dve.bn_stats(s_t[:, t, :], src(t)).then_inc(st[i].sem, 1)
                    hold(dve, st[i].sem, st[i].value(dve, b))
                    for t in range(NT):
                        dve.bn_aggr(m[:, t, :], s_t[:, t, :]).then_inc(mv[i].sem, 1)

                def normal(i, dst, src, b, done):
                    _, m, _, r_s = sets[i]
                    dve.wait_ge(rs[i].sem, rs[i].value(dve, b))
                    for t in range(NT):
                        dve.tensor_scalar(dst[:, t, :], src(t), m[:, t, 0:1], r_s[:, t:t + 1],
                                          ALU.subtract, ALU.mult).then_inc(done.sem, 1)
                with dve.Fori(0, B) as b:
                    tiles = lambda: X[:, bass.ds(dve.snap(b * NT), NT), :]
                    tile = lambda t: X[:, bass.ds(dve.snap(b * NT + t), 1), :].rearrange("p o d -> p (o d)")
                    moments(0, tile, b)
                    normal(0, XF, tile, b, xg)
                    for c in range(NH):
                        dve.wait_ge(tg.sem, tg.value(dve, b, c + 1))
                        dve.scalar_tensor_tensor(SGU[:, c, :], TG[:, c, :], 1.0, PS[:, 1 + c, :], ALU.add, ALU.mult).then_inc(sgr.sem, 1)
                        dve.wait_ge(gu_ps.sem, gu_ps.value(dve, b, 2 * c + 2))
                        dve.wait_ge(sgr.sem, sgr.value(dve, b, c + 1))
                        dve.tensor_tensor(HU[:, c, :], SGU[:, c, :], PS[:, 1 + NH + c, :], ALU.mult).then_inc(hu.sem, 1)
                    dve.wait_ge(dn.sem, dn.value(dve, b))
                    dve.tensor_copy(T[:, :, :], PS[:, 7, :].rearrange("p (t d) -> p t d", t=NT)).then_inc(tk.sem, 1)
                    dve.wait_ge(tk.sem, tk.value(dve, b))
                    moments(1, lambda t: T[:, t, :], b)
                    normal(1, N1, lambda t: T[:, t, :], b, n1)
                    dve.wait_ge(n1.sem, n1.value(dve, b))
                    dve.tensor_tensor(tiles(), tiles(), N1[:, :, :], ALU.add).then_inc(x4.sem, 1)


_INS = ["L0_attn_x", "L0_attn_gamma", "L0_attn_beta", "L0_attn_w_ih", "L0_attn_w_hh", "L0_attn_b_ih", "L0_attn_b_hh",
        "L0_attn_w_out", "L0_attn_b_out", "L0_ffn_gate_W", "L0_ffn_gate_b", "L0_ffn_wi_W", "L0_ffn_wi_b", "L0_ffn_wo_W",
        "L0_ffn_wo_b", "L0_ffn_lora_A", "L0_ffn_lora_B", "L1_attn_W_in", "L1_attn_b_in", "L1_attn_in_ln_w",
        "L1_attn_in_ln_b", "L1_attn_W_out", "L1_attn_out_ln_w", "L1_attn_out_ln_b", "L1_attn_smear_factor",
        "L1_attn_log_scale", "L1_ffn_w_gate", "L1_ffn_w_up", "L1_ffn_w_down"]


def kernel(**inputs):
    import numpy as _np
    import concourse.bacc as _bacc
    from concourse import mybir as _mybir
    from concourse.bass_utils import run_bass_kernel_spmd as _run

    nc = _bacc.Bacc("TRN2", target_bir_lowering=False, num_devices=1)
    arrays, args = {}, []
    for name in _INS:
        a = _np.ascontiguousarray(inputs[name])
        arrays[f"in_{name}_dram"] = a
        args.append(nc.dram_tensor(f"in_{name}_dram", a.shape, _mybir.dt.from_np(a.dtype), kind="ExternalInput").ap())
    args.append(nc.dram_tensor("out_0_dram", (B, S, D), F32, kind="ExternalOutput").ap())
    build(nc, *args)
    r = _run(nc, [arrays], core_ids=[0])
    return r.results[0]["out_0_dram"]
```

```python
from contextlib import ExitStack

import concourse.bass as bass
from concourse import mybir

F32 = mybir.dt.float32
BF16 = mybir.dt.bfloat16
FP16 = mybir.dt.float16
I32 = mybir.dt.int32
U32 = mybir.dt.uint32
ALU = mybir.AluOpType
ACT = mybir.ActivationFunctionType
AX = mybir.AxisListType

P = 128
B, S, D = 8, 512, 128
NT = S // P
H = 256
HC = H // P
F, E, R = 512, 8, 4
FC = F // P
HEADS, DH = 16, 16
DE = HEADS * DH
HID = 384
NH = HID // P
EPS = 1e-5
NEG_BIG = -1e10
U = 4
NSTEP = HC * B


class Signal:

    def __init__(self, sem, per=1, credit=0):
        self.sem, self.per, self.credit = sem, per, credit

    def value(self, eng, b, k=None):
        v = b * self.per + (self.credit + (self.per if k is None else k))
        return v if isinstance(v, int) else eng.snap(v)

    def before(self, eng, b):
        return self.value(eng, b, 0)


def build(nc, x_d, gamma_d, beta_d, w_ih_d, w_hh_d, b_ih_d, b_hh_d, w_out_d, b_out_d,
          gate_w_d, gate_b_d, wi_d, wi_b_d, wo_d, wo_b_d, lora_a_d, lora_b_d,
          w_in_d, b_in_d, in_ln_w_d, in_ln_b_d, w_aout_d, out_ln_w_d, out_ln_b_d, smear_d, log_scale_d,
          w_gate_d, w_up_d, w_down_d, out_d):
    top = ExitStack()
    with top:
        def sb(ctx, name, shape, dt=F32):
            return ctx.enter_context(nc.sbuf_tensor(name, shape, dt))

        X = sb(top, "X", [P, NT * B, D])
        by_sequence = X[:, :, :].rearrange("p (t b) d -> p t b d", b=B)
        MV = sb(top, "MV", [P, B * NT, 2])
        R1 = sb(top, "R1", [P, B * NT])
        RR = sb(top, "RR", [P, B * NT])
        half = sb(top, "half", [P, B * NT])
        eps = sb(top, "eps", [P, NT])
        ident = sb(top, "ident", [P, P])
        identb = sb(top, "identb", [P, P], BF16)
        wihT = sb(top, "wihT", [P, 3 * H])
        woutT = sb(top, "woutT", [P, HC, D])
        wiT = sb(top, "wiT", [P, F])
        woT = sb(top, "woT", [P, FC, D])
        gaT = sb(top, "gaT", [P, E + E * R])
        lbT = sb(top, "lbT", [E * R, F])
        winT = sb(top, "winT", [P, 4 * DE + HEADS])
        waoT = sb(top, "waoT", [P, DE // P, D])
        wguT = sb(top, "wguT", [P, 2 * HID])
        wdT = sb(top, "wdT", [P, NH, D])
        gam = sb(top, "gam", [P, 1])
        bet = sb(top, "bet", [P, 1])
        bih = sb(top, "bih", [P, 6])
        bhh = sb(top, "bhh", [P, 6])
        wib = sb(top, "wib", [P, FC])
        bqk = sb(top, "bqk", [P, 4])
        ilw = sb(top, "ilw", [P, 1])
        ilb = sb(top, "ilb", [P, 1])
        bout = sb(top, "bout", [P, D])
        gateb = sb(top, "gateb", [P, E])
        wob = sb(top, "wob", [P, D])
        bvpy = sb(top, "bvpy", [P, 2 * DE + HEADS])
        olw = sb(top, "olw", [P, D])
        olb = sb(top, "olb", [P, D])
        iota_e = sb(top, "iota_e", [P, E, R])
        hs8 = sb(top, "hs8", [8, 6])
        qsc = sb(top, "qsc", [P, 6])
        kscale = sb(top, "kscale", [P, 4])
        S_gru = kscale[:, 2:3]
        bX = sb(top, "bX", [P, 6])
        PS = top.enter_context(nc.psum_tensor("PS", [P, 8, 512], F32))

        def signal(name, per=1, credit=0):
            return Signal(top.enter_context(nc.semaphore(name)), per, credit)

        passed = signal("passed").sem
        warmed = signal("tanh_table_loaded")

        def hold(eng, sem, value):
            eng.wait_ge(sem, value)
            eng.sem_inc(passed, 1)

        def x_moments(dve, s_t, m, st, mv, kept):
            with dve.Fori(0, NT) as k:
                for b in range(B):
                    dve.bn_stats(s_t[:, b, :], X[:, bass.ds(dve.snap(k * B + b), 1), :].rearrange("p o d -> p (o d)")).then_inc(st.sem, 1)
                hold(dve, st.sem, st.value(dve, k))
                for b in range(B):
                    dve.bn_aggr(m[:, b, :], s_t[:, b, :]).then_inc(mv.sem, 1)
                dve.wait_ge(mv.sem, mv.value(dve, k))
                dve.tensor_scalar(MV[:, bass.ds(dve.snap(k * B), B), :], m[:, :, :], 1.0, None, ALU.mult).then_inc(kept.sem, 1)

        def token_scales(pool, tmp, step, first, last, done):
            view = lambda x: x.rearrange("p (t b) -> p t b", b=B)[:, :, first:last]
            var, tmp, r1, rr, power = view(MV[:, :, 1]), view(tmp[:, :]), view(R1[:, :]), view(RR[:, :]), view(half[:, :])
            pool.tensor_scalar(tmp, var, EPS, None, ALU.add).then_inc(step, 1)
            pool.wait_ge(step, done + 1)
            pool.tensor_tensor(r1, tmp, power, ALU.pow).then_inc(step, 1)
            pool.wait_ge(step, done + 2)
            pool.tensor_tensor(tmp, r1, r1, ALU.mult).then_inc(step, 1)
            pool.wait_ge(step, done + 3)
            pool.tensor_tensor(tmp, tmp, var, ALU.mult).then_inc(step, 1)
            pool.wait_ge(step, done + 4)
            pool.tensor_scalar(tmp, tmp, EPS, None, ALU.add).then_inc(step, 1)
            pool.wait_ge(step, done + 5)
            pool.tensor_tensor(tmp, tmp, power, ALU.pow).then_inc(step, 1)
            pool.wait_ge(step, done + 6)
            pool.tensor_tensor(rr, tmp, r1, ALU.mult).then_inc(step, 1)

        gru_scope = ExitStack()
        top.enter_context(gru_scope)
        W1 = sb(gru_scope, "W1", [P, HC, 3 * H], FP16)
        W2 = sb(gru_scope, "W2", [P, HC, 3 * H], FP16)
        HS = sb(gru_scope, "HS", [P, S, HC, B])
        xi_scope = ExitStack()
        gru_scope.enter_context(xi_scope)
        XI = sb(xi_scope, "XI", [P, S + 2 * U, 6, B])

        ctx = ExitStack()
        with ctx:
            staging = HS[:, :, :, :].rearrange("p s c b -> p (s c b)")
            taken = [0]

            def stage(shape, dt=F32):
                n = 1
                for k in shape:
                    n *= k
                at = staging[:, taken[0]:taken[0] + n]
                taken[0] += n
                at = at if dt == F32 else at.bitcast(dt)
                return at if len(shape) == 1 else at.rearrange("p (c k) -> p c k", c=shape[0])
            s_ih = stage((6, D))
            s_hh = stage((6, H))
            s_out = stage((H,))
            s_wi = stage((FC, D))
            s_wo = stage((F,))
            s_lb = stage((FC, E * R))
            s_in = stage((8, D))
            s_ao = stage((DE,))
            s_gi = stage((2 * NH, D), I32)
            s_di = stage((HID,), I32)
            s_g = stage((2 * NH, D))
            s_d = stage((HID,))
            s_ga = sb(ctx, "s_ga", [E + E * R, D])
            s_iny = sb(ctx, "s_iny", [HEADS, D])
            whhT = sb(ctx, "whhT", [P, HC, 3 * H])
            mx = sb(ctx, "mx", [P, 1])
            mrow = sb(ctx, "mrow", [1, 1])
            onesr = sb(ctx, "onesr", [1, P])
            sel8 = sb(ctx, "sel8", [8, P])
            STb = sb(ctx, "STb", [P, B, 6])
            MVb = sb(ctx, "MVb", [P, B, 2])
            rt = sb(ctx, "rt", [P, B * NT])
            YN = sb(ctx, "YN", [P, NT, D])
            YT = sb(ctx, "YT", [P, S])
            warm = sb(ctx, "warm", [P, 1])

            loads_x = signal("loads_x")
            loads_gru = signal("loads_gru")
            loads_rest = signal("loads_rest")
            consts = signal("consts")
            turned = signal("weights_turned")
            kept = signal("gru_weights_kept")
            kept_rest = signal("other_weights_kept")
            casts = signal("int_weights_cast")
            sc_v = signal("scale_step_v")
            sc_p = signal("scale_step_p")
            sc_a = signal("head_scalar_exps")
            hv = signal("head_scalars_ready")
            bx = signal("input_bias_ready")
            stats = signal("x_stats", B)
            aggr = signal("x_aggr", B)
            mv_kept = signal("x_moments_kept")
            rstd = signal("x_rstd_steps")
            y_ready = signal("y_ready", NT)
            yT_ps = signal("yT_ps", 1, 1)
            yT_ready = signal("yT_ready", 1, 1)
            xi_ps = signal("xi_ps", 6, 6)
            xi_v = signal("xi_by_vector", 3, 3)
            xi_a = signal("xi_by_scalar", 3, 3)

            gru_jobs = [(s_hh[:, c, kc * P:(kc + 1) * P], whhT[:, kc, c * P:(c + 1) * P], 0.25 if c >= 4 else 0.5)
                        for c in range(6) for kc in range(HC)]
            gru_jobs += [(s_ih[:, c, :], wihT[:, c * P:(c + 1) * P], 1.0) for c in range(6)]
            jobs = [(s_out[:, c * P:(c + 1) * P], woutT[:, c, :], 0.5) for c in range(HC)]
            jobs += [(s_wi[:, c, :], wiT[:, c * P:(c + 1) * P], 1.0) for c in range(FC)]
            jobs += [(s_wo[:, c * P:(c + 1) * P], woT[:, c, :], 1.0) for c in range(FC)]
            jobs += [(s_ga[:, :], gaT[:, :], 1.0)]
            jobs += [(s_lb[:, c, :], lbT[:, c * P:(c + 1) * P], 1.0) for c in range(FC)]
            jobs += [(s_in[:, c, :], winT[:, c * P:(c + 1) * P], 1.0) for c in range(8)]
            jobs += [(s_iny[:, :], winT[:, 4 * DE:4 * DE + HEADS], 1.0)]
            jobs += [(s_ao[:, c * P:(c + 1) * P], waoT[:, c, :], 0.5) for c in range(DE // P)]
            jobs += [(s_g[:, c, :], wguT[:, c * P:(c + 1) * P], 1.0) for c in range(2 * NH)]
            jobs += [(s_d[:, c * P:(c + 1) * P], wdT[:, c, :], 0.5) for c in range(NH)]
            NG = len(gru_jobs)
            alljobs = gru_jobs + jobs
            NJ = len(alljobs)

            block = ctx.enter_context(nc.Block())

            @block.sync
            def _(sp):
                sp.dma_start(s_hh, w_hh_d.rearrange("(c p) k -> p c k", p=P)).then_inc(loads_gru.sem, 16)
                sp.dma_start(s_ih, w_ih_d.rearrange("(c p) k -> p c k", p=P)).then_inc(loads_gru.sem, 16)
                for b in range(B):
                    sp.dma_start(by_sequence[:, :, b, :],
                                 x_d[b].rearrange("(t p) d -> p t d", p=P)).then_inc(loads_x.sem, 16)
                sp.dma_start(s_out[:, :], w_out_d).then_inc(loads_rest.sem, 16)
                sp.dma_start(s_wi[:, :, :], wi_d.rearrange("(c p) k -> p c k", p=P)).then_inc(loads_rest.sem, 16)
                sp.dma_start(s_wo[:, :], wo_d).then_inc(loads_rest.sem, 16)
                sp.dma_start(s_ga[0:E, :], gate_w_d).then_inc(loads_rest.sem, 16)
                sp.dma_start(s_ga[E:E + E * R, :], lora_a_d.rearrange("e r d -> (e r) d")).then_inc(loads_rest.sem, 16)
                for c in range(FC):
                    sp.dma_start(s_lb[:, c, :].rearrange("p (e r) -> p e r", e=E),
                                 lora_b_d[:, c * P:(c + 1) * P, :].rearrange("e p r -> p e r")).then_inc(loads_rest.sem, 16)
                sp.dma_start(s_in[:, :, :], w_in_d[0:4 * DE, :].rearrange("(c p) k -> p c k", p=P)).then_inc(loads_rest.sem, 16)
                sp.dma_start(s_iny[:, :], w_in_d[4 * DE:, :]).then_inc(loads_rest.sem, 16)
                sp.dma_start(s_ao[:, :], w_aout_d).then_inc(loads_rest.sem, 16)
                sp.dma_start(s_gi[:, 0:NH, :], w_gate_d.rearrange("(c p) k -> p c k", p=P)).then_inc(loads_rest.sem, 16)
                sp.dma_start(s_gi[:, NH:, :], w_up_d.rearrange("(c p) k -> p c k", p=P)).then_inc(loads_rest.sem, 16)
                sp.dma_start(s_di[:, :], w_down_d).then_inc(loads_rest.sem, 16)

            N_REST = 11 + FC + 16

            @block.gpsimd
            def _(pool):
                pool.memset(ident[:, :], 0.0).then_inc(consts.sem, 1)
                pool.memset(half[:, :], -0.5).then_inc(consts.sem, 1)
                pool.memset(eps[:, :], EPS).then_inc(consts.sem, 1)
                pool.memset(sel8[:, :], 1.0).then_inc(consts.sem, 1)
                pool.memset(onesr[:, :], 1.0).then_inc(consts.sem, 1)
                pool.iota(iota_e[:, :, :], [[1, E], [0, R]], base=0, channel_multiplier=0,
                          allow_small_or_imprecise_dtypes=True).then_inc(consts.sem, 1)
                pool.memset(XI[:, S:, :, :], 0.0).then_inc(consts.sem, 1)
                pool.wait_ge(consts.sem, 7)
                pool.affine_select(out=ident[:, :], in_=ident[:, :], compare_op=ALU.not_equal, fill=1.0, base=0,
                                   pattern=[[-1, P]], channel_multiplier=1).then_inc(consts.sem, 1)
                pool.affine_select(out=sel8[:, :], in_=sel8[:, :], compare_op=ALU.is_ge, fill=0.0, base=0,
                                   pattern=[[1, P]], channel_multiplier=-DH).then_inc(consts.sem, 1)
                pool.wait_ge(consts.sem, 9)
                pool.tensor_copy(identb[:, :], ident[:, :]).then_inc(consts.sem, 1)
                pool.affine_select(out=sel8[:, :], in_=sel8[:, :], compare_op=ALU.is_ge, fill=0.0, base=DH - 1,
                                   pattern=[[-1, P]], channel_multiplier=DH).then_inc(consts.sem, 1)
                pool.wait_ge(loads_rest.sem, 16 * N_REST)
                pool.tensor_scalar(s_g[:, :, :], s_gi[:, :, :], 1.0 / 127.0, None, ALU.mult).then_inc(casts.sem, 1)
                pool.tensor_scalar(s_d[:, :], s_di[:, :], 1.0 / 127.0, None, ALU.mult).then_inc(casts.sem, 1)
                pool.wait_ge(mv_kept.sem, NT)
                token_scales(pool, rt, rstd.sem, 0, 1, 0)
                pool.wait_ge(rstd.sem, 7)
                token_scales(pool, rt, rstd.sem, 1, B, 7)

            @block.tensor
            def _(pe):
                def turn(i):
                    src, dst, _ = alljobs[i]
                    k, m = src.shape[0], src.shape[1]
                    if 8 <= i < NG + 8:
                        pe.wait_ge(kept.sem, i - 7)
                    if i >= NG + 8:
                        pe.wait_ge(kept_rest.sem, i - 7 - NG)
                    pe.transpose(PS[0:m, i % 8, 0:k], src, ident[0:k, 0:k]).then_inc(turned.sem, 1)
                pe.wait_ge(consts.sem, 11)
                pe.wait_ge(loads_gru.sem, 32)
                for i in range(NG):
                    turn(i)
                pe.wait_ge(kept.sem, NG)
                pe.wait_ge(sc_v.sem, 1)
                pe.transpose(PS[0:1, 0, 0:P], mx[:, :], ident[:, :]).then_inc(sc_p.sem, 1)
                pe.wait_ge(sc_v.sem, 4)
                pe.matmul(PS[:, 1, 0:1], onesr[:, :], mrow[:, :], start=True, stop=True).then_inc(sc_p.sem, 1)
                pe.wait_ge(sc_v.sem, 6)
                pe.wait_ge(loads_rest.sem, 16 * N_REST)
                pe.wait_ge(casts.sem, 2)
                for i in range(NG, NJ):
                    turn(i)
                pe.wait_ge(kept_rest.sem, NJ - NG)
                pe.wait_ge(hv.sem, 3)
                pe.matmul(PS[:, 2, 0:6], sel8[:, :], hs8[:, :], start=True, stop=True).then_inc(sc_p.sem, 1)
                pe.wait_ge(sc_v.sem, 12)
                pe.sem_inc(yT_ps.sem, yT_ps.credit)
                pe.sem_inc(xi_ps.sem, xi_ps.credit)

                def turn_y(b):
                    pe.wait_ge(y_ready.sem, y_ready.value(pe, b))
                    pe.wait_ge(yT_ready.sem, yT_ready.before(pe, b))
                    for t in range(NT):
                        last = pe.transpose(PS[:, 0, t * P:(t + 1) * P], YN[:, t, :], ident[:, :])
                    last.then_inc(yT_ps.sem, 1)

                def product(b, c):
                    if c == 0:
                        pe.wait_ge(yT_ready.sem, yT_ready.value(pe, b))
                    done = xi_v if c % 2 else xi_a
                    pe.wait_ge(done.sem, b * 3 + (c // 2 + 1) if isinstance(b, int) else pe.snap(b * 3 + (c // 2 + 1)))
                    pe.matmul(PS[:, 1 + c, :], wihT[:, c * P:(c + 1) * P], YT[:, :], start=True, stop=True).then_inc(xi_ps.sem, 1)
                turn_y(0)
                with pe.Fori(0, B - 1) as b:
                    for c in range(6):
                        product(b, c)
                        if c == 2:
                            turn_y(pe.snap(b + 1))
                for c in range(6):
                    product(B - 1, c)

            @block.scalar
            def _(act):
                def col(dst, src, c):
                    act.dma_start(dst, src.rearrange("(c p) -> p c", c=c),
                                   allow_slow_non_contiguous=True).then_inc(loads_rest.sem, 16)

                def row(dst, src):
                    act.dma_start(dst, src.partition_broadcast(P)).then_inc(loads_rest.sem, 16)
                col(gam[:, :], gamma_d, 1)
                col(bet[:, :], beta_d, 1)
                col(bih[:, :], b_ih_d, 6)
                col(bhh[:, :], b_hh_d, 6)
                col(wib[:, :], wi_b_d, FC)
                col(bqk[:, :], b_in_d[0:2 * DE], 4)
                col(ilw[:, :], in_ln_w_d, 1)
                col(ilb[:, :], in_ln_b_d, 1)
                row(bout[:, :], b_out_d)
                row(gateb[:, :], gate_b_d)
                row(wob[:, :], wo_b_d)
                row(bvpy[:, :], b_in_d[2 * DE:])
                row(olw[:, :], out_ln_w_d)
                row(olb[:, :], out_ln_b_d)
                act.dma_start(hs8[:, 0:2], smear_d.rearrange("(c h) -> h c", c=2),
                               allow_slow_non_contiguous=True).then_inc(loads_rest.sem, 16)
                act.dma_start(hs8[:, 2:4], log_scale_d.rearrange("(c h) -> h c", c=2),
                               allow_slow_non_contiguous=True).then_inc(loads_rest.sem, 16)
                act.wait_ge(consts.sem, 11)
                act.activation(warm[:, :], half[:, 0:1], ACT.Tanh).then_inc(sc_a.sem, 1)
                act.wait_ge(loads_rest.sem, 16 * N_REST)
                act.activation(hs8[:, 4:6], hs8[:, 2:4], ACT.Exp, scale=-2.0).then_inc(sc_a.sem, 1)
                act.wait_ge(sc_a.sem, 2)
                act.activation(hs8[:, 2:4], hs8[:, 0:2], ACT.Exp, scale=-1.0).then_inc(sc_a.sem, 1)
                act.wait_ge(sc_a.sem, 3)
                act.activation(hs8[:, 0:2], hs8[:, 0:2], ACT.Exp).then_inc(sc_a.sem, 1)
                for i in range(NG, NJ):
                    src, dst, f = alljobs[i]
                    act.wait_ge(turned.sem, i + 1)
                    act.activation(dst, PS[0:src.shape[1], i % 8, 0:src.shape[0]], ACT.Copy, scale=f).then_inc(kept_rest.sem, 1)
                for s in (yT_ready, xi_a):
                    act.sem_inc(s.sem, s.credit)
                act.wait_ge(bx.sem, 1)
                with act.Fori(0, B) as b:
                    act.wait_ge(yT_ps.sem, yT_ps.value(act, b))
                    act.wait_ge(xi_ps.sem, xi_ps.before(act, b))
                    act.activation(YT[:, :], PS[:, 0, :], ACT.Identity, scale=gam[:, 0:1],
                                   bias=bet[:, 0:1]).then_inc(yT_ready.sem, 1)
                    for c in (0, 2, 4):
                        act.wait_ge(xi_ps.sem, xi_ps.value(act, b, c + 1))
                        act.activation(XI[:, 0:S, c, bass.ds(b, 1)].rearrange("p s o -> p (s o)"), PS[:, 1 + c, :], ACT.Identity,
                                       scale=S_gru, bias=bX[:, c:c + 1]).then_inc(xi_a.sem, 1)

            @block.vector
            def _(dve):
                def keep(i):
                    src, dst, f = alljobs[i]
                    dve.wait_ge(turned.sem, i + 1)
                    dve.tensor_scalar(dst, PS[0:src.shape[1], i % 8, 0:src.shape[0]], f, None,
                                      ALU.mult).then_inc(kept.sem, 1)
                for i in range(NG):
                    keep(i)
                dve.wait_ge(kept.sem, NG)
                dve.tensor_reduce(mx[:, :], whhT[:, :, :].rearrange("p a b -> p (a b)"), AX.X, ALU.max,
                                  apply_absolute_value=True).then_inc(sc_v.sem, 1)
                dve.wait_ge(sc_p.sem, 1)
                dve.tensor_reduce(mrow[:, :], PS[0:1, 0, 0:P], AX.X, ALU.max).then_inc(sc_v.sem, 1)
                dve.wait_ge(sc_v.sem, 2)
                dve.tensor_scalar(mrow[:, :], mrow[:, :], 2.0 ** -60, None, ALU.max).then_inc(sc_v.sem, 1)
                dve.wait_ge(sc_v.sem, 3)
                dve.tensor_scalar(mrow[:, :].bitcast(I32), mrow[:, :].bitcast(I32), 0x7f800000, None,
                                  ALU.bitwise_and).then_inc(sc_v.sem, 1)
                dve.wait_ge(sc_p.sem, 2)
                dve.tensor_scalar(kscale[:, 0:1], PS[:, 1, 0:1], 2.0 ** -15, None, ALU.mult).then_inc(sc_v.sem, 1)
                dve.tensor_scalar(kscale[:, 1:2], PS[:, 1, 0:1], 2.0 ** -14, None, ALU.mult).then_inc(sc_v.sem, 1)
                dve.wait_ge(sc_v.sem, 6)
                dve.reciprocal(kscale[:, 2:3], kscale[:, 1:2]).then_inc(sc_v.sem, 1)
                dve.wait_ge(sc_v.sem, 7)
                flat = lambda w: w[:, :, :].rearrange("p a b -> p (a b)")
                dve.tensor_scalar(flat(whhT), flat(whhT), S_gru, None, ALU.mult).then_inc(sc_v.sem, 1)
                dve.wait_ge(sc_v.sem, 8)
                dve.tensor_copy(flat(W1), flat(whhT)).then_inc(sc_v.sem, 1)
                dve.wait_ge(sc_v.sem, 9)
                dve.tensor_tensor(flat(W2), flat(whhT), flat(W1), ALU.subtract).then_inc(sc_v.sem, 1)
                dve.wait_ge(loads_x.sem, 16 * B)
                x_moments(dve, STb, MVb, stats, aggr, mv_kept)
                dve.wait_ge(sc_a.sem, 4)
                dve.tensor_scalar(hs8[:, 0:4], hs8[:, 0:4], 1.0, None, ALU.add).then_inc(hv.sem, 1)
                dve.tensor_scalar(hs8[:, 4:6], hs8[:, 4:6], float(DH) ** -0.5, None, ALU.mult).then_inc(hv.sem, 1)
                dve.wait_ge(hv.sem, 2)
                dve.reciprocal(hs8[:, 0:4], hs8[:, 0:4]).then_inc(hv.sem, 1)
                dve.wait_ge(sc_p.sem, 3)
                dve.tensor_copy(qsc[:, :], PS[:, 2, 0:6]).then_inc(sc_v.sem, 1)
                dve.tensor_tensor(bih[:, 0:4], bih[:, 0:4], bhh[:, 0:4], ALU.add).then_inc(sc_v.sem, 1)
                dve.wait_ge(sc_v.sem, 12)
                dve.tensor_scalar(bX[:, :], bih[:, :], S_gru, None, ALU.mult).then_inc(bx.sem, 1)
                dve.wait_ge(rstd.sem, 7)
                dve.wait_ge(bx.sem, 1)
                dve.sem_inc(xi_v.sem, xi_v.credit)

                def normal_y(b):
                    dve.wait_ge(yT_ps.sem, yT_ps.before(dve, b))
                    for t in range(NT):
                        at = slice(t * B + b, t * B + b + 1) if isinstance(b, int) else bass.ds(dve.snap(b + t * B), 1)
                        dve.tensor_scalar(YN[:, t, :], X[:, at, :].rearrange("p o d -> p (o d)"),
                                          MV[:, at, 0:1].rearrange("p o k -> p (o k)"), RR[:, at],
                                          ALU.subtract, ALU.mult).then_inc(y_ready.sem, 1)

                def keep_products(b):
                    for c in (1, 3, 5):
                        dve.wait_ge(xi_ps.sem, xi_ps.value(dve, b, c + 1))
                        one = slice(b, b + 1) if isinstance(b, int) else bass.ds(b, 1)
                        dve.tensor_scalar(XI[:, 0:S, c, one].rearrange("p s o -> p (s o)"), PS[:, 1 + c, :], S_gru,
                                          bX[:, c:c + 1], ALU.mult, ALU.add).then_inc(xi_v.sem, 1)
                normal_y(0)
                dve.wait_ge(rstd.sem, 14)
                with dve.Fori(0, B - 1) as b:
                    normal_y(dve.snap(b + 1))
                    keep_products(b)
                keep_products(B - 1)

        SLOTS = P // B
        ctx = ExitStack()
        with ctx:
            bh = sb(ctx, "bh", [P, U, NSTEP])
            XS = sb(ctx, "XS", [P, 2, U, 6, B])
            HR = sb(ctx, "HR", [P, 2, U, NSTEP])
            G1 = sb(ctx, "G1", [P, HC, B], FP16)
            G2 = sb(ctx, "G2", [P, HC, B], FP16)
            tr = sb(ctx, "tr", [P, NSTEP])
            tz = sb(ctx, "tz", [P, NSTEP])
            u_ = sb(ctx, "u_", [P, NSTEP])
            v_ = sb(ctx, "v_", [P, NSTEP])
            n_ = sb(ctx, "n_", [P, NSTEP])
            zg = sb(ctx, "zg", [P, NSTEP])
            zn = sb(ctx, "zn", [P, NSTEP])
            warm = sb(ctx, "warm2", [P, 1])
            free = sb(ctx, "free", [P, 2])
            pR = PS[:, 0:2, :]
            pZ = PS[:, 2:4, :]
            pN = PS[:, 4:6, :]

            xs_in = [signal(f"xs_in{p}") for p in range(2)]
            hr_out = [signal(f"hr_out{p}") for p in range(2)]
            bh_start = signal("bh_start")
            bh_ready = signal("bh_ready")
            injected = signal("injected")
            r_ps = signal("r_ps")
            hn_tr = signal("hn_ps_and_tr")
            z_ps = signal("z_ps")
            tz_ready = signal("tz_ready")
            u_ready = signal("u_ready")
            v_ready = signal("v_ready")
            n_ready = signal("n_ready")
            zg_ready = signal("zg_ready")
            zn_ready = signal("zn_ready")
            g1_ready = signal("g1_ready")
            g_ready = signal("g_ready")
            g2_ready = signal("g2_ready")

            HB = sb(ctx, "HB", [P, HC, P])
            X0 = sb(ctx, "X0", [P, D])
            X0b = sb(ctx, "X0b", [P, D])
            T = sb(ctx, "T", [P, D])
            N1 = sb(ctx, "N1", [P, D])
            XF = sb(ctx, "XF", [P, D])
            XFT = sb(ctx, "XFT", [P, P])
            LG = sb(ctx, "LG", [P, E])
            LM = sb(ctx, "LM", [P, 8])
            LI = sb(ctx, "LI", [P, 8], U32)
            LF = sb(ctx, "LF", [P, 1])
            LA = sb(ctx, "LA", [P, E * R])
            ML = sb(ctx, "ML", [P, E * R])
            LAT = sb(ctx, "LAT", [E * R, P])
            INT = sb(ctx, "INT", [P, FC, P])
            T2 = sb(ctx, "T2", [P, D])
            N2 = sb(ctx, "N2", [P, D])
            sets = []
            for i in range(3):
                sets.append((sb(ctx, f"st{i}", [P, 6]), sb(ctx, f"mv{i}", [P, 2]),
                             sb(ctx, f"rt{i}", [P, 1]), sb(ctx, f"rs{i}", [P, 1])))
            p_gy = PS[:, 6, 0:D]
            p_xfT = PS[:, 7, 0:P]
            p_ga = PS[:, 7, 0:E + E * R]
            p_laT = PS[0:E * R, 6, 0:P]
            p_base = [PS[:, 6 if c == 2 else 7, 0:P] for c in range(FC)]
            p_dn = PS[:, 6, 0:D]

            hb = signal("hb_copied", HC)
            x0 = signal("x0_ready")
            x0b = signal("x0b_ready")
            gy = signal("gru_out_ps")
            t_sum = signal("gru_sum_ready")
            st = [signal(f"c_stats{i}") for i in range(3)]
            mv = [signal(f"c_moments{i}") for i in range(3)]
            rs = [signal(f"c_scale{i}", 2) for i in range(3)]
            nn = signal("n1_ready")
            x1 = signal("x1_ready")
            xf = signal("xf_ready")
            xfT_ps = signal("xfT_ps")
            xfT = signal("xfT_ready")
            ga = signal("gate_lora_ps")
            lg = signal("logits_ready", 2)
            lm = signal("logit_max_ready")
            li = signal("expert_index_ready")
            lf = signal("expert_number_ready")
            ml = signal("masked_lora_ready")
            laT_ps = signal("loraT_ps")
            laT = signal("loraT_ready")
            base = signal("base_ps", FC)
            inter = signal("inter_ready", FC)
            dn = signal("ffn_out_ps")
            t2 = signal("ffn_sum_ready")
            n2 = signal("n2_ready")

            def schedule(eng, steps, early, late):
                def value(v):
                    return v if isinstance(v, int) else eng.snap(v)

                def unit(k, b, before, scan=True):
                    u = value(k * B + b)
                    for s in range(SLOTS):
                        if scan and steps:
                            steps(value(u * SLOTS + (P + s // (2 * U) * (2 * U))), s % (2 * U))
                        early(u, k, b, s)
                        if before:
                            late(value(u - 1), s)
                if steps:
                    with eng.Fori(0, P // (2 * U)) as q:
                        for j in range(2 * U):
                            steps(eng.snap(q * (2 * U)), j)
                unit(0, 0, False)
                with eng.Fori(0, B - 1) as b:
                    unit(0, value(b + 1), True)
                with eng.Fori(0, NT - 2) as k:
                    with eng.Fori(0, B) as b:
                        unit(value(k + 1), b, True)
                with eng.Fori(0, B) as b:
                    unit(NT - 1, b, True, False)
                for s in range(SLOTS):
                    late(NT * B - 1, s)

            block = ctx.enter_context(nc.Block())

            @block.sync
            def _(sp):
                for p in range(2):
                    sp.dma_start(XS[:, p], XI[:, p * U:(p + 1) * U]).then_inc(xs_in[p].sem, 16)
                with sp.Fori(0, S // (2 * U)) as q:
                    for p in range(2):
                        sp.wait_ge(g_ready.sem, sp.snap(q * (2 * U) + U * (p + 1)))
                        at = sp.snap(q * (2 * U) + U * p)
                        sp.dma_start(HS[:, bass.ds(at, U)].rearrange("p u c b -> p u (c b)"),
                                     HR[:, p]).then_inc(hr_out[p].sem, 16)
                        sp.dma_start(XS[:, p], XI[:, bass.ds(sp.snap(q * (2 * U) + U * (p + 2)), U)]).then_inc(xs_in[p].sem, 16)
                for p in range(2):
                    sp.wait_ge(hr_out[p].sem, 16 * (S // (2 * U) + 1))
                    sp.wait_ge(xs_in[p].sem, 16 * (S // (2 * U) + 1))

            @block.gpsimd
            def _(pool):
                def scale(u, i):
                    _, m, r_t, r_s = sets[i]
                    pool.wait_ge(mv[i].sem, mv[i].value(pool, u))
                    pool.tensor_tensor(r_t[:, :], m[:, 1:2], eps[:, 0:1], ALU.add).then_inc(rs[i].sem, 1)
                    pool.wait_ge(rs[i].sem, rs[i].value(pool, u, 1))
                    pool.tensor_tensor(r_s[:, :], r_t[:, :], half[:, 0:1], ALU.pow).then_inc(rs[i].sem, 1)

                def early(u, k, b, s):
                    if s == 0:
                        pool.wait_ge(x0.sem, x0.value(pool, u))
                        pool.tensor_tensor(X0b[:, :], X0[:, :], bout[:, :], ALU.add).then_inc(x0b.sem, 1)
                    if s == 4:
                        scale(u, 0)
                    if s == 8:
                        scale(u, 1)

                def late(u, s):
                    if s == 14:
                        scale(u, 2)
                schedule(pool, None, early, late)

            @block.tensor
            def _(pe):
                gates = {"r": (pR, 0), "z": (pZ, 1), "n": (pN, 2)}
                by_g1 = [(mc, kc, W) for mc in range(HC) for kc in range(HC) for W in (W1, W2)]
                by_g2 = [(mc, kc, W1) for mc in range(HC) for kc in range(HC)]

                def product(gate, p, k, mc, kc, W, G):
                    bank, g = gates[gate]
                    w = (HC * g + mc) * P
                    o = NSTEP * k + B * mc
                    return pe.matmul(bank[:, p, o:o + B], W[:, kc, w:w + P], G[:, kc, :],
                                     start=False, stop=True, skip_group_check=True)

                def inject(gate, p):
                    src = {"r": XS[:, p, :, 0:2, :], "z": XS[:, p, :, 2:4, :], "n": bh[:, :, :]}[gate]
                    return pe.matmul(gates[gate][0][:, p, 0:U * NSTEP], ident[:, :], src,
                                     start=True, stop=False, skip_group_check=True)
                pe.wait_ge(bh_ready.sem, 2)
                pe.wait_ge(xs_in[0].sem, 16)
                for gate in "rnz":
                    inject(gate, 0)

                def steps(first, j):
                    p, k = j // U, j % U
                    n = first + (j + 1) if isinstance(first, int) else pe.snap(first + (j + 1))
                    pe.wait_ge(g1_ready.sem, n)
                    for w in by_g1:
                        product("r", p, k, *w, G1)
                    for w in by_g1[:3]:
                        product("n", p, k, *w, G1)
                    pe.wait_ge(g2_ready.sem, n)
                    for w in by_g2:
                        last = product("r", p, k, *w, G2)
                    last.then_inc(r_ps.sem, 1)
                    for w in by_g1[3:]:
                        product("n", p, k, *w, G1)
                    for w in by_g2:
                        last = product("n", p, k, *w, G2)
                    last.then_inc(hn_tr.sem, 1)
                    for w in by_g1:
                        product("z", p, k, *w, G1)
                    for w in by_g2:
                        last = product("z", p, k, *w, G2)
                    last.then_inc(z_ps.sem, 1)
                    if k == 1:
                        ready = first * 2 + 16 * (p + 1)
                        pe.wait_ge(xs_in[1 - p].sem, ready if isinstance(first, int) else pe.snap(ready))
                    if 1 <= k <= 3:
                        inject("rnz"[k - 1], 1 - p).then_inc(injected.sem, 1)

                def early(u, k, b, s):
                    if s == 2:
                        if not isinstance(u, int):
                            pe.wait_ge(laT.sem, laT.before(pe, u))
                        pe.wait_ge(hb.sem, hb.value(pe, u))
                        pe.matmul(p_gy, HB[:, 0, :], woutT[:, 0, :], start=True, stop=False)
                    if s == 3:
                        pe.matmul(p_gy, HB[:, 1, :], woutT[:, 1, :], start=False, stop=True).then_inc(gy.sem, 1)
                    if s == 5:
                        pe.wait_ge(t_sum.sem, t_sum.value(pe, u))
                    if s == 10:
                        if not isinstance(u, int):
                            pe.wait_ge(inter.sem, inter.before(pe, u))
                        pe.wait_ge(xf.sem, xf.value(pe, u))
                        pe.transpose(p_xfT, XF[:, :], ident[:, :]).then_inc(xfT_ps.sem, 1)
                    if s == 12:
                        pe.wait_ge(xfT.sem, xfT.value(pe, u))
                        pe.matmul(p_ga, XFT[:, :], gaT[:, :], start=True, stop=True).then_inc(ga.sem, 1)
                    if s == 15:
                        pe.wait_ge(ml.sem, ml.value(pe, u))
                        pe.transpose(p_laT, ML[:, :], ident[:, :]).then_inc(laT_ps.sem, 1)

                def late(u, s):
                    for c in {0: (0,), 4: (1,), 5: (2,), 7: (3,)}.get(s, ()):
                        if c in (1, 3):
                            pe.wait_ge(inter.sem, inter.value(pe, u, 1 + c // 2))
                        pe.matmul(p_base[c], wiT[:, c * P:(c + 1) * P], XFT[:, :], start=True, stop=False)
                    for c in {1: (0,), 4: (1,), 6: (2,), 8: (3,)}.get(s, ()):
                        if c == 0:
                            pe.wait_ge(laT.sem, laT.value(pe, u))
                        pe.matmul(p_base[c], lbT[:, c * P:(c + 1) * P], LAT[:, :], start=False, stop=True).then_inc(base.sem, 1)
                    for c in {8: (0,), 9: (1,), 11: (2,), 12: (3,)}.get(s, ()):
                        if c == 0:
                            pe.wait_ge(inter.sem, inter.value(pe, u, 3))
                        if c == 3:
                            pe.wait_ge(inter.sem, inter.value(pe, u))
                        last = pe.matmul(p_dn, INT[:, c, :], woT[:, c, :], start=(c == 0), stop=(c == FC - 1))
                        if c == FC - 1:
                            last.then_inc(dn.sem, 1)
                schedule(pe, steps, early, late)

            @block.scalar
            def _(act):
                act.activation(warm[:, :], half[:, 0:1], ACT.Tanh).then_inc(warmed.sem, 1)
                gate_scale = act.alloc_register("gate_scale")
                n_scale = act.alloc_register("n_scale")
                act.load(gate_scale, kscale[0:1, 0:1].bitcast(I32))
                act.load(n_scale, kscale[0:1, 1:2].bitcast(I32))

                def steps(first, j):
                    p, k = j // U, j % U
                    n = first + (j + 1) if isinstance(first, int) else act.snap(first + (j + 1))
                    o = NSTEP * k
                    act.wait_ge(r_ps.sem, n)
                    act.activation(tr[:, :], pR[:, p, o:o + NSTEP], ACT.Tanh, scale=gate_scale).then_inc(hn_tr.sem, 1)
                    act.wait_ge(z_ps.sem, n)
                    act.activation(tz[:, :], pZ[:, p, o:o + NSTEP], ACT.Tanh, scale=gate_scale).then_inc(tz_ready.sem, 1)
                    act.wait_ge(v_ready.sem, n)
                    act.activation(n_[:, :], v_[:, :], ACT.Tanh, scale=n_scale).then_inc(n_ready.sem, 1)

                def early(u, k, b, s):
                    if s == 1:
                        states = k * (16 * P // (2 * U)) + 16 * (P // (2 * U) + 1)
                        for p in range(2):
                            act.wait_ge(hr_out[p].sem, states if isinstance(k, int) else act.snap(states))
                        if not isinstance(u, int):
                            act.wait_ge(gy.sem, gy.before(act, u))
                        rows = slice(k * P, (k + 1) * P) if isinstance(k, int) else bass.ds(act.snap(k * P), P)
                        one = slice(b, b + 1) if isinstance(b, int) else bass.ds(b, 1)
                        for c in range(HC):
                            act.activation(HB[:, c, :], HS[:, rows, c, one].rearrange("p s o -> p (s o)"),
                                           ACT.Copy).then_inc(hb.sem, 1)
                    if s == 11:
                        act.wait_ge(xfT_ps.sem, xfT_ps.value(act, u))
                        act.activation(XFT[:, :], p_xfT, ACT.Copy).then_inc(xfT.sem, 1)

                def late(u, s):
                    if s == 0:
                        act.wait_ge(laT_ps.sem, laT_ps.value(act, u))
                        act.activation(LAT[:, :], p_laT, ACT.Copy).then_inc(laT.sem, 1)
                    for c in {2: (0,), 5: (1,), 7: (2,), 9: (3,)}.get(s, ()):
                        act.wait_ge(base.sem, base.value(act, u, c + 1))
                        act.activation(INT[:, c, :], p_base[c], ACT.Relu, bias=wib[:, c:c + 1]).then_inc(inter.sem, 1)
                schedule(act, steps, early, late)

            @block.vector
            def _(dve):
                dve.memset(bh[:, :, :], 0.0).then_inc(bh_start.sem, 1)
                dve.memset(HR[:, :, :, :], 0.0).then_inc(bh_start.sem, 1)
                dve.memset(G1[:, :, :], 0.0).then_inc(g1_ready.sem, 1)
                dve.memset(G2[:, :, :], 0.0).then_inc(g2_ready.sem, 1)
                dve.tensor_scalar(bhh[:, 4:6], bhh[:, 4:6], S_gru, 0.5, ALU.mult, ALU.mult).then_inc(bh_start.sem, 1)
                dve.wait_ge(bh_start.sem, 3)
                for c in range(HC):
                    x = bh[:, :, c * B:(c + 1) * B]
                    dve.tensor_scalar(x, x, bhh[:, 4 + c:5 + c], None, ALU.add).then_inc(bh_ready.sem, 1)
                for p in range(2):
                    dve.memset(free[:, p:p + 1], 0.0).then_inc(hr_out[p].sem, 16)
                flat = lambda g: g[:, :, :].rearrange("p c b -> p (c b)")

                def steps(first, j):
                    p, k = j // U, j % U
                    n = first + (j + 1) if isinstance(first, int) else dve.snap(first + (j + 1))
                    n2 = (first + (j + 1)) * 2 if isinstance(first, int) else dve.snap(first * 2 + 2 * (j + 1))
                    o = NSTEP * k
                    before = HR[:, p, k - 1, :] if k else HR[:, 1 - p, U - 1, :]
                    dve.wait_ge(hn_tr.sem, n2)
                    dve.scalar_tensor_tensor(u_[:, :], tr[:, :], 1.0, pN[:, p, o:o + NSTEP],
                                             ALU.add, ALU.mult).then_inc(u_ready.sem, 1)
                    dve.wait_ge(u_ready.sem, n)
                    dve.tensor_tensor(v_[:, :], u_[:, :], XS[:, p, k, 4:6, :].rearrange("p c b -> p (c b)"),
                                      ALU.add).then_inc(v_ready.sem, 1)
                    dve.wait_ge(tz_ready.sem, n)
                    dve.scalar_tensor_tensor(zg[:, :], tz[:, :], 1.0, before, ALU.add, ALU.mult).then_inc(zg_ready.sem, 1)
                    dve.wait_ge(n_ready.sem, n)
                    dve.scalar_tensor_tensor(zn[:, :], tz[:, :], 1.0, n_[:, :], ALU.subtract, ALU.mult).then_inc(zn_ready.sem, 1)
                    dve.wait_ge(zn_ready.sem, n)
                    dve.scalar_tensor_tensor(flat(G1), zg[:, :], 0.5, zn[:, :], ALU.mult, ALU.subtract).then_inc(g1_ready.sem, 1)
                    if k == 0:
                        gone = first * 2 + 16
                        dve.wait_ge(hr_out[p].sem, gone if isinstance(first, int) else dve.snap(gone))
                    dve.scalar_tensor_tensor(HR[:, p, k, :], zg[:, :], 0.5, zn[:, :], ALU.mult, ALU.subtract).then_inc(g_ready.sem, 1)
                    dve.wait_ge(g_ready.sem, n)
                    dve.tensor_tensor(flat(G2), HR[:, p, k, :], flat(G1), ALU.subtract).then_inc(g2_ready.sem, 1)

                def at(u):
                    return slice(u, u + 1) if isinstance(u, int) else bass.ds(u, 1)

                def tile(u):
                    return X[:, at(u), :].rearrange("p o d -> p (o d)")

                def stats(u, i, src):
                    dve.bn_stats(sets[i][0][:, :], src).then_inc(st[i].sem, 1)

                def aggregate(u, i):
                    s_t, m, _, _ = sets[i]
                    hold(dve, st[i].sem, st[i].value(dve, u))
                    dve.bn_aggr(m[:, :], s_t[:, :]).then_inc(mv[i].sem, 1)

                def normal(u, i, dst, src, done):
                    _, m, _, r_s = sets[i]
                    dve.wait_ge(rs[i].sem, rs[i].value(dve, u))
                    dve.tensor_scalar(dst[:, :], src, m[:, 0:1], r_s[:, 0:1], ALU.subtract, ALU.mult).then_inc(done.sem, 1)

                def early(u, k, b, s):
                    if s == 0:
                        dve.tensor_scalar(X0[:, :], tile(u), MV[:, at(u), 0:1].rearrange("p o k -> p (o k)"), R1[:, at(u)],
                                          ALU.subtract, ALU.mult).then_inc(x0.sem, 1)
                    if s == 3:
                        dve.wait_ge(x0b.sem, x0b.value(dve, u))
                        dve.wait_ge(gy.sem, gy.value(dve, u))
                        dve.tensor_tensor(T[:, :], X0b[:, :], p_gy, ALU.add).then_inc(t_sum.sem, 1)
                    if s == 4:
                        dve.wait_ge(t_sum.sem, t_sum.value(dve, u))
                        stats(u, 0, T[:, :])
                        aggregate(u, 0)
                    if s == 6:
                        normal(u, 0, N1, T[:, :], nn)
                        dve.wait_ge(nn.sem, nn.value(dve, u))
                        dve.tensor_tensor(tile(u), tile(u), N1[:, :], ALU.add).then_inc(x1.sem, 1)
                    if s == 7:
                        hold(dve, x1.sem, x1.value(dve, u))
                        stats(u, 1, tile(u))
                    if s == 8:
                        aggregate(u, 1)
                    if s == 9:
                        normal(u, 1, XF, tile(u), xf)
                    if s == 12:
                        dve.wait_ge(ga.sem, ga.value(dve, u))
                        dve.tensor_tensor(LG[:, :], p_ga[:, 0:E], gateb[:, :], ALU.add).then_inc(lg.sem, 1)
                        dve.tensor_copy(LA[:, :], p_ga[:, E:]).then_inc(lg.sem, 1)
                    if s == 13:
                        hold(dve, lg.sem, lg.value(dve, u))
                        dve.max(LM[:, :], LG[:, :]).then_inc(lm.sem, 1)
                        hold(dve, lm.sem, lm.value(dve, u))
                        dve.max_index(LI[:, :], LM[:, :], LG[:, :]).then_inc(li.sem, 1)
                    if s == 14:
                        dve.wait_ge(li.sem, li.value(dve, u))
                        dve.tensor_copy(LF[:, :], LI[:, 0:1]).then_inc(lf.sem, 1)
                        dve.wait_ge(lf.sem, lf.value(dve, u))
                        dve.scalar_tensor_tensor(ML[:, :], iota_e[:, :, :].rearrange("p e r -> p (e r)"), LF[:, 0:1],
                                                 LA[:, :], ALU.is_equal, ALU.mult).then_inc(ml.sem, 1)

                def late(u, s):
                    if s == 12:
                        dve.wait_ge(dn.sem, dn.value(dve, u))
                        dve.tensor_tensor(T2[:, :], p_dn, wob[:, :], ALU.add).then_inc(t2.sem, 1)
                    if s == 13:
                        dve.wait_ge(t2.sem, t2.value(dve, u))
                        stats(u, 2, T2[:, :])
                    if s == 14:
                        aggregate(u, 2)
                    if s == 15:
                        normal(u, 2, N2, T2[:, :], n2)
                        dve.wait_ge(n2.sem, n2.value(dve, u))
                        dve.tensor_tensor(tile(u), tile(u), N2[:, :], ALU.add)
                schedule(dve, steps, early, late)
        xi_scope.close()

        def layer_norm_scale(eng, mv, rt, rs, step, b, k):
            eng.tensor_tensor(rt[:, :], mv[:, :, 1], eps[:, :], ALU.add).then_inc(step.sem, 1)
            eng.wait_ge(step.sem, step.value(eng, b, k + 1))
            eng.tensor_tensor(rs[:, :], rt[:, :], half[:, 0:NT], ALU.pow).then_inc(step.sem, 1)

        gru_scope.close()

        KM, KF = 99, 102
        NG4 = HEADS // 4
        ctx = ExitStack()
        with ctx:
            qd = nc.dram_tensor("q_parts", (B, 3, DE, S), BF16).ap()
            kd = nc.dram_tensor("k_parts", (B, 3, DE, S), BF16).ap()
            ad = nc.dram_tensor("k_extra", (B, HEADS * 6, S), BF16).ap()
            QS = sb(ctx, "QS", [KF, 2, HEADS, S], BF16)
            KS = sb(ctx, "KS", [KF, 2, HEADS, S], BF16)
            VV = sb(ctx, "VV", [P, 2, NT, HEADS, 32])
            SP = sb(ctx, "SP", [P, 2, NT, DE])
            PT = sb(ctx, "PT", [P, 2, 4, S])
            XN = sb(ctx, "XN", [P, NT, D])
            XT = sb(ctx, "XT", [P, S])
            QF = sb(ctx, "QF", [P, 2, S])
            KF_ = sb(ctx, "KF_", [P, 2, S])
            KK = sb(ctx, "KK", [P, 2, S])
            PQ = sb(ctx, "PQ", [P, 2, 3, S], BF16)
            PK = sb(ctx, "PK", [P, 2, 3, S], BF16)
            RES = sb(ctx, "RES", [P, 2, S])
            YB = sb(ctx, "YB", [P, NT, HEADS])
            SG = sb(ctx, "SG", [P, NT, HEADS])
            PR = sb(ctx, "PR", [P, NT, HEADS])
            KA = sb(ctx, "KA", [P, NT, HEADS, 6], BF16)
            KAT = sb(ctx, "KAT", [HEADS * 6, S], BF16)
            PB = sb(ctx, "PB", [P, 2, DE])
            TH = sb(ctx, "TH", [P, 2, DE])
            MX = sb(ctx, "MX", [P, 4, NT])
            MR = sb(ctx, "MR", [P, 4, NT])
            QA = sb(ctx, "QA", [P, 4, NT, 6], BF16)
            OT = sb(ctx, "OT", [P, S])
            RS_ = sb(ctx, "RS_", [P, NT, 4])
            ON = sb(ctx, "ON", [P, NT, HEADS, DH])
            GT = sb(ctx, "GT", [P, 2, S])
            T = sb(ctx, "T_a", [P, NT, D])
            N1 = sb(ctx, "N1_a", [P, NT, D])
            STa = sb(ctx, "STa", [P, B, 6])
            MVa = sb(ctx, "MVa", [P, B, 2])
            rta = sb(ctx, "rta", [P, B * NT])
            sets = []
            for i in range(2):
                sets.append((sb(ctx, f"sta{i}", [P, NT, 6]), sb(ctx, f"mva{i}", [P, NT, 2]),
                             sb(ctx, f"rt_a{i}", [P, NT]), sb(ctx, f"rs_a{i}", [P, NT])))
            tri = sb(ctx, "tri", [P, P])
            ones = sb(ctx, "ones_a", [P, P])
            maskU = sb(ctx, "maskU", [P, P], BF16)
            maskL = sb(ctx, "maskL", [P, P], BF16)
            bqs = sb(ctx, "bqs", [P, 2])
            warm = sb(ctx, "warm4", [P, 1])

            p_x = PS[:, 0:2, :]
            p_e = PS[:, 2:4, :]
            p_o = PS[:, 4, :]
            p_m = PS[:, 5, :]
            p_a = PS[:, 6, :]
            p_b = PS[:, 7, :]

            acon = signal("att_consts")
            acon2 = signal("q_bias_ready")
            astats = signal("att_x_stats", B)
            aaggr = signal("att_x_aggr", B)
            amv_kept = signal("att_x_moments_kept")
            arst = signal("att_rstd_steps")
            xn = signal("xn_ready", NT)
            xnT_ps = signal("xnT_ps")
            xnT = signal("xnT_ready")
            y_ps = signal("y_ps")
            yb = signal("yb_ready")
            th = signal("gate_tanh_ready")
            sg = signal("gate_sigmoid_ready")
            qk_ps = signal("qk_ps", 4)
            qk = signal("qk_ready", 4)
            kk1 = signal("k_scaled", 2)
            kk2 = signal("k_smeared", 2)
            part1 = signal("part1_ready", 4)
            rest1 = signal("rest1_ready", 4)
            part2 = signal("part2_ready", 4)
            part3 = signal("part3_ready", 4)
            vp_ps = signal("vp_ps", NT)
            pb = signal("pb_ready", NT)
            pth = signal("silu_tanh_ready", NT)
            sp_ = signal("silu_ready", NT)
            pos_ps = signal("pos_ps")
            ka = signal("ka_ready", 5)
            kaT_ps = signal("kaT_ps")
            kaT = signal("kaT_ready")
            q_out = signal("q_parts_to_dram", 16 * 2)
            k_out = signal("k_parts_to_dram", 16 * 2)
            a_out = signal("k_extra_to_dram", 16)
            stack_in = signal("stacks_in", 16 * 13)
            s_ps = signal("score_ps", 16 * NG4)
            mx_ = signal("max_ready", 16 * NG4)
            qa = signal("max_parts_ready", 5 * NG4)
            m_ps = signal("max_rows_ps", NG4)
            m_in = signal("max_rows_ready", 4 * NG4)
            e_ps = signal("score_minus_max_ps", 16 * NG4)
            ex = signal("exp_ready", 16 * NG4)
            o_ps = signal("o_ps", NG4)
            o_kept = signal("o_kept", NG4)
            oT_ps = signal("oT_ps", NG4)
            rden = signal("inverse_sum_ready", NG4)
            on = signal("o_normal", NG4)
            gated = signal("gated_ready")
            gT_ps = signal("gatedT_ps", 2)
            gT = signal("gatedT_ready", 2)
            w_ps = signal("att_out_ps")
            t_kept = signal("att_out_kept")
            st = [signal(f"a_stats{i}", NT) for i in range(2)]
            mv = [signal(f"a_moments{i}", NT) for i in range(2)]
            rs = [signal(f"a_scale{i}", 2) for i in range(2)]
            n1 = signal("a_n1_ready", NT)
            n1w = signal("a_n1w_ready", 2)
            n2 = signal("a_n2_ready", NT)

            block = ctx.enter_context(nc.Block())

            def sequences(eng, project, maxima, rows_of_maxima, slot, output):
                for s in range(15):
                    project(0, 0, s)
                for j in range(NT):
                    maxima(0, 0, 0, j)
                rows_of_maxima(0, 0, 0)
                maxima(0, 0, 1, 0)

                def body(b, p, before, after):
                    def group(g):
                        return (b, p, g) if g < NG4 else None if after is None else (after, 1 - p, g - NG4)
                    for g in range(NG4):
                        for j in range(NT):
                            s = NT * g + j
                            more = group(g + 1) if j + 1 < NT else group(g + 2)
                            slot(b, p, g, j, more, (j + 1) % NT, before)
                            if j == NT - 1 and group(g + 1):
                                rows_of_maxima(*group(g + 1))
                            if after is not None and s < 15:
                                project(after, 1 - p, s)
                            if before is not None:
                                output(before, 1 - p, s)
                            if j == NT - 1:
                                slot(b, p, g, NT, None, 0, before)
                body(0, 0, None, 1)
                with eng.Fori(0, B // 2 - 1) as q:
                    for k in range(2):
                        body(eng.snap(q * 2 + (k + 1)), 1 - k, eng.snap(q * 2 + k), eng.snap(q * 2 + (k + 2)))
                body(B - 1, 1, B - 2, None)
                slot(B, 0, 0, 1, None, 0, B - 1)
                for s in range(NT * NG4):
                    output(B - 1, 1, s)

            def group_before(b, g, before):
                return (b, g - 1) if g else (before, NG4 - 1)

            @block.sync
            def _(sp):
                def project(b, p):
                    at = bass.ds(b, 1)
                    one = lambda ap: ap.rearrange("o a n -> (o a) n") if len(ap.shape) == 3 else ap.rearrange("o s a n -> (o s) a n")

                    def head_rows(dram, s):
                        return one(dram[at])[s, :, :].rearrange("(h d) n -> d h n", d=DH)
                    for n, (parts, dram, stack, order, out) in enumerate(
                            ((PQ, qd, QS, (0, 0, 0, 1, 1, 2), q_out), (PK, kd, KS, (0, 1, 2, 0, 1, 0), k_out))):
                        if n == 1:
                            sp.wait_ge(kaT.sem, kaT.value(sp, b))
                            sp.dma_start(one(ad[at]), KAT[:, :]).then_inc(a_out.sem, 16)
                            sp.wait_ge(a_out.sem, a_out.value(sp, b))
                            sp.dma_start(KS[96:KF, p, :, :], one(ad[at]).rearrange("(h r) n -> r h n", r=6)).then_inc(stack_in.sem, 16)
                        for c in range(2):
                            sp.wait_ge(part3.sem, part3.value(sp, b, 2 * n + c + 1))
                            sp.dma_start(one(dram[at])[:, c * P:(c + 1) * P, :].rearrange("s p n -> p s n"),
                                         parts[:, c, :, :]).then_inc(out.sem, 16)
                        sp.wait_ge(out.sem, out.value(sp, b))
                        for r, part in enumerate(order):
                            sp.dma_start(stack[r * DH:(r + 1) * DH, p, :, :], head_rows(dram, part)).then_inc(stack_in.sem, 16)

                with sp.Fori(0, B // 2) as q:
                    for p in range(2):
                        project(sp.snap(q * 2 + p), p)

            @block.gpsimd
            def _(pool):
                pool.memset(tri[:, :], 1.0).then_inc(acon.sem, 1)
                pool.memset(ones[:, :], 1.0).then_inc(acon.sem, 1)
                pool.memset(maskU[:, :], 0.0).then_inc(acon.sem, 1)
                pool.memset(maskL[:, :], 0.0).then_inc(acon.sem, 1)
                pool.memset(VV[:, :, :, :, DH:32], 0.0).then_inc(acon.sem, 1)
                pool.memset(KA[:, :, :, :], 1.0).then_inc(acon.sem, 1)
                pool.memset(QA[:, :, :, :], 1.0).then_inc(acon.sem, 1)
                pool.wait_ge(acon.sem, 7)
                pool.memset(VV[:, :, :, :, DH:DH + 1], 1.0).then_inc(acon.sem, 1)
                pool.affine_select(out=tri[:, :], in_=tri[:, :], compare_op=ALU.is_ge, fill=0.0, base=0,
                                   pattern=[[1, P]], channel_multiplier=-1).then_inc(acon.sem, 1)
                pool.affine_select(out=maskU[:, :], in_=maskU[:, :], compare_op=ALU.is_ge, fill=NEG_BIG, base=0,
                                   pattern=[[-1, P]], channel_multiplier=1).then_inc(acon.sem, 1)
                pool.affine_select(out=maskL[:, :], in_=maskL[:, :], compare_op=ALU.is_ge, fill=NEG_BIG, base=0,
                                   pattern=[[1, P]], channel_multiplier=-1).then_inc(acon.sem, 1)
                pool.wait_ge(acon.sem, 11)
                pool.memset(QS[96:KF, :, :, :], 1.0).then_inc(acon.sem, 1)
                pool.wait_ge(acon.sem, 12)
                pool.wait_ge(amv_kept.sem, NT)
                token_scales(pool, rta, arst.sem, 0, 1, 0)
                pool.wait_ge(arst.sem, 7)
                token_scales(pool, rta, arst.sem, 1, B, 7)
                pool.wait_ge(arst.sem, 14)

                def attend(b):
                    for i in range(2):
                        _, m, r_t, r_s = sets[i]
                        pool.wait_ge(mv[i].sem, mv[i].value(pool, b))
                        layer_norm_scale(pool, m, r_t, r_s, rs[i], b, 0)
                with pool.Fori(0, B) as b:
                    attend(b)

            @block.tensor
            def _(pe):
                pe.wait_ge(acon.sem, 12)

                def project(b, p, s):
                    if s == 0:
                        if not (isinstance(b, int) and b == 0):
                            pe.wait_ge(pb.sem, pb.before(pe, b))
                        pe.wait_ge(xn.sem, xn.value(pe, b))
                        for t in range(NT):
                            last = pe.transpose(p_a[:, t * P:(t + 1) * P], XN[:, t, :], ident[:, :])
                        last.then_inc(xnT_ps.sem, 1)
                    if s == 1:
                        pe.wait_ge(xnT.sem, xnT.value(pe, b))
                        p_y = p_b[:, 0:NT * HEADS].rearrange("p (t h) -> p t h", t=NT)
                        for t in range(NT):
                            last = pe.matmul(p_y[:, t, :], XT[:, t * P:(t + 1) * P], winT[:, 4 * DE:], start=True, stop=True)
                        last.then_inc(y_ps.sem, 1)
                    for c in {1: (0,), 3: (1,), 4: (2, 3)}.get(s, ()):
                        if c == 1:
                            pe.wait_ge(yb.sem, yb.value(pe, b))
                        if c >= 2:
                            pe.wait_ge(qk.sem, qk.value(pe, b, c - 1))
                        if c == 2:
                            wait_output(b)
                        pe.matmul(PS[:, 6 + c % 2, :], winT[:, c * P:(c + 1) * P], XT[:, :],
                                  start=True, stop=True).then_inc(qk_ps.sem, 1)
                    for t in {8: (0,), 11: (1,), 12: (2,), 13: (3,)}.get(s, ()):
                        if t == 0:
                            pe.wait_ge(ka.sem, ka.value(pe, b))
                        elif t == 1:
                            pe.wait_ge(kaT.sem, kaT.value(pe, b))
                        else:
                            pe.wait_ge(pb.sem, pb.value(pe, b, t - 1))
                        pe.matmul(PS[:, 6 + t % 2, :], XT[:, t * P:(t + 1) * P], winT[:, 2 * DE:4 * DE],
                                  start=True, stop=True).then_inc(vp_ps.sem, 1)
                    if s == 5:
                        pe.wait_ge(qk.sem, qk.value(pe, b, 3))
                        pe.wait_ge(sg.sem, sg.value(pe, b))
                        p_p = p_a[:, 0:NT * HEADS].rearrange("p (t h) -> p t h", t=NT)
                        for t in range(NT):
                            for i in range(t + 1):
                                last = pe.matmul(p_p[:, t, :], (tri if i == t else ones)[:, :], SG[:, i, :],
                                                 start=(i == 0), stop=(i == t))
                        last.then_inc(pos_ps.sem, 1)
                    if s == 7:
                        pe.wait_ge(qk.sem, qk.value(pe, b))
                        pe.wait_ge(ka.sem, ka.value(pe, b))
                        p_k = p_b.bitcast(BF16)[0:HEADS * 6, 0:S]
                        for t in range(NT):
                            last = pe.transpose(p_k[:, t * P:(t + 1) * P], KA[:, t, :, :].rearrange("p h r -> p (h r)"), identb[:, :])
                        last.then_inc(kaT_ps.sem, 1)

                def wait_output(b):
                    if not isinstance(b, int):
                        pe.wait_ge(t_kept.sem, pe.snap(b - 1))
                    elif b >= 2:
                        pe.wait_ge(t_kept.sem, b - 1)

                def score_for_max(b, p, g, it, i):
                    n = (it + 1) * P
                    u, h = 4 * it + i, 4 * g + i
                    if not (isinstance(b, int) and b == 0) or 16 * g + u >= 2:
                        pe.wait_ge(mx_.sem, mx_.value(pe, b, 16 * g + u - 1))
                    pe.matmul(p_x[:, i % 2, 0:n], QS[0:KM, p, h, it * P:(it + 1) * P], KS[0:KM, p, h, 0:n], start=True, stop=False)
                    pe.matmul(p_x[:, i % 2, n - P:n], identb[:, :], maskU[:, :], start=False, stop=True).then_inc(s_ps.sem, 1)

                def rows_of_maxima(b, p, g):
                    pe.wait_ge(qa.sem, qa.value(pe, b, 5 * (g + 1)))
                    for i in range(4):
                        for t in range(NT):
                            last = pe.transpose(p_m.bitcast(BF16)[32 * i:32 * i + 6, t * P:(t + 1) * P], QA[:, i, t, :],
                                                identb[:, :], tile_position=(0, 32 * i))
                    last.then_inc(m_ps.sem, 1)

                def maxima(b, p, g, it):
                    if it == 0 and g == 0:
                        pe.wait_ge(stack_in.sem, stack_in.value(pe, b))
                    for i in range(4):
                        score_for_max(b, p, g, it, i)

                def times_v(b, p, g, j):
                    pe.wait_ge(ex.sem, ex.value(pe, b, 16 * g + 4 * j + 4))
                    for i in range(4):
                        last = pe.matmul(p_o[32 * i:32 * i + 32, j * P:S], VV[:, p, j, 4 * g + i, :], PT[:, j % 2, i, 0:S - j * P],
                                         start=(j == 0), stop=(j == NT - 1), tile_position=(0, 32 * i), skip_group_check=True)
                    return last

                def slot(b, p, g, j, more, it, before):
                    if j == NT:
                        times_v(b, p, g, NT - 1).then_inc(o_ps.sem, 1)
                        return
                    if not (isinstance(b, int) and b == B):
                        if j == 0:
                            pe.wait_ge(m_in.sem, m_in.value(pe, b, 4 * (g + 1)))
                            if g == 0:
                                pe.wait_ge(pb.sem, pb.value(pe, b))
                        if more and it == 0 and more[2] == 0:
                            pe.wait_ge(stack_in.sem, stack_in.value(pe, more[0]))
                        n = S - j * P
                        for i in range(4):
                            u, h = 4 * j + i, 4 * g + i
                            if u >= 2:
                                pe.wait_ge(ex.sem, ex.value(pe, b, 16 * g + u - 1))
                            pe.matmul(p_e[:, i % 2, 0:n], KS[0:KF, p, h, j * P:(j + 1) * P],
                                      QS[0:KF, p, h, j * P:S], start=True, stop=False)
                            pe.matmul(p_e[:, i % 2, 0:P], identb[:, :], maskL[:, :], start=False, stop=True).then_inc(e_ps.sem, 1)
                            if more:
                                score_for_max(*more, it, i)
                        if j >= 1:
                            if j == 1:
                                o = group_before(b, g, before)
                                if o[0] is not None:
                                    pe.wait_ge(o_kept.sem, o_kept.value(pe, o[0], o[1] + 1))
                            times_v(b, p, g, j - 1)
                    if j == 1:
                        o = group_before(b, g, before)
                        if o[0] is not None:
                            pe.wait_ge(o_kept.sem, o_kept.value(pe, o[0], o[1] + 1))
                            for t in range(NT):
                                last = pe.transpose(p_m[:, t * P:(t + 1) * P], OT[:, t * P:(t + 1) * P], ident[:, :])
                            last.then_inc(oT_ps.sem, 1)
                    if j == 3:
                        o = group_before(b, g, before)
                        if o[0] is not None:
                            pe.wait_ge(on.sem, on.value(pe, o[0], o[1] + 1))

                def output(b, p, s):
                    if s == 2:
                        pe.wait_ge(gated.sem, gated.value(pe, b))
                        for c in range(2):
                            for t in range(NT):
                                last = pe.transpose(PS[:, 6 + c, t * P:(t + 1) * P],
                                                    ON[:, t, 8 * c:8 * c + 8, :].rearrange("p h d -> p (h d)"), ident[:, :])
                            last.then_inc(gT_ps.sem, 1)
                    if s == 3:
                        pe.wait_ge(gT.sem, gT.value(pe, b))
                        p_w = p_a.rearrange("p (t d) -> p t d", t=NT)
                        for t in range(NT):
                            for c in range(2):
                                last = pe.matmul(p_w[:, t, :], GT[:, c, t * P:(t + 1) * P], waoT[:, c, :], start=(c == 0), stop=(c == 1))
                        last.then_inc(w_ps.sem, 1)
                sequences(pe, project, maxima, rows_of_maxima, slot, output)

            @block.scalar
            def _(act):
                act.activation(warm[:, :], half[:, 0:1], ACT.Tanh).then_inc(warmed.sem, 1)

                act.wait_ge(acon2.sem, 1)

                def project(b, p, s):
                    if s == 0:
                        act.wait_ge(xnT_ps.sem, xnT_ps.value(act, b))
                        act.activation(XT[:, :], p_a, ACT.Identity, scale=ilw[:, 0:1], bias=ilb[:, 0:1]).then_inc(xnT.sem, 1)
                    for c in {1: (0,), 3: (1,), 4: (2, 3)}.get(s, ()):
                        act.wait_ge(qk_ps.sem, qk_ps.value(act, b, c + 1))
                        if c < 2:
                            act.activation(QF[:, c, :], PS[:, 6 + c, :], ACT.Identity, scale=qsc[:, 4 + c:5 + c],
                                           bias=bqs[:, c:c + 1]).then_inc(qk.sem, 1)
                        else:
                            act.activation(KF_[:, c - 2, :], PS[:, 4 + c, :], ACT.Identity, bias=bqk[:, c:c + 1]).then_inc(qk.sem, 1)
                    if s == 3:
                        act.wait_ge(yb.sem, yb.value(act, b))
                        act.activation(SG[:, :, :], YB[:, :, :], ACT.Tanh, scale=0.5).then_inc(th.sem, 1)
                    if s == 4:
                        act.wait_ge(k_out.sem, k_out.before(act, b))
                    for i in {4: (0, 1), 5: (2,), 6: (3,)}.get(s, ()):
                        src, dst = (QF, PQ) if i < 2 else (KK, PK)
                        if i < 2:
                            act.wait_ge(qk.sem, qk.value(act, b, i + 1))
                        else:
                            act.wait_ge(kk2.sem, kk2.value(act, b, i - 1))
                        act.activation(dst[:, i % 2, 0, :], src[:, i % 2, :], ACT.Copy).then_inc(part1.sem, 1)
                    for t in {8: (0,), 11: (1,), 12: (2,), 13: (3,)}.get(s, ()):
                        act.wait_ge(pb.sem, pb.value(act, b, t + 1))
                        act.activation(TH[:, t % 2, :], PB[:, t % 2, :], ACT.Tanh, scale=0.5).then_inc(pth.sem, 1)
                    if s == 7:
                        act.wait_ge(kaT_ps.sem, kaT_ps.value(act, b))
                        act.activation(KAT[:, :], p_b.bitcast(BF16)[0:HEADS * 6, 0:S], ACT.Copy).then_inc(kaT.sem, 1)

                def rows_of_maxima(b, p, g):
                    act.wait_ge(m_ps.sem, m_ps.value(act, b, g + 1))
                    for i in range(4):
                        act.activation(QS[96:KF, p, 4 * g + i, :], p_m.bitcast(BF16)[32 * i:32 * i + 6, 0:S],
                                       ACT.Copy).then_inc(m_in.sem, 1)

                def maxima(b, p, g, it):
                    pass

                def slot(b, p, g, j, more, it, before):
                    if isinstance(b, int) and b == B:
                        return
                    if j == NT:
                        act.wait_ge(o_ps.sem, o_ps.value(act, b, g + 1))
                        act.activation(OT[:, :], p_o, ACT.Copy).then_inc(o_kept.sem, 1)
                        return
                    n = S - j * P
                    for i in range(4):
                        act.wait_ge(e_ps.sem, e_ps.value(act, b, 16 * g + 4 * j + i + 1))
                        act.activation(PT[:, j % 2, i, 0:n], p_e[:, i % 2, 0:n], ACT.Exp).then_inc(ex.sem, 1)

                def output(b, p, s):
                    if s == 2:
                        for c in range(2):
                            act.wait_ge(gT_ps.sem, gT_ps.value(act, b, c + 1))
                            act.activation(GT[:, c, :], PS[:, 6 + c, :], ACT.Copy).then_inc(gT.sem, 1)
                sequences(act, project, maxima, rows_of_maxima, slot, output)

            @block.vector
            def _(dve):
                dve.tensor_tensor(bqs[:, :], bqk[:, 0:2], qsc[:, 4:6], ALU.mult).then_inc(acon2.sem, 1)
                x_moments(dve, STa, MVa, astats, aaggr, amv_kept)
                dve.wait_ge(arst.sem, 7)

                def project(b, p, s):
                    if s == 0:
                        if isinstance(b, int) and b == 1:
                            dve.wait_ge(arst.sem, 14)
                        for t in range(NT):
                            if isinstance(b, int):
                                at = slice(t * B + b, t * B + b + 1)
                            else:
                                at = bass.ds(dve.snap(b + t * B), 1)
                            dve.tensor_scalar(XN[:, t, :], X[:, at, :].rearrange("p o d -> p (o d)"),
                                              MV[:, at, 0:1].rearrange("p o k -> p (o k)"), RR[:, at],
                                              ALU.subtract, ALU.mult).then_inc(xn.sem, 1)
                    if s == 1:
                        dve.wait_ge(y_ps.sem, y_ps.value(dve, b))
                        dve.tensor_tensor(YB[:, :, :], p_b[:, 0:NT * HEADS].rearrange("p (t h) -> p t h", t=NT),
                                          bvpy[:, 2 * DE:].unsqueeze(1).to_broadcast([P, NT, HEADS]), ALU.add).then_inc(yb.sem, 1)
                    if s == 4:
                        dve.wait_ge(th.sem, th.value(dve, b))
                        dve.tensor_scalar(SG[:, :, :], SG[:, :, :], 0.5, 0.5, ALU.mult, ALU.add).then_inc(sg.sem, 1)
                    for c in {5: (0,), 6: (1,)}.get(s, ()):
                        dve.wait_ge(qk.sem, qk.value(dve, b, 3 + c))
                        dve.tensor_scalar(KK[:, c, :], KF_[:, c, :], qsc[:, c:c + 1], None, ALU.mult).then_inc(kk1.sem, 1)
                        dve.wait_ge(kk1.sem, kk1.value(dve, b, c + 1))
                        dve.scalar_tensor_tensor(KK[:, c, 1:S], KF_[:, c, 0:S - 1], qsc[:, 2 + c:3 + c], KK[:, c, 1:S],
                                                 ALU.mult, ALU.add).then_inc(kk2.sem, 1)
                    for t in {9: (0,), 12: (1,), 13: (2,), 14: (3,)}.get(s, ()):
                        dve.wait_ge(pth.sem, pth.value(dve, b, t + 1))
                        dve.scalar_tensor_tensor(SP[:, p, t, :], TH[:, t % 2, :], 1.0, PB[:, t % 2, :], ALU.add, ALU.mult).then_inc(sp_.sem, 1)
                    for t in {8: (0,), 11: (1,), 12: (2,), 13: (3,)}.get(s, ()):
                        if t >= 2:
                            dve.wait_ge(sp_.sem, sp_.value(dve, b, t - 1))
                        dve.wait_ge(vp_ps.sem, vp_ps.value(dve, b, t + 1))
                        bank = PS[:, 6 + t % 2, :]
                        dve.tensor_tensor(VV[:, p, t, :, 0:DH], bank[:, 0:DE].rearrange("p (h d) -> p h d", d=DH),
                                          bvpy[:, 0:DE].rearrange("p (h d) -> p h d", d=DH), ALU.add)
                        dve.tensor_tensor(PB[:, t % 2, :], bank[:, DE:], bvpy[:, DE:2 * DE], ALU.add).then_inc(pb.sem, 1)
                    for i in {5: (0,), 7: (1, 2), 8: (3,)}.get(s, ()):
                        src, dst = (QF, PQ) if i < 2 else (KK, PK)
                        c = i % 2
                        if i >= 2:
                            dve.wait_ge(part3.sem, part3.value(dve, b, i - 1))
                        dve.wait_ge(part1.sem, part1.value(dve, b, i + 1))
                        dve.tensor_tensor(RES[:, c, :], src[:, c, :], dst[:, c, 0, :], ALU.subtract).then_inc(rest1.sem, 1)
                        dve.wait_ge(rest1.sem, rest1.value(dve, b, i + 1))
                        dve.tensor_copy(dst[:, c, 1, :], RES[:, c, :]).then_inc(part2.sem, 1)
                        dve.wait_ge(part2.sem, part2.value(dve, b, i + 1))
                        dve.tensor_tensor(dst[:, c, 2, :], RES[:, c, :], dst[:, c, 1, :], ALU.subtract).then_inc(part3.sem, 1)
                    if s == 6:
                        p_p = p_a[:, 0:NT * HEADS].rearrange("p (t h) -> p t h", t=NT)
                        dve.wait_ge(pos_ps.sem, pos_ps.value(dve, b))
                        dve.tensor_copy(KA[:, :, :, 0], p_p).then_inc(ka.sem, 1)
                        dve.wait_ge(ka.sem, ka.value(dve, b, 1))
                        dve.tensor_tensor(PR[:, :, :], p_p, KA[:, :, :, 0], ALU.subtract).then_inc(ka.sem, 1)
                        dve.wait_ge(ka.sem, ka.value(dve, b, 2))
                        dve.tensor_copy(KA[:, :, :, 1], PR[:, :, :]).then_inc(ka.sem, 1)
                        dve.wait_ge(ka.sem, ka.value(dve, b, 3))
                        dve.tensor_tensor(KA[:, :, :, 2], PR[:, :, :], KA[:, :, :, 1], ALU.subtract).then_inc(ka.sem, 2)

                def maxima(b, p, g, it):
                    n = (it + 1) * P
                    for i in range(4):
                        dve.wait_ge(s_ps.sem, s_ps.value(dve, b, 16 * g + 4 * it + i + 1))
                        dve.tensor_reduce(MX[:, i, it:it + 1], p_x[:, i % 2, 0:n], AX.X, ALU.max,
                                          negate=True).then_inc(mx_.sem, 1)
                    if it == NT - 1:
                        dve.wait_ge(mx_.sem, mx_.value(dve, b, 16 * (g + 1)))
                        dve.tensor_copy(QA[:, :, :, 3], MX[:, :, :]).then_inc(qa.sem, 1)
                        dve.wait_ge(qa.sem, qa.value(dve, b, 5 * g + 1))
                        dve.tensor_tensor(MR[:, :, :], MX[:, :, :], QA[:, :, :, 3], ALU.subtract).then_inc(qa.sem, 1)
                        dve.wait_ge(qa.sem, qa.value(dve, b, 5 * g + 2))
                        dve.tensor_copy(QA[:, :, :, 4], MR[:, :, :]).then_inc(qa.sem, 1)
                        dve.wait_ge(qa.sem, qa.value(dve, b, 5 * g + 3))
                        dve.tensor_tensor(QA[:, :, :, 5], MR[:, :, :], QA[:, :, :, 4], ALU.subtract).then_inc(qa.sem, 2)

                def rows_of_maxima(b, p, g):
                    pass

                def slot(b, p, g, j, more, it, before):
                    if j == NT:
                        return
                    if more:
                        maxima(*more, it)
                    o = group_before(b, g, before)
                    if j == 1 and o[0] is not None:
                        o_b, o_g = o
                        dve.wait_ge(oT_ps.sem, oT_ps.value(dve, o_b, o_g + 1))
                        o4 = p_m.rearrange("p (t h d) -> p t h d", t=NT, h=4)
                        dve.reciprocal(RS_[:, :, :], o4[:, :, :, DH]).then_inc(rden.sem, 1)
                        dve.wait_ge(rden.sem, rden.value(dve, o_b, o_g + 1))
                        dve.tensor_tensor(ON[:, :, 4 * o_g:4 * o_g + 4, :], o4[:, :, :, 0:DH],
                                          RS_[:, :, :].unsqueeze(3).to_broadcast([P, NT, 4, DH]), ALU.mult).then_inc(on.sem, 1)

                def moments(i, src, b):
                    s_t, m, _, _ = sets[i]
                    for t in range(NT):
                        dve.bn_stats(s_t[:, t, :], src[:, t, :]).then_inc(st[i].sem, 1)
                    hold(dve, st[i].sem, st[i].value(dve, b))
                    for t in range(NT):
                        dve.bn_aggr(m[:, t, :], s_t[:, t, :]).then_inc(mv[i].sem, 1)

                def normal(i, dst, src, b, done):
                    _, m, _, r_s = sets[i]
                    dve.wait_ge(rs[i].sem, rs[i].value(dve, b))
                    for t in range(NT):
                        dve.tensor_scalar(dst[:, t, :], src[:, t, :], m[:, t, 0:1], r_s[:, t:t + 1],
                                          ALU.subtract, ALU.mult).then_inc(done.sem, 1)
                    dve.wait_ge(done.sem, done.value(dve, b))

                def output(b, p, s):
                    if s == 1:
                        dve.wait_ge(on.sem, on.value(dve, b))
                        flat = ON[:, :, :, :].rearrange("p t h d -> p (t h d)")
                        dve.tensor_tensor(flat, flat, SP[:, p, :, :].rearrange("p t n -> p (t n)"), ALU.mult).then_inc(gated.sem, 1)
                    if s == 3:
                        dve.wait_ge(w_ps.sem, w_ps.value(dve, b))
                        dve.tensor_copy(T[:, :, :], p_a.rearrange("p (t d) -> p t d", t=NT)).then_inc(t_kept.sem, 1)
                        dve.wait_ge(t_kept.sem, t_kept.value(dve, b))
                        moments(0, T, b)
                    if s == 9:
                        normal(0, N1, T, b, n1)
                        dve.tensor_tensor(N1[:, :, :], N1[:, :, :], olw[:, :].unsqueeze(1).to_broadcast([P, NT, D]), ALU.mult).then_inc(n1w.sem, 1)
                    if s == 10:
                        dve.wait_ge(n1w.sem, n1w.value(dve, b, 1))
                        dve.tensor_tensor(N1[:, :, :], N1[:, :, :], olb[:, :].unsqueeze(1).to_broadcast([P, NT, D]), ALU.add).then_inc(n1w.sem, 1)
                        dve.wait_ge(n1w.sem, n1w.value(dve, b))
                        moments(1, N1, b)
                    if s == 15:
                        normal(1, T, N1, b, n2)
                        one = slice(b, b + 1) if isinstance(b, int) else bass.ds(b, 1)
                        x = by_sequence[:, :, one, :].rearrange("p t o d -> p (t o) d")
                        dve.tensor_tensor(x, x, T[:, :, :], ALU.add)
                sequences(dve, project, maxima, rows_of_maxima, slot, output)

        ctx = ExitStack()
        with ctx:
            XF = sb(ctx, "XF_e", [P, NT, D])
            XT = sb(ctx, "XT_e", [P, S])
            TG = sb(ctx, "TG", [P, NH, S])
            SGU = sb(ctx, "SGU", [P, NH, S])
            HU = sb(ctx, "HU", [P, NH, S])
            T = sb(ctx, "T_e", [P, NT, D])
            N1 = sb(ctx, "N1_e", [P, NT, D])
            sets = []
            for i in range(2):
                sets.append((sb(ctx, f"ste{i}", [P, NT, 6]), sb(ctx, f"mve{i}", [P, NT, 2]),
                             sb(ctx, f"rt_e{i}", [P, NT]), sb(ctx, f"rs_e{i}", [P, NT])))
            warm = sb(ctx, "warm5", [P, 1])
            st = [signal(f"e_stats{i}", NT) for i in range(2)]
            mv = [signal(f"e_moments{i}", NT) for i in range(2)]
            rs = [signal(f"e_scale{i}", 2) for i in range(2)]
            xg = signal("xg_ready", NT)
            xgT_ps = signal("xgT_ps")
            xgT = signal("xgT_ready")
            gu_ps = signal("gate_up_ps", 2 * NH)
            tg = signal("swiglu_tanh_ready", NH)
            sgr = signal("swiglu_gate_ready", NH)
            hu = signal("hidden_ready", NH)
            dn = signal("down_ps")
            tk = signal("down_kept")
            n1 = signal("e_n1_ready", NT)
            x4 = signal("x4_ready")
            stored = signal("stored", 16)
            block = ctx.enter_context(nc.Block())

            def pipeline(eng, early, both, late):
                early(0)
                with eng.Fori(0, B - 1) as b:
                    both(b, eng.snap(b + 1))
                late(B - 1)

            @block.sync
            def _(sp):
                for b in range(B):
                    sp.wait_ge(x4.sem, b + 1)
                    sp.dma_start(out_d[b].rearrange("(t p) d -> p t d", p=P), by_sequence[:, :, b, :]).then_inc(stored.sem, 16)
                sp.wait_ge(stored.sem, 16 * B)

            @block.gpsimd
            def _(pool):
                def scales(b, i):
                    _, m, r_t, r_s = sets[i]
                    pool.wait_ge(mv[i].sem, mv[i].value(pool, b))
                    layer_norm_scale(pool, m, r_t, r_s, rs[i], b, 0)

                def both(b, after):
                    scales(after, 0)
                    scales(b, 1)
                pipeline(pool, lambda b: scales(b, 0), both, lambda b: scales(b, 1))

            @block.tensor
            def _(pe):
                def early(b):
                    pe.wait_ge(xg.sem, xg.value(pe, b))
                    for t in range(NT):
                        last = pe.transpose(PS[:, 0, t * P:(t + 1) * P], XF[:, t, :], ident[:, :])
                    last.then_inc(xgT_ps.sem, 1)

                def gate_and_up(b):
                    pe.wait_ge(xgT.sem, xgT.value(pe, b))
                    for c in range(NH):
                        for o in range(2):
                            pe.matmul(PS[:, 1 + NH * o + c, :], wguT[:, o * HID + c * P:o * HID + (c + 1) * P], XT[:, :],
                                      start=True, stop=True).then_inc(gu_ps.sem, 1)

                def down(b):
                    p_dn = PS[:, 7, :].rearrange("p (t d) -> p t d", t=NT)
                    for t in range(NT):
                        for c in range(NH):
                            if t == 0:
                                pe.wait_ge(hu.sem, hu.value(pe, b, c + 1))
                            last = pe.matmul(p_dn[:, t, :], HU[:, c, t * P:(t + 1) * P], wdT[:, c, :],
                                             start=(c == 0), stop=(c == NH - 1))
                    last.then_inc(dn.sem, 1)

                def late(b):
                    gate_and_up(b)
                    down(b)

                def both(b, after):
                    gate_and_up(b)
                    early(after)
                    down(b)
                pipeline(pe, early, both, late)

            @block.scalar
            def _(act):
                act.activation(warm[:, :], half[:, 0:1], ACT.Tanh).then_inc(warmed.sem, 1)

                def early(b):
                    act.wait_ge(xgT_ps.sem, xgT_ps.value(act, b))
                    act.activation(XT[:, :], PS[:, 0, :], ACT.Copy).then_inc(xgT.sem, 1)

                def late(b):
                    for c in range(NH):
                        act.wait_ge(gu_ps.sem, gu_ps.value(act, b, 2 * c + 1))
                        act.activation(TG[:, c, :], PS[:, 1 + c, :], ACT.Tanh, scale=0.5).then_inc(tg.sem, 1)

                def both(b, after):
                    late(b)
                    early(after)
                pipeline(act, early, both, late)

            @block.vector
            def _(dve):
                def moments(i, src, b):
                    s_t, m, _, _ = sets[i]
                    for t in range(NT):
                        dve.bn_stats(s_t[:, t, :], src(t)).then_inc(st[i].sem, 1)
                    hold(dve, st[i].sem, st[i].value(dve, b))
                    for t in range(NT):
                        dve.bn_aggr(m[:, t, :], s_t[:, t, :]).then_inc(mv[i].sem, 1)

                def normal(i, dst, src, b, done):
                    _, m, _, r_s = sets[i]
                    dve.wait_ge(rs[i].sem, rs[i].value(dve, b))
                    for t in range(NT):
                        dve.tensor_scalar(dst[:, t, :], src(t), m[:, t, 0:1], r_s[:, t:t + 1],
                                          ALU.subtract, ALU.mult).then_inc(done.sem, 1)

                def tiles(b):
                    one = slice(b, b + 1) if isinstance(b, int) else bass.ds(b, 1)
                    return by_sequence[:, :, one, :].rearrange("p t o d -> p (t o) d")

                def tile(b):
                    return lambda t: (X[:, t * B + b, :] if isinstance(b, int) else
                                      X[:, bass.ds(dve.snap(b + t * B), 1), :].rearrange("p o d -> p (o d)"))

                def early_moments(b):
                    moments(0, tile(b), b)

                def early_normal(b):
                    if not isinstance(b, int):
                        dve.wait_ge(xgT_ps.sem, xgT_ps.before(dve, b))
                    normal(0, XF, tile(b), b, xg)

                def hidden(b):
                    for c in range(NH):
                        dve.wait_ge(tg.sem, tg.value(dve, b, c + 1))
                        dve.scalar_tensor_tensor(SGU[:, c, :], TG[:, c, :], 1.0, PS[:, 1 + c, :], ALU.add, ALU.mult).then_inc(sgr.sem, 1)
                        dve.wait_ge(gu_ps.sem, gu_ps.value(dve, b, 2 * c + 2))
                        dve.wait_ge(sgr.sem, sgr.value(dve, b, c + 1))
                        dve.tensor_tensor(HU[:, c, :], SGU[:, c, :], PS[:, 1 + NH + c, :], ALU.mult).then_inc(hu.sem, 1)

                def output(b):
                    dve.wait_ge(dn.sem, dn.value(dve, b))
                    dve.tensor_copy(T[:, :, :], PS[:, 7, :].rearrange("p (t d) -> p t d", t=NT)).then_inc(tk.sem, 1)
                    dve.wait_ge(tk.sem, tk.value(dve, b))
                    moments(1, lambda t: T[:, t, :], b)
                    normal(1, N1, lambda t: T[:, t, :], b, n1)
                    dve.wait_ge(n1.sem, n1.value(dve, b))
                    dve.tensor_tensor(tiles(b), tiles(b), N1[:, :, :], ALU.add).then_inc(x4.sem, 1)

                def early(b):
                    early_moments(b)
                    early_normal(b)

                def late(b):
                    hidden(b)
                    output(b)

                def both(b, after):
                    early_moments(after)
                    early_normal(after)
                    hidden(b)
                    output(b)
                pipeline(dve, early, both, late)


_INS = ["L0_attn_x", "L0_attn_gamma", "L0_attn_beta", "L0_attn_w_ih", "L0_attn_w_hh", "L0_attn_b_ih", "L0_attn_b_hh",
        "L0_attn_w_out", "L0_attn_b_out", "L0_ffn_gate_W", "L0_ffn_gate_b", "L0_ffn_wi_W", "L0_ffn_wi_b", "L0_ffn_wo_W",
        "L0_ffn_wo_b", "L0_ffn_lora_A", "L0_ffn_lora_B", "L1_attn_W_in", "L1_attn_b_in", "L1_attn_in_ln_w",
        "L1_attn_in_ln_b", "L1_attn_W_out", "L1_attn_out_ln_w", "L1_attn_out_ln_b", "L1_attn_smear_factor",
        "L1_attn_log_scale", "L1_ffn_w_gate", "L1_ffn_w_up", "L1_ffn_w_down"]


def kernel(**inputs):
    import numpy as _np
    import concourse.bacc as _bacc
    from concourse import mybir as _mybir
    from concourse.bass_utils import run_bass_kernel_spmd as _run

    nc = _bacc.Bacc("TRN2", target_bir_lowering=False, num_devices=1)
    arrays, args = {}, []
    for name in _INS:
        a = _np.ascontiguousarray(inputs[name])
        arrays[f"in_{name}_dram"] = a
        args.append(nc.dram_tensor(f"in_{name}_dram", a.shape, _mybir.dt.from_np(a.dtype), kind="ExternalInput").ap())
    args.append(nc.dram_tensor("out_0_dram", (B, S, D), F32, kind="ExternalOutput").ap())
    build(nc, *args)
    r = _run(nc, [arrays], core_ids=[0])
    return r.results[0]["out_0_dram"]
```
